# Optimizing a Trainium2 kernel written in Bass

```python
import numpy as np
import jax
import jax.numpy as jnp

def _softmax(x, axis=-1):
    return jax.nn.softmax(x, axis=axis)

def _gelu(x):
    return jax.nn.gelu(x, approximate=True)

def _silu(x):
    return jax.nn.silu(x)

def _sigmoid(x):
    return jax.nn.sigmoid(x)

def _layernorm(x, axis=-1, eps=1e-05):
    m = jnp.mean(x, axis=axis, keepdims=True)
    v = jnp.var(x, axis=axis, keepdims=True)
    return (x - m) / jnp.sqrt(v + eps)

def _scatter_add(tgt, idx, src, axis=0):
    return tgt.at[idx].add(src)

def _segment_sum(src, seg, n):
    return jax.ops.segment_sum(src, seg, n)
kernel_name = 'mk_gnn_preln_d2_gnn_r8_844b83'

def setup_inputs(seed: int=0):
    np.random.seed(seed)
    _w = jnp.asarray

    def _rec_inputs():
        import jax
        import jax.numpy as jnp
        _gk = jax.random.key(seed)
        x = -0.0002117 + 1 * jax.random.normal(jax.random.fold_in(_gk, 1), (6250, 512), jnp.float32)
        src = jax.random.randint(jax.random.fold_in(_gk, 2), (100000,), 0, 6250, jnp.int32)
        dst = jnp.minimum((6250 * jax.random.uniform(jax.random.fold_in(_gk, 3), (100000,)) ** 2.0).astype(jnp.int32), 49999)
        _o = jnp.argsort(dst, stable=True)
        src = src[_o]
        dst = dst[_o]
        edge_attr_8 = jax.random.uniform(jax.random.fold_in(_gk, 13), (100000, 8), jnp.float32, 0.0, 1)
        return (x, src, dst, edge_attr_8)
    x, src, dst, edge_attr_8 = _rec_inputs()

    def _L0_gnn_setup():
        import jax, jax.numpy as jnp
        import numpy as np
        N = 6250
        E = 100000
        IN_DIM = 512
        OUT_DIM = 64
        NUM_HEADS = 8
        NEG_SLOPE = 0.2
        key = jax.random.key(seed)
        ks = jax.random.split(key, 8)
        feat = jax.random.normal(ks[0], (N, IN_DIM), dtype=jnp.float32)
        dist = jax.random.uniform(ks[1], (E, NUM_HEADS), dtype=jnp.float32)
        src = jax.random.randint(ks[2], (E,), 0, N, dtype=jnp.int32)
        dst = jax.random.randint(ks[3], (E,), 0, N, dtype=jnp.int32)
        W = jax.random.normal(ks[4], (NUM_HEADS * OUT_DIM, IN_DIM), dtype=jnp.float32) / np.sqrt(IN_DIM)
        b = jax.random.normal(ks[5], (NUM_HEADS * OUT_DIM,), dtype=jnp.float32) * 0.01
        w_att_src = jax.random.normal(ks[6], (NUM_HEADS, OUT_DIM), dtype=jnp.float32)
        w_att_dst = jax.random.normal(ks[7], (NUM_HEADS, OUT_DIM), dtype=jnp.float32)
        return {'feat': feat, 'dist': dist, 'src': src, 'dst': dst, 'W': W, 'b': b, 'w_att_src': w_att_src, 'w_att_dst': w_att_dst}
    _L0_gnn_all = _L0_gnn_setup()
    _L0_gnn_in = {k: v for k, v in _L0_gnn_all.items() if k in ('W', 'b', 'w_att_src', 'w_att_dst')}
    del _L0_gnn_all

    def _L1_gnn_setup():
        import jax, jax.numpy as jnp
        import numpy as np
        N_NODES = 1250
        N_EDGES = 20000
        IN_DIM = 512
        OUT_DIM = 512
        LN_EPS = 1e-05
        key = jax.random.key(seed)
        k_x, k_src, k_ws, k_wn = jax.random.split(key, 4)
        x = jax.random.normal(k_x, (N_NODES, IN_DIM), dtype=jnp.float32)
        edge_src = jax.random.randint(k_src, (N_EDGES,), 0, N_NODES, dtype=jnp.int32)
        edge_dst = jnp.repeat(jnp.arange(N_NODES, dtype=jnp.int32), N_EDGES // N_NODES)
        deg = jnp.full((N_NODES,), float(N_EDGES // N_NODES), dtype=jnp.float32)
        scale = 1.0 / np.sqrt(IN_DIM)
        W_self = jax.random.normal(k_ws, (OUT_DIM, IN_DIM), dtype=jnp.float32) * scale
        W_neigh = jax.random.normal(k_wn, (OUT_DIM, IN_DIM), dtype=jnp.float32) * scale
        bias = jnp.zeros((OUT_DIM,), dtype=jnp.float32)
        gamma = jnp.ones((OUT_DIM,), dtype=jnp.float32)
        beta = jnp.zeros((OUT_DIM,), dtype=jnp.float32)
        return {'x': x, 'edge_src': edge_src, 'edge_dst': edge_dst, 'deg': deg, 'W_self': W_self, 'W_neigh': W_neigh, 'bias': bias, 'gamma': gamma, 'beta': beta}
    _L1_gnn_all = _L1_gnn_setup()
    _L1_gnn_in = {k: v for k, v in _L1_gnn_all.items() if k in ('W_self', 'W_neigh', 'bias', 'gamma', 'beta')}
    del _L1_gnn_all
    return {'x': x, 'src': src, 'dst': dst, 'edge_attr_8': edge_attr_8, 'L0_gnn_W': _L0_gnn_in['W'], 'L0_gnn_b': _L0_gnn_in['b'], 'L0_gnn_w_att_src': _L0_gnn_in['w_att_src'], 'L0_gnn_w_att_dst': _L0_gnn_in['w_att_dst'], 'L1_gnn_W_self': _L1_gnn_in['W_self'], 'L1_gnn_W_neigh': _L1_gnn_in['W_neigh'], 'L1_gnn_bias': _L1_gnn_in['bias'], 'L1_gnn_gamma': _L1_gnn_in['gamma'], 'L1_gnn_beta': _L1_gnn_in['beta']}

def reference(x, src, dst, edge_attr_8, L0_gnn_W, L0_gnn_b, L0_gnn_w_att_src, L0_gnn_w_att_dst, L1_gnn_W_self, L1_gnn_W_neigh, L1_gnn_bias, L1_gnn_gamma, L1_gnn_beta):
    import jax
    import jax.numpy as jnp

    def _L0_gnn_ref(feat, dist, src, dst, W, b, w_att_src, w_att_dst):
        import jax, jax.numpy as jnp
        import numpy as np
        N = 6250
        E = 100000
        IN_DIM = 512
        OUT_DIM = 64
        NUM_HEADS = 8
        NEG_SLOPE = 0.2
        h = jax.nn.leaky_relu(feat @ W.T + b, negative_slope=NEG_SLOPE)
        h = h.reshape(N, NUM_HEADS, OUT_DIM)
        e_src = jnp.sum(h * w_att_src, axis=-1)
        e_dst = jnp.sum(h * w_att_dst, axis=-1)
        e = jax.nn.leaky_relu(e_src[src] + e_dst[dst], negative_slope=NEG_SLOPE)
        m = jax.ops.segment_max(e, dst, num_segments=N)
        ex = jnp.exp(e - m[dst])
        s = jax.ops.segment_sum(ex, dst, num_segments=N)
        a = ex / s[dst] * dist
        msg = h[src] * a[:, :, None]
        out = jax.ops.segment_sum(msg, dst, num_segments=N)
        return out.reshape(N, NUM_HEADS * OUT_DIM)

    def _L1_gnn_ref(x, edge_src, edge_dst, deg, W_self, W_neigh, bias, gamma, beta):
        import jax, jax.numpy as jnp
        import numpy as np
        N_NODES = 1250
        N_EDGES = 20000
        IN_DIM = 512
        OUT_DIM = 512
        LN_EPS = 1e-05
        n = x.shape[0]
        h_self = jnp.einsum('nd,od->no', x, W_self)
        neigh_sum = jax.ops.segment_sum(x[edge_src], edge_dst, num_segments=n)
        neigh_mean = neigh_sum / jnp.maximum(deg, 1.0)[:, None]
        h_neigh = jnp.einsum('nd,od->no', neigh_mean, W_neigh)
        h = h_self + h_neigh + bias
        mu = jnp.mean(h, axis=-1, keepdims=True)
        var = jnp.mean(jnp.square(h - mu), axis=-1, keepdims=True)
        h = (h - mu) * jax.lax.rsqrt(var + LN_EPS)
        return h * gamma + beta
    deg = jnp.maximum(jax.ops.segment_sum(jnp.ones(dst.shape, jnp.float32), dst, num_segments=6250), 1.0)
    h = jnp.maximum(_layernorm(x, axis=-1), 0.0)
    x = x + _L0_gnn_ref(h, edge_attr_8, src, dst, L0_gnn_W, L0_gnn_b, L0_gnn_w_att_src, L0_gnn_w_att_dst)
    h = jnp.maximum(_layernorm(x, axis=-1), 0.0)
    x = x + _L1_gnn_ref(h, src, dst, deg, L1_gnn_W_self, L1_gnn_W_neigh, L1_gnn_bias, L1_gnn_gamma, L1_gnn_beta)
    return x

_drawn_inputs = setup_inputs


def setup_inputs(seed=0):
    import zlib

    import numpy as np

    out = dict(_drawn_inputs(seed))
    spreads = {'L1_gnn_bias': (0.0, 0.1), 'L1_gnn_gamma': (1.0, 0.2), 'L1_gnn_beta': (0.0, 0.1)}
    factors = {'L0_gnn_b': 8.0}
    for name, (base, spread) in spreads.items():
        noise = np.random.default_rng([zlib.crc32(name.encode()), seed]).standard_normal(out[name].shape)
        drawn = base * np.exp(spread * noise) if base else spread * noise
        out[name] = jnp.asarray(drawn.astype(out[name].dtype))
    for name, factor in factors.items():
        out[name] = (out[name] * factor).astype(out[name].dtype)
    return out
```

```python
import concourse.bass as bass
from concourse import mybir
from contextlib import ExitStack

F32 = mybir.dt.float32
F32R = mybir.dt.float32r
BF16 = mybir.dt.bfloat16
I32 = mybir.dt.int32
ALU = mybir.AluOpType
ACT = mybir.ActivationFunctionType
AX = mybir.AxisListType

N_NODES, N_EDGES, DIM, HEADS = 6250, 100000, 512, 8
HEAD_DIM = DIM // HEADS
P = 128
KC = DIM // P
NT = -(-N_NODES // P)
LAST_ROWS = N_NODES - (NT - 1) * P
CHUNKS = P // HEADS
TILES = -(-N_EDGES // (P * CHUNKS)) * CHUNKS
TPC = TILES // CHUNKS
CHUNK = TPC * P
PAIRS = TILES // 2
LAST_PAIR = (N_EDGES - 1) // (2 * P)
ROWS = TILES // 8
ROW_EDGES = 8 * P
FULL_ROWS = N_EDGES // ROW_EDGES
REST = N_EDGES - FULL_ROWS * ROW_EDGES
PAD_DST = 8000
BIG = 1e38
EPS = 1e-5
SLOPE = 0.2
RING = 4
WORK = 3
GW = 2 * DIM
EW = HEADS + 1
CODE = 512


def wait(eng, sem, value):
    if not (isinstance(value, int) and value <= 0):
        eng.wait_ge(sem, value)


def ring(buf, u, depth, width):
    return buf[:, bass.ds((u % depth) * width, width)]


def gnn_kernel(nc, x, src, dst, dist, w0t, b0, att_src, att_dst, wst, wnt, bias, gamma, beta, out):
    h_tab = nc.dram_tensor("h_tab", (NT * P, DIM), F32).ap()
    es_tab = nc.dram_tensor("es_tab", (NT * P, HEADS), F32).ap()
    x1_tab = nc.dram_tensor("x1_tab", (NT * P, DIM), F32).ap()
    h1_tab = nc.dram_tensor("h1_tab", (NT * P, DIM), F32).ap()

    ctx = ExitStack()
    with ctx:
        def sb(name, shape, dt=F32):
            return ctx.enter_context(nc.sbuf_tensor(name, shape, dt))

        def sem(name):
            return ctx.enter_context(nc.semaphore(name))

        ident = sb("ident", [P, P])
        ident_b = sb("ident_b", [P, P], BF16)
        iota_i = sb("iota_i", [P, P], I32)
        iota_f = sb("iota_f", [P, P])
        first_i = sb("first_i", [P, NT + 1], I32)
        first_f = sb("first_f", [P, NT + 1])
        thr_i = sb("thr_i", [P, 1], I32)
        thr_f = sb("thr_f", [P, 1])
        pick_last = sb("pick_last", [P, 64])
        eps_c = sb("eps_c", [P, 1])
        row_b0 = sb("row_b0", [P, DIM])
        row_as = sb("row_as", [P, DIM])
        row_ad = sb("row_ad", [P, DIM])
        src_e = sb("src_e", [P, TILES + 2 * RING], I32)
        src_g = sb("src_g", [P, TILES], I32)
        dst_e = sb("dst_e", [P, TILES])
        same = sb("same", [P, CHUNK + 1], BF16)
        ex_buf = sb("ex_buf", [P, TILES * EW])
        coef = sb("coef", [P, TILES * HEADS])
        scan = sb("scan", [P, CHUNK])
        g_ring = sb("g_ring", [P, RING * GW])
        idx_ring = sb("idx_ring", [P, RING * 2], I32)
        xt = [sb(f"xt{k}", [P, DIM]) for k in range(2)]
        hn = [sb(f"hn{k}", [P, DIM]) for k in range(2)]
        hT = [sb(f"hT{k}", [P, DIM]) for k in range(2)]
        ho = [sb(f"ho{k}", [P, DIM]) for k in range(2)]
        st = [sb(f"st{k}", [P, 6]) for k in range(2)]
        mv = [sb(f"mv{k}", [P, 2]) for k in range(2)]
        sd = [sb(f"sd{k}", [P, 1]) for k in range(2)]
        rs = [sb(f"rs{k}", [P, 1]) for k in range(2)]
        nm = [sb(f"nm{k}", [P, 1]) for k in range(2)]
        es_st = [sb(f"es_st{k}", [P, HEADS]) for k in range(2)]
        ed_n = sb("ed_n", [P, NT * HEADS])
        ed_r = sb("ed_r", [P, NT * HEADS])
        ed3 = sb("ed3", [P, NT * 3 * HEADS], BF16)
        rdeg = sb("rdeg", [P, NT])
        cnt = sb("cnt", [64, 1])
        lst = sb("lst", [64, PAIRS])
        bnd_f = sb("bnd_f", [1, 64])
        code_f = sb("code_f", [1, 64])
        code = sb("code", [1, 64], I32)
        iod = [sb(f"iod{k}", [P, P]) for k in range(2)]
        oh_b = sb("oh_b", [P, 2 * P], BF16)
        ohT_b = sb("ohT_b", [P, 2 * P], BF16)
        red = sb("red", [P, 2 * HEADS])
        oh = [sb(f"oh{k}", [P, P]) for k in range(2)]
        ohr = [sb(f"ohr{k}", [P, P], F32R) for k in range(2)]
        st_i = [sb(f"st_i{k}", [P, CHUNKS], I32) for k in range(2)]
        es_r = [sb(f"es_r{k}", [P, P]) for k in range(2)]
        ends = sb("ends", [P, 4])
        rows = sb("rows", [1, 4 * P])
        cont = sb("cont", [1, P])
        one = sb("one", [1, P])
        kl = sb("kl", [1, P])
        outr = sb("outr", [1, P])
        inits = [sb(f"inits{k}", [1, P]) for k in range(2)]
        init_c = sb("init_c", [P, 2])
        r9 = [sb(f"r9{k}", [P, EW]) for k in range(2)]
        rr = [sb(f"rr{k}", [P, EW]) for k in range(2)]

        with nc.sbuf_tensor("edf", [P, 2 * CHUNK], F32) as edf:
            pass
        msg = sb("msg", [P, WORK * GW])
        hi_r = sb("hi_r", [P, WORK * GW], F32R)
        lo_r = sb("lo_r", [P, WORK * GW], F32R)
        mT = [sb(f"mT{k}", [P, DIM]) for k in range(2)]
        yo = [sb(f"yo{k}", [P, DIM]) for k in range(2)]

        ps = [ctx.enter_context(nc.psum_tensor(f"bank{b}", [P, 512], F32)) for b in range(8)]

        src_c = ex_buf[0:ROWS, 0:ROW_EDGES].bitcast(I32)
        dst_c = ex_buf[0:ROWS, ROW_EDGES:2 * ROW_EDGES].bitcast(I32)
        src_cf = ex_buf[0:ROWS, 2 * ROW_EDGES:3 * ROW_EDGES]
        dst_cf = ex_buf[0:ROWS, 3 * ROW_EDGES:4 * ROW_EDGES]
        dist_c = edf[0:ROWS, 0:ROW_EDGES * HEADS]
        dst_s = scan[:, :].bitcast(I32)
        ed_e = edf[:, 0:CHUNK]
        es_all = edf[:, CHUNK:2 * CHUNK]
        fwd = edf[:, CHUNK:2 * CHUNK]
        mx_e = edf[:, CHUNK:2 * CHUNK]
        ws = scan[:, 0:KC * DIM]
        wn = scan[:, KC * DIM:2 * KC * DIM]
        w0 = g_ring[:, 0:KC * DIM]
        ms, md = ([g_ring[:, (KC + 2 * q + k) * DIM:(KC + 2 * q + k + 1) * DIM] for k in range(2)] for q in range(2))
        row_bias, row_gamma, row_beta = (scan[:, (2 * KC + q) * DIM:(2 * KC + q + 1) * DIM] for q in range(3))
        ex3 = ex_buf[:, :].rearrange("p (t h) -> p t h", h=EW)

        s_w = sem("s_w"); s_row = sem("s_row"); s_ec = sem("s_ec"); s_dist = sem("s_dist"); s_ds = sem("s_ds"); s_w1 = sem("s_w1")
        padded = sem("padded"); p_go = sem("p_go"); v_go = sem("v_go")
        k_id = sem("k_id"); k_cst = sem("k_cst"); k_cf = sem("k_cf")
        e_f = sem("e_f"); e_tr = sem("e_tr"); e_ev = sem("e_ev"); e_same = sem("e_same"); e_sg = sem("e_sg")
        b_mm = sem("b_mm"); b_cnt = sem("b_cnt"); b_tr = sem("b_tr"); b_row = sem("b_row"); b_code = sem("b_code")
        x_in = [sem(f"x_in{k}") for k in range(2)]
        h_out = [sem(f"h_out{k}") for k in range(2)]
        es_out = [sem(f"es_out{k}") for k in range(2)]
        a_st = sem("a_st"); a_mv = sem("a_mv"); a_sd = sem("a_sd"); a_rs = sem("a_rs"); a_nm = sem("a_nm")
        a_h0 = sem("a_h0"); a_tr = sem("a_tr"); a_hT = sem("a_hT"); a_mm = sem("a_mm"); a_hb = sem("a_hb")
        a_h = sem("a_h"); a_ms = sem("a_ms"); a_md = sem("a_md"); a_es = sem("a_es"); a_ed = sem("a_ed")
        d_split = sem("d_split")
        st_in = [sem(f"st_in{k}") for k in range(2)]
        eg_in = [sem(f"eg_in{k}") for k in range(2)]
        es_mv = [sem(f"es_mv{k}") for k in range(2)]
        d_iod = sem("d_iod"); d_oh = sem("d_oh"); d_tr = sem("d_tr"); d_cp = sem("d_cp"); d_mm = sem("d_mm")
        d_red = sem("d_red"); d_add = sem("d_add"); d_zero = sem("d_zero")
        t_tr = sem("t_tr"); t_cp = sem("t_cp"); t_x = sem("t_x"); t_v = sem("t_v"); t_pe = sem("t_pe")
        t_bt = sem("t_bt"); t_z = sem("t_z"); t_e = sem("t_e"); t_ex = sem("t_ex"); t_co = sem("t_co")
        g_in0 = [sem(f"g_in0{k}") for k in range(RING)]
        in0 = sem("in0"); idx0 = sem("idx0"); msg0 = sem("msg0"); iod0 = sem("iod0")
        oh_a0 = sem("oh_a0"); oh_b0 = sem("oh_b0"); done_a0 = sem("done_a0"); done_b0 = sem("done_b0")
        xl = [sem(f"xl{k}") for k in range(2)]
        x1_out = [sem(f"x1_out{k}") for k in range(2)]
        h1_out = [sem(f"h1_out{k}") for k in range(2)]
        f_r9 = sem("f_r9"); f_rr = sem("f_rr"); f_w = sem("f_w"); f_x1 = sem("f_x1"); f_st = sem("f_st")
        f_mv = sem("f_mv"); f_sd = sem("f_sd"); f_rs = sem("f_rs"); f_nm = sem("f_nm"); f_h1 = sem("f_h1")
        g_in1 = [sem(f"g_in1{k}") for k in range(RING)]
        in1 = sem("in1"); idx1 = sem("idx1"); hi1 = sem("hi1"); lo1 = sem("lo1"); iod1 = sem("iod1")
        oh_a1 = sem("oh_a1"); oh_b1 = sem("oh_b1"); done_a1 = sem("done_a1"); done_b1 = sem("done_b1")
        hl = [sem(f"hl{k}") for k in range(2)]
        x1l = [sem(f"x1l{k}") for k in range(2)]
        y_out = [sem(f"y_out{k}") for k in range(2)]
        m_mn = sem("m_mn"); m_htr = sem("m_htr"); m_mtr = sem("m_mtr"); m_hT = sem("m_hT"); m_mT = sem("m_mT")
        m_self = sem("m_self"); m_y = sem("m_y"); n_y = sem("n_y"); n_st = sem("n_st"); n_mv = sem("n_mv")
        n_sd = sem("n_sd"); n_rs = sem("n_rs"); n_nm = sem("n_nm"); n_yn = sem("n_yn"); n_g = sem("n_g")
        n_b = sem("n_b"); n_o = sem("n_o")

        block = ctx.enter_context(nc.Block())

        def bounds(eng, d):
            c = eng.value_load(code[0:1, bass.ds(d, 1)], min_val=0, max_val=LAST_PAIR * CODE + LAST_PAIR)
            lo = nc.s_assert_within(c // CODE, 0, LAST_PAIR, skip_runtime_bounds_check_because="a count of pairs")
            hi = nc.s_assert_within(c % CODE, 0, LAST_PAIR, skip_runtime_bounds_check_because="a count of pairs")
            return eng.snap(lo), eng.snap(hi)

        def rest_of(eng, lo, hi, body):
            with eng.If(lo < hi):
                with eng.Fori(lo + 1, hi + 1) as u:
                    body(u)
                eng.nop()
            eng.nop()

        def node_tiles(eng, body):
            body(0, 0)
            body(1, 1)
            with eng.Fori(1, NT // 2 - 1) as j:
                body(2 * j, 0)
                body(2 * j + 1, 1)
            for d in range(NT - 3, NT):
                body(d, d % 2)

        def tiles_by_two(eng, body):
            body(0, 0, 0)
            body(1, 1, 0)
            with eng.Fori(1, NT // 2) as j:
                body(2 * j, 0, j)
                body(2 * j + 1, 1, j)
            body(NT - 1, 0, NT // 2)

        def prev(d):
            return d - 1

        @block.sync
        def _(sp):
            def edge_rows(part, of, width, signal):
                view = of[0:FULL_ROWS * ROW_EDGES * width].rearrange("(r e) -> r e", r=FULL_ROWS)
                rest = of[FULL_ROWS * ROW_EDGES * width:N_EDGES * width].rearrange("(r e) -> r e", r=1)
                sp.dma_start(part[0:FULL_ROWS, :], view).then_inc(signal, 16)
                sp.dma_start(part[FULL_ROWS:FULL_ROWS + 1, 0:REST * width], rest).then_inc(signal, 16)

            sp.wait_ge(padded, 4)
            edge_rows(dst_c, dst, 1, s_ec)
            edge_rows(src_c, src, 1, s_ec)
            sp.dma_start(xt[0][:, :], x[0:P, :]).then_inc(x_in[0], 16)
            sp.dma_start(w0[:, :].rearrange("p (k n) -> p k n", k=KC),
                         w0t.rearrange("(k p) n -> p k n", p=P)).then_inc(s_w, 16)
            sp.dma_start(xt[1][:, :], x[P:2 * P, :]).then_inc(x_in[1], 16)
            edge_rows(dist_c, dist.rearrange("e h -> (e h)"), HEADS, s_dist)
            def load_row(row, of, signal):
                sp.dma_start(row[:, :], of.rearrange("(a n) -> a n", a=1).to_broadcast([P, DIM])).then_inc(signal, 16)

            for row, of in ((row_b0, b0), (row_as, att_src), (row_ad, att_dst)):
                load_row(row, of, s_row)
            for c in range(CHUNKS):
                n = min(CHUNK, N_EDGES - c * CHUNK)
                sp.dma_start(dst_s[c * HEADS:(c + 1) * HEADS, 0:n],
                             dst[c * CHUNK:c * CHUNK + n].rearrange("(a n) -> a n", a=1)
                             .to_broadcast([HEADS, n])).then_inc(s_ds, 16)

            def store(i, k):
                sp.wait_ge(a_h, i + 1)
                sp.dma_start(h_tab[bass.ds(i * P, P), :], ho[k][:, :]).then_inc(h_out[k], 16)
                sp.wait_ge(a_es, i + 1)
                sp.dma_start(es_tab[bass.ds(i * P, P), :], es_st[k][:, :]).then_inc(es_out[k], 16)

            def load(i, k, n=P):
                sp.wait_ge(a_h0, i - 1)
                sp.dma_start(xt[k][0:n, :], x[bass.ds(i * P, n), :]).then_inc(x_in[k], 16)

            with sp.Fori(0, NT // 2 - 1) as j:
                load(2 * j + 2, 0)
                store(2 * j, 0)
                load(2 * j + 3, 1)
                store(2 * j + 1, 1)
            load(NT - 1, 0, LAST_ROWS)
            store(NT - 3, 0)
            store(NT - 2, 1)
            store(NT - 1, 0)

            sp.wait_ge(e_sg, 1)

            def hand(j, k):
                sp.dma_start(st_i[k][:, :], src_g[:, bass.ds(j * CHUNKS, CHUNKS)]).then_inc(st_in[k], 16)

            def move(j, k, n):
                sp.wait_ge(eg_in[k], 16 * CHUNKS * (n + 1))
                sp.dma_start(es_all[:, bass.ds(j * P, P)], es_r[k][:, :]).then_inc(es_mv[k], 16)

            hand(0, 0)
            hand(1, 1)
            sp.wait_ge(e_ev, 20)
            with sp.Fori(0, TPC // 2 - 1) as j:
                move(2 * j, 0, j)
                hand(2 * j + 2, 0)
                move(2 * j + 1, 1, j)
                hand(2 * j + 3, 1)
            move(TPC - 3, 0, TPC // 2 - 1)
            hand(TPC - 1, 0)
            move(TPC - 2, 1, TPC // 2 - 1)
            move(TPC - 1, 0, TPC // 2)

            with sp.Fori(0, PAIRS // RING) as i:
                for k in range(RING):
                    sp.wait_ge(g_in0[k], 32 * (i + 1))
                    sp.sem_inc(in0, 1)
            sp.dma_start(ws.rearrange("p (k n) -> p k n", k=KC),
                         wst.rearrange("(k p) n -> p k n", p=P)).then_inc(s_w1, 16)
            sp.dma_start(wn.rearrange("p (k n) -> p k n", k=KC),
                         wnt.rearrange("(k p) n -> p k n", p=P)).then_inc(s_w1, 16)
            for row, of in ((row_bias, bias), (row_gamma, gamma), (row_beta, beta)):
                load_row(row, of, s_w1)
            with sp.Fori(0, PAIRS // RING) as i:
                for k in range(RING):
                    sp.wait_ge(g_in1[k], 32 * (i + 1))
                    sp.sem_inc(in1, 1)

        @block.gpsimd
        def _(pool):
            pool.memset(dst_c, PAD_DST).then_inc(padded, 1)
            pool.memset(src_c, 0).then_inc(padded, 1)
            pool.memset(ident[:, :], 0.0).then_inc(k_id, 1)
            pool.memset(pick_last[:, :], 0.0).then_inc(k_id, 1)
            pool.iota(iota_i[:, :], pattern=[[1, P]], base=0, channel_multiplier=0).then_inc(k_cst, 1)
            pool.iota(first_i[:, :], pattern=[[P, NT + 1]], base=0, channel_multiplier=0).then_inc(k_cst, 1)
            pool.iota(thr_i[:, :], pattern=[[0, 1]], base=0, channel_multiplier=P).then_inc(k_cst, 1)
            pool.wait_ge(k_id, 2)
            pool.affine_select(out=ident[:, :], in_=ident[:, :], compare_op=ALU.not_equal, fill=1.0, base=0,
                               pattern=[[-1, P]], channel_multiplier=1).then_inc(k_id, 1)
            pool.affine_select(out=pick_last[:, :], in_=pick_last[:, :], compare_op=ALU.not_equal, fill=1.0,
                               base=1 - P, pattern=[[0, 64]], channel_multiplier=1).then_inc(k_id, 1)

            pool.wait_ge(s_row, 48)

            def products(i, k, n):
                pool.wait_ge(a_h, i + 1)
                wait(pool, a_es, i - 1)
                pool.tensor_tensor(ms[k][:, :], ho[k][:, :], row_as[:, :], ALU.mult).then_inc(a_ms, 1)
                wait(pool, a_ed, i - 1)
                pool.tensor_tensor(md[k][:, :], ho[k][:, :], row_ad[:, :], ALU.mult).then_inc(a_md, 1)

            tiles_by_two(pool, products)

            for k in range(2):
                pool.wait_ge(es_out[k], 16 * ((NT + 1 - k) // 2))

            def group(k, n):
                pool.wait_ge(st_in[k], 16 * (n + 1))
                wait(pool, es_mv[k], 16 * n)
                pool.sem_inc(p_go, 1)
                for c in range(CHUNKS):
                    pool.indirect_dma_start(
                        es_r[k][:, c * HEADS:(c + 1) * HEADS], None, es_tab,
                        bass.IndirectOffsetOnAxis(ap=st_i[k][:, c:c + 1], axis=0)).then_inc(eg_in[k], 16)

            group(0, 0)
            group(1, 0)
            with pool.Fori(1, TPC // 2) as j:
                group(0, j)
                group(1, j)
            group(0, TPC // 2)

            def gathers(table, landed, idx_ready, used):
                def pair(i, k):
                    u = RING * i + k
                    pool.wait_ge(idx_ready, u + 1)
                    wait(pool, used, u + 1 - RING)
                    pool.sem_inc(p_go, 1)
                    for t in range(2):
                        pool.indirect_dma_start(
                            g_ring[:, k * GW + t * DIM:k * GW + (t + 1) * DIM], None, table,
                            bass.IndirectOffsetOnAxis(ap=idx_ring[:, 2 * k + t:2 * k + t + 1], axis=0)
                        ).then_inc(landed[k], 16)

                for k in range(RING):
                    pair(0, k)
                with pool.Fori(1, PAIRS // RING) as i:
                    for k in range(RING):
                        pair(i, k)

            for k in range(2):
                pool.wait_ge(h_out[k], 16 * ((NT + 1 - k) // 2))
            gathers(h_tab, g_in0, idx0, msg0)
            for k in range(2):
                pool.wait_ge(h1_out[k], 16 * ((NT + 1 - k) // 2))
            gathers(h1_tab, g_in1, idx1, lo1)

        @block.scalar
        def _(act):
            def normalise(i, k, n):
                act.wait_ge(a_mv, i + 1)
                act.activation(sd[k][:, :], mv[k][:, 1:2], ACT.Sqrt, bias=eps_c[:, :]).then_inc(a_sd, 1)
                act.wait_ge(a_nm, i + 1)
                wait(act, a_tr, i - 1)
                act.activation(hn[k][:, :], xt[k][:, :], ACT.Relu, bias=nm[k][:, :],
                               scale=rs[k][:, :]).then_inc(a_h0, 1)
                act.wait_ge(a_tr, i + 1)
                wait(act, a_mm, i - 1)
                act.copy(hT[k][:, :], ps[k][:, :]).then_inc(a_hT, 1)

            act.wait_ge(k_cf, 1)
            tiles_by_two(act, normalise)

            def step_d(d, u):
                s = d + u
                act.wait_ge(d_tr, s + 2)
                act.wait_ge(d_mm, s + 1)
                act.copy(ohT_b[:, :], ps[2][:, 0:P].bitcast(BF16)).then_inc(d_cp, 1)

            def tile_d(d, k):
                lo, hi = bounds(act, d)
                step_d(d, lo)
                rest_of(act, lo, hi, lambda u: step_d(d, u))

            act.wait_ge(b_code, 1)
            node_tiles(act, tile_d)

            act.wait_ge(e_same, 3)
            for g in range(0, TPC, 4):
                m = min(4, TPC - g)
                act.wait_ge(t_tr, g // 4 + 1)
                act.copy(scan[:, g * P:(g + m) * P], ps[g // 4 % 2][:, 0:m * P]).then_inc(t_cp, 1)
            act.wait_ge(t_e, 1)
            act.activation(ex3[:, :, 0:HEADS], ex3[:, :, 0:HEADS], ACT.Exp).then_inc(t_ex, 1)

            def stage(u, ready):
                act.copy(idx_ring[:, bass.ds((u % RING) * 2, 2)], src_e[:, bass.ds(2 * u, 2)]).then_inc(ready, 1)

            for u in range(RING):
                stage(u, idx0)
            for k in range(2):
                act.dma_start(xt[k][:, :], x[k * P:(k + 1) * P, :]).then_inc(xl[k], 16)

            def new_pair0(u):
                act.wait_ge(in0, u + 1)
                stage(u + RING, idx0)

            def flush0(d, k):
                act.wait_ge(f_mv, d + 1)
                act.activation(sd[k][:, :], mv[k][:, 1:2], ACT.Sqrt, bias=eps_c[:, :]).then_inc(f_sd, 1)
                act.wait_ge(f_nm, d + 1)
                wait(act, h1_out[k], 8 * (d - k))
                act.activation(ho[k][:, :], hn[k][:, :], ACT.Relu, bias=nm[k][:, :],
                               scale=rs[k][:, :]).then_inc(f_h1, 1)
                act.dma_start(x1_tab[bass.ds(d * P, P), :], hn[k][:, :]).then_inc(x1_out[k], 16)
                act.wait_ge(f_h1, d + 1)
                act.dma_start(h1_tab[bass.ds(d * P, P), :], ho[k][:, :]).then_inc(h1_out[k], 16)

            def tile0(d, k):
                lo, hi = bounds(act, d)
                if not isinstance(d, int) or d >= 1:
                    flush0(prev(d), 1 - k)
                    if not isinstance(d, int) or d + 1 < NT:
                        n = LAST_ROWS if isinstance(d, int) and d + 1 == NT - 1 else P
                        act.dma_start(xt[1 - k][0:n, :], x[bass.ds((d + 1) * P, n), :]).then_inc(xl[1 - k], 16)
                rest_of(act, lo, hi, lambda u: new_pair0(u + 1))

            new_pair0(0)
            new_pair0(1)
            node_tiles(act, tile0)
            flush0(NT - 1, (NT - 1) % 2)

            act.wait_ge(in0, PAIRS)
            for u in range(RING):
                stage(u, idx1)
            for k in range(2):
                act.wait_ge(x1_out[k], 16 * ((NT + 1 - k) // 2))
            for k in range(2):
                act.wait_ge(h1_out[k], 16 * ((NT + 1 - k) // 2))

            def load_tile(d, k):
                act.dma_start(ho[k][:, :], h1_tab[bass.ds(d * P, P), :]).then_inc(hl[k], 16)

            def load_x1(d, k):
                act.dma_start(xt[k][:, :], x1_tab[bass.ds(d * P, P), :]).then_inc(x1l[k], 16)

            def new_pair1(d, u):
                act.wait_ge(in1, u + 1)
                act.wait_ge(done_b1, d + u)
                act.activation(ring(hi_r, u, WORK, GW), ring(g_ring, u, RING, GW), ACT.Copy).then_inc(hi1, 1)
                stage(u + RING, idx1)

            def mean1(d, k, lo):
                act.wait_ge(done_b1, d + lo + 3)
                wait(act, m_mtr, d - 1)
                act.activation(hn[k][:, :], ps[k][:, :], ACT.Copy, scale=rdeg[:, bass.ds(d, 1)]).then_inc(m_mn, 1)
                act.wait_ge(m_htr, d + 1)
                wait(act, m_self, d - 1)
                act.copy(hT[k][:, :], ps[4][:, :]).then_inc(m_hT, 1)
                act.wait_ge(m_mtr, d + 1)
                wait(act, m_y, d - 1)
                act.copy(mT[k][:, :], ps[5][:, :]).then_inc(m_mT, 1)

            def final1(d, k, n=P):
                act.wait_ge(n_mv, d + 1)
                act.activation(sd[k][:, :], mv[k][:, 1:2], ACT.Sqrt, bias=eps_c[:, :]).then_inc(n_sd, 1)
                act.wait_ge(n_o, d + 1)
                act.dma_start(out[bass.ds(d * P, n), :], yo[k][0:n, :]).then_inc(y_out[k], 16)

            def tile1(d, k):
                lo, hi = bounds(act, d)
                known = isinstance(d, int)
                if not known or d >= 1:
                    mean1(prev(d), 1 - k, lo)
                if not known or d >= 2:
                    final1(d - 2, k)
                    load_x1(d, k)
                else:
                    load_x1(d, k)
                if not known or d >= 1:
                    if not known or d + 1 < NT:
                        load_tile(d + 1, 1 - k)
                rest_of(act, lo, hi, lambda u: new_pair1(d, u + 1))

            load_tile(0, 0)
            load_tile(1, 1)
            new_pair1(0, 0)
            new_pair1(0, 1)
            node_tiles(act, tile1)
            mean1(NT - 1, 0, LAST_PAIR)
            final1(NT - 2, 1)
            final1(NT - 1, 0, LAST_ROWS)
            for k in range(2):
                act.wait_ge(y_out[k], 16 * ((NT + 1 - k) // 2))
            act.wait_ge(s_w1, 80)

        @block.tensor
        def _(pe):
            mm = nc.tensor.matmul

            pe.wait_ge(k_cf, 1)
            pe.wait_ge(e_f, 2)
            n = 0
            for part in (dst_cf, src_cf):
                for q in range(2):
                    wait(pe, e_ev, n - 1)
                    for b in range(4):
                        t = part[:, (4 * q + b) * P:(4 * q + b + 1) * P]
                        last = pe.transpose(ps[4 + n % 2][:, b * ROWS:(b + 1) * ROWS], t, ident[0:ROWS, 0:ROWS])
                    last.then_inc(e_tr, 1)
                    n += 1

            pe.wait_ge(s_w, 16)

            def project(i, k, n):
                pe.wait_ge(a_h0, i + 1)
                wait(pe, a_hT, i - 1)
                for c in range(KC):
                    last = pe.transpose(ps[k][:, c * P:(c + 1) * P], hn[k][:, c * P:(c + 1) * P], ident[:, :])
                last.then_inc(a_tr, 1)
                pe.wait_ge(a_hT, i + 1)
                wait(pe, a_hb, i - 1)
                for c in range(KC):
                    last = mm(ps[2 + k][:, :], hT[k][:, c * P:(c + 1) * P], w0[:, c * DIM:(c + 1) * DIM],
                              start=(c == 0), stop=(c == KC - 1))
                last.then_inc(a_mm, 1)

            tiles_by_two(pe, project)

            pe.wait_ge(s_dist, 32)
            for b in range(8):
                for q in range(2):
                    wait(pe, e_ev, n - 1)
                    for h in range(4):
                        t = dist_c[:, b * P * HEADS + 4 * q + h:(b + 1) * P * HEADS:HEADS]
                        last = pe.transpose(ps[4 + n % 2][:, h * ROWS:(h + 1) * ROWS], t, ident[0:ROWS, 0:ROWS])
                    last.then_inc(e_tr, 1)
                    n += 1

            pe.wait_ge(e_ev, 4)
            mm(ps[6][0:64, 0:PAIRS], pick_last[:, :], dst_e[:, 1::2], start=True, stop=True).then_inc(b_mm, 1)
            pe.wait_ge(b_cnt, 1)
            pe.transpose(ps[7][0:1, 0:64], cnt[:, :], ident[0:64, 0:64]).then_inc(b_tr, 1)

            pe.sem_inc(d_tr, 1)
            pe.sem_inc(d_mm, 1)
            pe.wait_ge(d_split, 5)

            def step_d(d, u):
                s = d + u
                pe.wait_ge(d_oh, s + 1)
                pe.wait_ge(d_cp, s + 1)
                for i in range(2):
                    last = pe.transpose(ps[2][:, i * P // 2:(i + 1) * P // 2].bitcast(BF16),
                                        oh_b[:, i * P:(i + 1) * P], ident_b[:, :])
                last.then_inc(d_tr, 1)
                pe.wait_ge(d_cp, s + 2)
                pe.wait_ge(d_red, s + 1)
                for i in range(2):
                    last = mm(ps[3][:, i * 3 * HEADS:(i + 1) * 3 * HEADS], ohT_b[:, i * P:(i + 1) * P],
                              ed3[:, bass.ds(d * 3 * HEADS, 3 * HEADS)], start=True, stop=True)
                last.then_inc(d_mm, 1)

            def tile_d(d, k):
                lo, hi = bounds(pe, d)
                step_d(d, lo)
                rest_of(pe, lo, hi, lambda u: step_d(d, u))

            pe.wait_ge(b_code, 1)
            pe.sem_inc(d_cp, 1)
            node_tiles(pe, tile_d)

            for k in range(2):
                pe.wait_ge(es_mv[k], 16 * ((TPC + 1 - k) // 2))
            for g in range(0, TPC, 4):
                wait(pe, t_cp, g // 4 - 1)
                for j in range(g, min(g + 4, TPC)):
                    last = pe.transpose(ps[g // 4 % 2][:, (j - g) * P:(j - g + 1) * P], es_all[:, j * P:(j + 1) * P],
                                        ident[:, :])
                last.then_inc(t_tr, 1)
            pe.wait_ge(t_v, 6)
            for q in range(4):
                last = pe.transpose(ps[2][0:1, q * P:(q + 1) * P], ends[:, q:q + 1], ident[:, :])
            last.then_inc(t_pe, 1)
            pe.wait_ge(t_v, 20)
            for q in range(2):
                last = pe.transpose(ps[3][:, q:q + 1], inits[q][0:1, :], ident[0:1, 0:1])
            last.then_inc(t_pe, 1)
            pe.wait_ge(t_v, 23)
            for g in range(0, TPC, 4):
                wait(pe, t_z, g // 4 - 1)
                for j in range(g, min(g + 4, TPC)):
                    last = pe.transpose(ps[g // 4 % 2][:, (j - g) * P:(j - g + 1) * P], scan[:, j * P:(j + 1) * P],
                                        ident[:, :])
                last.then_inc(t_bt, 1)

            pe.sem_inc(done_a0, 1)
            pe.sem_inc(done_b0, 2)
            pe.wait_ge(t_co, 2)

            def step0(d, u, k, start):
                s = d + u
                pe.wait_ge(msg0, u + 1)
                for t, (ready, done) in enumerate(((oh_a0, done_a0), (oh_b0, done_b0))):
                    pe.wait_ge(ready, s + 1)
                    mm(ps[k][:, :], oh[t][:, :], msg[:, bass.ds((u % WORK) * GW + t * DIM, DIM)],
                       start=start and t == 0, stop=True, skip_group_check=True)
                    mm(ps[2 + k][:, 0:EW], oh[t][:, :], ex_buf[:, bass.ds((2 * u + t) * EW, EW)],
                       start=start and t == 0, stop=True, skip_group_check=True).then_inc(done, 1)

            def tile0(d, k):
                lo, hi = bounds(pe, d)
                wait(pe, f_w, d - 1)
                step0(d, lo, k, True)
                rest_of(pe, lo, hi, lambda u: step0(d, u, k, False))

            node_tiles(pe, tile0)

            pe.sem_inc(done_a1, 1)
            pe.sem_inc(done_b1, 2)
            pe.wait_ge(s_w1, 80)

            def step1(d, u, k, start):
                s = d + u
                pe.wait_ge(lo1, u + 1)
                for t, (ready, done) in enumerate(((oh_a1, done_a1), (oh_b1, done_b1))):
                    pe.wait_ge(ready, s + 1)
                    for part in (hi_r, lo_r):
                        last = mm(ps[k][:, :], ohr[t][:, :], part[:, bass.ds((u % WORK) * GW + t * DIM, DIM)],
                                  start=start and t == 0 and part is hi_r, stop=True, skip_group_check=True)
                    last.then_inc(done, 1)

            def update1(d, k, n):
                pe.wait_ge(hl[k], n)
                wait(pe, m_hT, d)
                for c in range(KC):
                    last = pe.transpose(ps[4][:, c * P:(c + 1) * P], ho[k][:, c * P:(c + 1) * P], ident[:, :])
                last.then_inc(m_htr, 1)
                pe.wait_ge(m_mn, d + 1)
                wait(pe, m_mT, d)
                for c in range(KC):
                    last = pe.transpose(ps[5][:, c * P:(c + 1) * P], hn[k][:, c * P:(c + 1) * P], ident[:, :])
                last.then_inc(m_mtr, 1)
                pe.wait_ge(m_hT, d + 1)
                wait(pe, n_y, d - 1)
                for c in range(KC):
                    last = mm(ps[6 + k][:, :], hT[k][:, c * P:(c + 1) * P], ws[:, c * DIM:(c + 1) * DIM],
                              start=(c == 0), stop=False)
                last.then_inc(m_self, 1)
                pe.wait_ge(m_mT, d + 1)
                for c in range(KC):
                    last = mm(ps[6 + k][:, :], mT[k][:, c * P:(c + 1) * P], wn[:, c * DIM:(c + 1) * DIM],
                              start=False, stop=(c == KC - 1))
                last.then_inc(m_y, 1)

            def tile1(d, k):
                lo, hi = bounds(pe, d)
                wait(pe, m_mn, d - 1)
                step1(d, lo, k, True)
                if not isinstance(d, int) or d >= 1:
                    update1(prev(d), 1 - k, 8 * (d - 1 - (1 - k)) + 16)
                rest_of(pe, lo, hi, lambda u: step1(d, u, k, False))

            node_tiles(pe, tile1)
            update1(NT - 1, 0, 8 * (NT - 1) + 16)

        @block.vector
        def _(dve):
            tt, ts, stt = nc.vector.tensor_tensor, nc.vector.tensor_scalar, nc.vector.scalar_tensor_tensor
            copy = nc.vector.tensor_copy

            dve.memset(dist_c, 0.0).then_inc(padded, 1)
            dve.memset(dst_s[96:P, :], PAD_DST).then_inc(padded, 1)
            dve.memset(eps_c[:, :], EPS)
            dve.memset(src_e[:, TILES:], 0)
            dve.wait_ge(k_cst, 3)
            copy(iota_f[:, :], iota_i[:, :])
            copy(first_f[:, :], first_i[:, :])
            copy(thr_f[:, :], thr_i[:, :])
            dve.wait_ge(k_id, 4)
            copy(ident_b[:, :], ident[:, :]).then_inc(k_cf, 1)
            dve.wait_ge(s_ec, 64)
            copy(dst_cf, dst_c).then_inc(e_f, 1)
            copy(src_cf, src_c).then_inc(e_f, 1)
            n = 0
            for part in (dst_e, src_e):
                for q in range(2):
                    dve.wait_ge(e_tr, n + 1)
                    o = part[:, 0:TILES].rearrange("p (a b) -> p b a", b=8)[:, 4 * q:4 * q + 4, :]
                    copy(o, ps[4 + n % 2][:, 0:4 * ROWS].rearrange("p (b a) -> p b a", b=4)).then_inc(e_ev, 1)
                    n += 1
            dve.wait_ge(e_ev, 4)
            copy(src_g[:, :].rearrange("p (j c) -> p j c", c=CHUNKS),
                 src_e[:, 0:TILES].rearrange("p (c j) -> p j c", c=CHUNKS)).then_inc(e_sg, 1)
            dve.wait_ge(s_row, 48)

            def stats(src_t, k, s_st, s_mv, d):
                dve.bn_stats(st[k][:, :], src_t).then_inc(s_st, 1)
                dve.wait_ge(s_st, d + 1)
                dve.sem_inc(v_go, 1)
                dve.bn_aggr(mv[k][:, :], st[k][:, :]).then_inc(s_mv, 1)

            def scale_and_shift(k, s_mv, s_sd, s_rs, s_nm, d):
                dve.wait_ge(s_sd, d + 1)
                dve.reciprocal(rs[k][:, :], sd[k][:, :]).then_inc(s_rs, 1)
                dve.wait_ge(s_rs, d + 1)
                stt(nm[k][:, :], mv[k][:, 0:1], -1.0, rs[k][:, :], ALU.mult, ALU.mult).then_inc(s_nm, 1)

            def norm_stats(i, k, n):
                dve.wait_ge(x_in[k], 16 * (n + 1))
                stats(xt[k][:, :], k, a_st, a_mv, i)
                wait(dve, a_h0, i - 1)
                scale_and_shift(k, a_mv, a_sd, a_rs, a_nm, i)

            def head_terms(i, k, n):
                dve.wait_ge(a_mm, i + 1)
                wait(dve, h_out[k], 16 * n)
                wait(dve, a_md, i - 1)
                tt(ho[k][:, :], ps[2 + k][:, :], row_b0[:, :], ALU.add).then_inc(a_hb, 1)
                dve.wait_ge(a_hb, i + 1)
                stt(ho[k][:, :], ho[k][:, :], SLOPE, ho[k][:, :], ALU.mult, ALU.max).then_inc(a_h, 1)

            def head_sums(i, k, n):
                dve.wait_ge(a_ms, i + 1)
                wait(dve, es_out[k], 16 * n)
                dve.tensor_reduce(es_st[k][:, :], ms[k][:, :].rearrange("p (h e) -> p h e", h=HEADS), AX.X,
                                  ALU.add).then_inc(a_es, 1)
                dve.wait_ge(a_md, i + 1)
                dve.tensor_reduce(ed_n[:, bass.ds(i * HEADS, HEADS)],
                                  md[k][:, :].rearrange("p (h e) -> p h e", h=HEADS), AX.X, ALU.add).then_inc(a_ed, 1)

            norm_stats(0, 0, 0)
            norm_stats(1, 1, 0)
            head_terms(0, 0, 0)
            norm_stats(2, 0, 1)
            head_sums(0, 0, 0)
            head_terms(1, 1, 0)
            with dve.Fori(1, NT // 2) as j:
                norm_stats(2 * j + 1, 1, j)
                head_sums(2 * j - 1, 1, j - 1)
                head_terms(2 * j, 0, j)
                norm_stats(2 * j + 2, 0, j + 1)
                head_sums(2 * j, 0, j)
                head_terms(2 * j + 1, 1, j)
            head_sums(NT - 2, 1, NT // 2 - 1)
            head_terms(NT - 1, 0, NT // 2)
            head_sums(NT - 1, 0, NT // 2)

            for b in range(8):
                for q in range(2):
                    dve.wait_ge(e_tr, n + 1)
                    o = coef[:, :].rearrange("p (a b h) -> p b h a", b=8, h=HEADS)[:, b, 4 * q:4 * q + 4, :]
                    copy(o, ps[4 + n % 2][:, 0:4 * ROWS].rearrange("p (h a) -> p h a", h=4)).then_inc(e_ev, 1)
                    n += 1

            dve.wait_ge(b_mm, 1)
            ts(lst[:, :], ps[6][0:64, 0:PAIRS], thr_f[0:64, :], None, ALU.is_lt, ALU.add,
               accum_out=cnt[:, :]).then_inc(b_cnt, 1)
            dve.wait_ge(b_tr, 1)
            copy(bnd_f[:, :], ps[7][0:1, 0:64]).then_inc(b_row, 1)
            dve.wait_ge(b_row, 1)
            stt(code_f[:, 0:63], bnd_f[:, 0:63], float(CODE), bnd_f[:, 1:64], ALU.mult, ALU.add).then_inc(b_row, 1)
            dve.wait_ge(b_row, 2)
            copy(code[:, 0:63], code_f[:, 0:63]).then_inc(b_code, 1)

            parts = ed3[:, :].rearrange("p (d q h) -> p q d h", q=3, h=HEADS)
            nodes = ed_n[:, :].rearrange("p (d h) -> p d h", h=HEADS)
            rest = ed_r[:, :].rearrange("p (d h) -> p d h", h=HEADS)
            dve.wait_ge(a_ed, NT)
            copy(parts[:, 0], nodes).then_inc(d_split, 1)
            dve.wait_ge(d_split, 1)
            tt(rest, nodes, parts[:, 0], ALU.subtract).then_inc(d_split, 1)
            dve.wait_ge(d_split, 2)
            copy(parts[:, 1], rest).then_inc(d_split, 1)
            dve.wait_ge(d_split, 3)
            tt(rest, rest, parts[:, 1], ALU.subtract).then_inc(d_split, 1)
            dve.wait_ge(d_split, 4)
            copy(parts[:, 2], rest).then_inc(d_split, 1)

            dve.wait_ge(s_ds, 16 * CHUNKS)
            tt(same[:, 1:CHUNK], dst_s[:, 1:CHUNK], dst_s[:, 0:CHUNK - 1], ALU.is_equal).then_inc(e_same, 1)
            copy(ends[:, 2:3], dst_s[:, 0:1])
            copy(ends[:, 3:4], dst_s[:, CHUNK - 1:CHUNK]).then_inc(e_same, 1)
            dve.wait_ge(e_same, 1)
            ts(same[:, 1:CHUNK], same[:, 1:CHUNK], 2 * BIG, -BIG, ALU.mult, ALU.add).then_inc(e_same, 1)
            dve.memset(same[:, 0:1], BIG)
            dve.memset(same[:, CHUNK:CHUNK + 1], BIG)
            dve.wait_ge(e_tr, 20)
            dve.memset(ed_e, 0.0).then_inc(d_zero, 1)
            dve.memset(ex3[:, :, HEADS:EW], 1.0)

            def new_iod(d, k, signal):
                ts(iod[k][:, :], iota_f[:, :], first_f[:, bass.ds(d, 1)], None, ALU.add).then_inc(signal, 1)
                dve.wait_ge(signal, d + 1)

            def hot_d(d, u, k):
                dve.wait_ge(d_tr, d + u + 1)
                ts(oh_b[:, 0:P], iod[k][:, :], dst_e[:, bass.ds(2 * u, 1)], None, ALU.is_equal)
                ts(oh_b[:, P:2 * P], iod[k][:, :], dst_e[:, bass.ds(2 * u + 1, 1)], None, ALU.is_equal).then_inc(d_oh, 1)

            def add_d(s, u):
                dve.wait_ge(d_mm, s + 2)
                wait(dve, d_add, s)
                dve.tensor_reduce(red[:, :].rearrange("p (i h) -> p i h", i=2),
                                  ps[3][:, 0:6 * HEADS].rearrange("p (i q h) -> p i h q", i=2, q=3), AX.X,
                                  ALU.add).then_inc(d_red, 1)
                dve.wait_ge(d_red, s + 2)
                o = ed_e[:, bass.ds(2 * u * HEADS, 2 * HEADS)]
                tt(o, o, red[:, :], ALU.add).then_inc(d_add, 1)

            def tile_d(d, k):
                lo, hi = bounds(dve, d)
                new_iod(d, k, d_iod)
                hot_d(d, lo, k)
                if not isinstance(d, int) or d >= 1:
                    add_d(d + lo - 1, lo)

                def body(u):
                    hot_d(d, u, k)
                    add_d(d + u - 1, u - 1)
                rest_of(dve, lo, hi, body)

            dve.sem_inc(d_red, 1)
            dve.wait_ge(d_zero, 1)
            dve.wait_ge(b_code, 1)
            node_tiles(dve, tile_d)
            add_d(NT - 1 + LAST_PAIR, LAST_PAIR)

            for k in range(2):
                dve.wait_ge(es_mv[k], 16 * ((TPC + 1 - k) // 2))
            dve.wait_ge(d_add, NT + LAST_PAIR)
            by_group = "p (c j h) -> p j c h"
            tt(ex3[:, :, 0:HEADS].rearrange("p (c j) h -> p j c h", j=TPC),
               es_all.rearrange("p (j c h) -> p j c h", c=CHUNKS, h=HEADS),
               ed_e.rearrange(by_group, c=CHUNKS, h=HEADS), ALU.add).then_inc(t_x, 1)
            dve.wait_ge(t_cp, -(-TPC // 4))
            dve.wait_ge(e_same, 3)
            v = [0]

            def link(ins):
                v[0] += 1
                ins.then_inc(t_v, 1)
                dve.wait_ge(t_v, v[0])

            def forward(initial):
                return dve.tensor_tensor_scan(fwd, same[:, 0:CHUNK], scan[:, :], initial, ALU.min, ALU.max)

            def backward(o, initial):
                return dve.tensor_tensor_scan(o[:, ::-1], same[:, CHUNK:0:-1], fwd[:, ::-1], initial, ALU.min, ALU.max)

            dve.wait_ge(t_x, 1)
            link(forward(-BIG))
            link(copy(ends[:, 1:2], fwd[:, CHUNK - 1:CHUNK]))
            link(backward(fwd, -BIG))
            link(copy(ends[:, 0:1], fwd[:, 0:1]))
            link(dve.memset(cont[:, :], -BIG))
            link(dve.memset(kl[:, :], -BIG))
            dve.wait_ge(t_pe, 1)
            link(copy(rows[:, :], ps[2][0:1, :]))
            first_mx, last_mx, first_d, last_d = (rows[:, q * P:(q + 1) * P] for q in range(4))
            link(tt(cont[:, HEADS:P], first_d[:, HEADS:P], last_d[:, 0:P - HEADS], ALU.is_equal))
            link(ts(cont[:, HEADS:P], cont[:, HEADS:P], 2 * BIG, -BIG, ALU.mult, ALU.add))
            link(tt(one[:, :], first_d, last_d, ALU.is_equal))
            link(ts(one[:, :], one[:, :], 2 * BIG, -BIG, ALU.mult, ALU.add))
            link(tt(kl[:, :], cont[:, :], one[:, :], ALU.min))
            for h in range(HEADS):
                last = dve.tensor_tensor_scan(outr[:, h::HEADS], kl[:, h::HEADS], last_mx[:, h::HEADS], -BIG,
                                              ALU.min, ALU.max)
            link(last)
            link(dve.memset(inits[0][:, :], -BIG))
            link(tt(inits[0][:, HEADS:P], cont[:, HEADS:P], outr[:, 0:P - HEADS], ALU.min))
            link(dve.memset(kl[:, :], -BIG))
            link(tt(kl[:, 0:P - HEADS], cont[:, HEADS:P], one[:, 0:P - HEADS], ALU.min))
            for h in range(HEADS):
                last = dve.tensor_tensor_scan(outr[:, h::HEADS][:, ::-1], kl[:, h::HEADS][:, ::-1],
                                              first_mx[:, h::HEADS][:, ::-1], -BIG, ALU.min, ALU.max)
            link(last)
            link(dve.memset(inits[1][:, :], -BIG))
            link(tt(inits[1][:, 0:P - HEADS], cont[:, HEADS:P], outr[:, HEADS:P], ALU.min))
            assert v[0] == 20
            dve.wait_ge(t_pe, 2)
            link(copy(init_c[:, :], ps[3][:, 0:2]))
            link(forward(init_c[:, 0:1]))
            link(backward(scan[:, :], init_c[:, 1:2]))
            assert v[0] == 23

            n_g4 = -(-TPC // 4)
            for g in range(0, TPC, 4):
                m = min(4, TPC - g)
                dve.wait_ge(t_bt, g // 4 + 1)
                sel = slice(g, g + m)
                tt(mx_e.rearrange(by_group, c=CHUNKS, h=HEADS)[:, sel],
                   ps[g // 4 % 2][:, 0:m * P].rearrange("p (j c h) -> p j c h", c=CHUNKS, h=HEADS),
                   ed_e.rearrange(by_group, c=CHUNKS, h=HEADS)[:, sel], ALU.add).then_inc(t_z, 1)
            dve.wait_ge(t_z, n_g4)
            link(stt(mx_e, mx_e, SLOPE, mx_e, ALU.mult, ALU.max))
            e8 = ex3[:, :, 0:HEADS]
            link(stt(e8, e8, SLOPE, e8, ALU.mult, ALU.max))
            tt(e8, e8, mx_e.rearrange("p (t h) -> p t h", h=HEADS), ALU.subtract).then_inc(t_e, 1)
            dve.wait_ge(t_ex, 1)
            c8 = coef[:, :].rearrange("p (t h) -> p t h", h=HEADS)
            dve.wait_ge(e_ev, 20)
            tt(c8, c8, e8, ALU.mult).then_inc(t_co, 1)
            dve.memset(iod[0][0:1, 0:1], 0.0).then_inc(t_co, 1)
            dve.wait_ge(t_co, 2)

            def new_pair0(d, u):
                dve.wait_ge(in0, u + 1)
                dve.wait_ge(done_b0, d + u)
                tt(ring(msg, u, WORK, GW).rearrange("p (a e) -> p a e", e=HEAD_DIM),
                   ring(g_ring, u, RING, GW).rearrange("p (a e) -> p a e", e=HEAD_DIM),
                   coef[:, bass.ds(2 * u * HEADS, 2 * HEADS)].unsqueeze(2).to_broadcast([P, 2 * HEADS, HEAD_DIM]),
                   ALU.mult).then_inc(msg0, 1)

            def hot(d, u, k, pairs):
                s = d + u
                for t, (buf, ready, done, credit) in enumerate(pairs):
                    dve.wait_ge(done, s + credit)
                    ts(buf[:, :], iod[k][:, :], dst_e[:, bass.ds(2 * u + t, 1)], None, ALU.is_equal).then_inc(ready, 1)

            def flush0(d, k, lo):
                dve.wait_ge(done_b0, d + lo + 3)
                ts(r9[k][:, 0:HEADS], ps[2 + k][:, 0:HEADS], 0.5, None, ALU.max)
                ts(r9[k][:, HEADS:EW], ps[2 + k][:, HEADS:EW], 1.0, None, ALU.max).then_inc(f_r9, 1)
                dve.wait_ge(f_r9, d + 1)
                dve.reciprocal(rr[k][:, :], r9[k][:, :]).then_inc(f_rr, 1)
                dve.wait_ge(f_rr, d + 1)
                copy(rdeg[:, bass.ds(d, 1)], rr[k][:, HEADS:EW])
                wait(dve, x1_out[k], 8 * (d - k))
                wait(dve, f_h1, d - 1)
                tt(hn[k][:, :].rearrange("p (h e) -> p h e", h=HEADS),
                   ps[k][:, :].rearrange("p (h e) -> p h e", h=HEADS),
                   rr[k][:, 0:HEADS].unsqueeze(2).to_broadcast([P, HEADS, HEAD_DIM]), ALU.mult).then_inc(f_w, 1)
                dve.wait_ge(f_w, d + 1)
                dve.wait_ge(xl[k], 8 * (d - k) + 16)
                tt(hn[k][:, :], hn[k][:, :], xt[k][:, :], ALU.add).then_inc(f_x1, 1)
                dve.wait_ge(f_x1, d + 1)
                stats(hn[k][:, :], k, f_st, f_mv, d)
                scale_and_shift(k, f_mv, f_sd, f_rs, f_nm, d)

            hot0 = ((oh[0], oh_a0, done_a0, 1), (oh[1], oh_b0, done_b0, 2))

            def tile0(d, k):
                lo, hi = bounds(dve, d)
                new_iod(d, k, iod0)
                hot(d, lo, k, hot0)
                if not isinstance(d, int) or d >= 1:
                    flush0(prev(d), 1 - k, lo)

                def body(u):
                    hot(d, u, k, hot0)
                    new_pair0(d, u + 1)
                rest_of(dve, lo, hi, body)

            new_pair0(1, 0)
            new_pair0(1, 1)
            node_tiles(dve, tile0)
            flush0(NT - 1, 0, LAST_PAIR)

            hot1 = ((ohr[0], oh_a1, done_a1, 1), (ohr[1], oh_b1, done_b1, 2))

            def new_pair1(u):
                dve.wait_ge(hi1, u + 1)
                tt(ring(lo_r, u, WORK, GW), ring(g_ring, u, RING, GW), ring(hi_r, u, WORK, GW).bitcast(F32),
                   ALU.subtract).then_inc(lo1, 1)

            def final1(d, k):
                dve.wait_ge(m_y, d + 1)
                wait(dve, y_out[k], 8 * (d - k))
                tt(yo[k][:, :], ps[6 + k][:, :], row_bias[:, :], ALU.add).then_inc(n_y, 1)
                dve.wait_ge(n_y, d + 1)
                stats(yo[k][:, :], k, n_st, n_mv, d)
                scale_and_shift(k, n_mv, n_sd, n_rs, n_nm, d)
                dve.wait_ge(n_nm, d + 1)
                ts(yo[k][:, :], yo[k][:, :], rs[k][:, :], nm[k][:, :], ALU.mult, ALU.add).then_inc(n_yn, 1)
                dve.wait_ge(n_yn, d + 1)
                tt(yo[k][:, :], yo[k][:, :], row_gamma[:, :], ALU.mult).then_inc(n_g, 1)
                dve.wait_ge(n_g, d + 1)
                tt(yo[k][:, :], yo[k][:, :], row_beta[:, :], ALU.add).then_inc(n_b, 1)
                dve.wait_ge(n_b, d + 1)
                dve.wait_ge(x1l[k], 8 * (d - k) + 16)
                tt(yo[k][:, :], yo[k][:, :], xt[k][:, :], ALU.add).then_inc(n_o, 1)

            def tile1(d, k):
                lo, hi = bounds(dve, d)
                new_iod(d, k, iod1)
                hot(d, lo, k, hot1)
                if not isinstance(d, int) or d >= 2:
                    final1(d - 2, k)

                def body(u):
                    hot(d, u, k, hot1)
                    new_pair1(u + 1)
                rest_of(dve, lo, hi, body)

            new_pair1(0)
            new_pair1(1)
            node_tiles(dve, tile1)
            final1(NT - 2, 1)
            final1(NT - 1, 0)


def kernel(x, src, dst, edge_attr_8, L0_gnn_W, L0_gnn_b, L0_gnn_w_att_src, L0_gnn_w_att_dst,
           L1_gnn_W_self, L1_gnn_W_neigh, L1_gnn_bias, L1_gnn_gamma, L1_gnn_beta):
    import numpy as np
    import concourse.bacc as bacc
    from concourse.bass_utils import run_bass_kernel_spmd

    arrays = {
        "x": np.asarray(x), "src": np.asarray(src), "dst": np.asarray(dst), "dist": np.asarray(edge_attr_8),
        "w0t": np.asarray(L0_gnn_W).T, "b0": np.asarray(L0_gnn_b),
        "att_src": np.asarray(L0_gnn_w_att_src).reshape(-1), "att_dst": np.asarray(L0_gnn_w_att_dst).reshape(-1),
        "wst": np.asarray(L1_gnn_W_self).T, "wnt": np.asarray(L1_gnn_W_neigh).T, "bias": np.asarray(L1_gnn_bias),
        "gamma": np.asarray(L1_gnn_gamma), "beta": np.asarray(L1_gnn_beta),
    }
    arrays = {k: np.ascontiguousarray(a) for k, a in arrays.items()}
    nc = bacc.Bacc("TRN2", target_bir_lowering=False, num_devices=1)
    args = [nc.dram_tensor(k, a.shape, mybir.dt.from_np(a.dtype), kind="ExternalInput").ap()
            for k, a in arrays.items()]
    out = nc.dram_tensor("out", (N_NODES, DIM), F32, kind="ExternalOutput").ap()
    gnn_kernel(nc, *args, out)
    return run_bass_kernel_spmd(nc, [arrays], core_ids=[0]).results[0]["out"]
```

```python
import concourse.bass as bass
from concourse import mybir
from contextlib import ExitStack

F32 = mybir.dt.float32
F32R = mybir.dt.float32r
BF16 = mybir.dt.bfloat16
I32 = mybir.dt.int32
ALU = mybir.AluOpType
ACT = mybir.ActivationFunctionType
AX = mybir.AxisListType

N_NODES, N_EDGES, DIM, HEADS = 6250, 100000, 512, 8
HEAD_DIM = DIM // HEADS
P = 128
KC = DIM // P
NT = -(-N_NODES // P)
LAST_ROWS = N_NODES - (NT - 1) * P
CHUNKS = P // HEADS
TILES = -(-N_EDGES // (P * CHUNKS)) * CHUNKS
TPC = TILES // CHUNKS
CHUNK = TPC * P
PAIRS = TILES // 2
LAST_PAIR = (N_EDGES - 1) // (2 * P)
ROWS = TILES // 8
ROW_EDGES = 8 * P
FULL_ROWS = N_EDGES // ROW_EDGES
REST = N_EDGES - FULL_ROWS * ROW_EDGES
FULL_TILES = N_EDGES // P
BUCKETS = NT + 1
PAD_DST = 8000
BIG = 1e38
EPS = 1e-5
SLOPE = 0.2
RING = 8
WORK = 3
GW = 2 * DIM
EW = HEADS + 1
COUNT_STEPS, PLACE_STEPS = 8, 17
CODE = 512


def wait(eng, sem, value):
    if not (isinstance(value, int) and value <= 0):
        eng.wait_ge(sem, value)


def ring(buf, u, depth, width):
    return buf[:, bass.ds((u % depth) * width, width)]


def gnn_kernel(nc, x, src, dst, dist, w0t, b0, att_src, att_dst, wst, wnt, bias, gamma, beta, out):
    h_tab = nc.dram_tensor("h_tab", (NT * P, DIM), F32).ap()
    es_tab = nc.dram_tensor("es_tab", (NT * P, HEADS), F32).ap()
    x1_tab = nc.dram_tensor("x1_tab", (NT * P, DIM), F32).ap()
    h1_tab = nc.dram_tensor("h1_tab", (NT * P, DIM), F32).ap()
    dst_tab = nc.dram_tensor("dst_tab", (TILES * P, 1), I32).ap()
    src_tab = nc.dram_tensor("src_tab", (TILES * P, 1), I32).ap()
    dist_tab = nc.dram_tensor("dist_tab", (TILES * P, HEADS), F32).ap()

    ctx = ExitStack()
    with ctx:
        def sb(name, shape, dt=F32):
            return ctx.enter_context(nc.sbuf_tensor(name, shape, dt))

        def sem(name):
            return ctx.enter_context(nc.semaphore(name))

        ident = sb("ident", [P, P])
        ident_b = sb("ident_b", [P, P], BF16)
        iota_i = sb("iota_i", [P, P], I32)
        iota_f = sb("iota_f", [P, P])
        first_i = sb("first_i", [P, NT + 1], I32)
        first_f = sb("first_f", [P, NT + 1])
        thr_i = sb("thr_i", [P, 1], I32)
        thr_f = sb("thr_f", [P, 1])
        pick_last = sb("pick_last", [P, 64])
        eps_c = sb("eps_c", [P, 1])
        row_b0 = sb("row_b0", [P, DIM])
        row_as = sb("row_as", [P, DIM])
        row_ad = sb("row_ad", [P, DIM])
        src_e = sb("src_e", [P, TILES + 2 * (RING + 1)], I32)
        src_g = sb("src_g", [P, TILES], I32)
        dst_e = sb("dst_e", [P, TILES])
        same = sb("same", [P, CHUNK + 1], BF16)
        ex_buf = sb("ex_buf", [P, TILES * EW])
        coef = sb("coef", [P, TILES * HEADS])
        scan = sb("scan", [P, CHUNK])
        idx_ring = sb("idx_ring", [P, RING * 2], I32)
        xt = [sb(f"xt{k}", [P, DIM]) for k in range(2)]
        hn = [sb(f"hn{k}", [P, DIM]) for k in range(2)]
        hT = [sb(f"hT{k}", [P, DIM]) for k in range(2)]
        ho = [sb(f"ho{k}", [P, DIM]) for k in range(2)]
        st = [sb(f"st{k}", [P, 6]) for k in range(2)]
        mv = [sb(f"mv{k}", [P, 2]) for k in range(2)]
        sd = [sb(f"sd{k}", [P, 1]) for k in range(2)]
        rs = [sb(f"rs{k}", [P, 1]) for k in range(2)]
        nm = [sb(f"nm{k}", [P, 1]) for k in range(2)]
        es_st = [sb(f"es_st{k}", [P, HEADS]) for k in range(2)]
        ed_n = sb("ed_n", [P, NT * HEADS])
        ed_r = sb("ed_r", [P, NT * HEADS])
        ed3 = sb("ed3", [P, NT * 3 * HEADS], BF16)
        rdeg = sb("rdeg", [P, NT])
        cnt = sb("cnt", [64, 1])
        falls = sb("falls", [P, 1])
        ones_c = sb("ones_c", [P, 1])
        flag = sb("flag", [1, 1], I32)
        bnd_f = sb("bnd_f", [1, 64])
        code_f = sb("code_f", [1, 64])
        code = sb("code", [1, 64], I32)
        iod = [sb(f"iod{k}", [P, P]) for k in range(2)]
        oh_b = sb("oh_b", [P, 2 * P], BF16)
        ohT_b = sb("ohT_b", [P, 2 * P], BF16)
        red = sb("red", [P, 2 * HEADS])
        oh_first = [sb(f"oh_first{t}", [P, P]) for t in range(2)]
        oh_rest = [sb(f"oh_rest{t}", [P, P]) for t in range(2)]
        ohr_first = [sb(f"ohr_first{t}", [P, P], F32R) for t in range(2)]
        ohr_rest = [sb(f"ohr_rest{t}", [P, P], F32R) for t in range(2)]
        st_i = [sb(f"st_i{k}", [P, CHUNKS], I32) for k in range(2)]
        es_r = [sb(f"es_r{k}", [P, P]) for k in range(2)]
        ends = sb("ends", [P, 4])
        rows = sb("rows", [1, 4 * P])
        cont = sb("cont", [1, P])
        one = sb("one", [1, P])
        kl = sb("kl", [1, P])
        outr = sb("outr", [1, P])
        inits = [sb(f"inits{k}", [1, P]) for k in range(2)]
        init_c = sb("init_c", [P, 2])
        r9 = [sb(f"r9{k}", [P, EW]) for k in range(2)]
        rr = [sb(f"rr{k}", [P, EW]) for k in range(2)]

        with nc.sbuf_tensor("edf", [P, 2 * CHUNK], F32) as edf:
            pass
        with nc.sbuf_tensor("msg", [P, WORK * GW], F32) as msg:
            pass
        hi_r = sb("hi_r", [P, WORK * GW], F32R)
        lo_r = sb("lo_r", [P, WORK * GW], F32R)
        mT = [sb(f"mT{k}", [P, DIM]) for k in range(2)]
        yo = [sb(f"yo{k}", [P, DIM]) for k in range(2)]
        g_ring = sb("g_ring", [P, RING * GW])

        ps = [ctx.enter_context(nc.psum_tensor(f"bank{b}", [P, 512], F32)) for b in range(8)]

        below = hn[0][0:64, 0:PAIRS]
        src_c = ex_buf[0:ROWS, 0:ROW_EDGES].bitcast(I32)
        dst_c = ex_buf[0:ROWS, ROW_EDGES:2 * ROW_EDGES].bitcast(I32)
        src_cf = ex_buf[0:ROWS, 2 * ROW_EDGES:3 * ROW_EDGES]
        dst_cf = ex_buf[0:ROWS, 3 * ROW_EDGES:4 * ROW_EDGES]
        dst_next = ex_buf[0:ROWS, 4 * ROW_EDGES:5 * ROW_EDGES].bitcast(I32)
        dist_c = edf[0:ROWS, 0:ROW_EDGES * HEADS]
        dst_s = scan[:, :].bitcast(I32)
        ed_e = edf[:, 0:CHUNK]
        es_all = edf[:, CHUNK:2 * CHUNK]
        fwd = edf[:, CHUNK:2 * CHUNK]
        mx_e = edf[:, CHUNK:2 * CHUNK]
        ws = scan[:, 0:KC * DIM]
        wn = scan[:, KC * DIM:2 * KC * DIM]
        late = RING * GW - 2 * KC * DIM
        w0 = g_ring[:, late:late + KC * DIM]
        ms, md = ([g_ring[:, late + (KC + 2 * q + k) * DIM:late + (KC + 2 * q + k + 1) * DIM] for k in range(2)]
                  for q in range(2))
        row_bias, row_gamma, row_beta = (scan[:, (2 * KC + q) * DIM:(2 * KC + q + 1) * DIM] for q in range(3))
        ex3 = ex_buf[:, :].rearrange("p (t h) -> p t h", h=EW)

        s_w = sem("s_w"); s_row = sem("s_row"); s_ec = sem("s_ec"); s_dist = sem("s_dist"); s_ds = sem("s_ds"); s_w1 = sem("s_w1")
        padded = sem("padded"); p_go = sem("p_go"); v_go = sem("v_go")
        k_id = sem("k_id"); k_cst = sem("k_cst"); k_cf = sem("k_cf")
        e_f = sem("e_f"); e_tr = sem("e_tr"); e_ev = sem("e_ev"); e_same = sem("e_same"); e_sg = sem("e_sg")
        b_mm = sem("b_mm"); b_cnt = sem("b_cnt"); b_tr = sem("b_tr"); b_row = sem("b_row"); b_code = sem("b_code")
        x_in = [sem(f"x_in{k}") for k in range(2)]
        h_out = [sem(f"h_out{k}") for k in range(2)]
        es_out = [sem(f"es_out{k}") for k in range(2)]
        a_st = sem("a_st"); a_mv = sem("a_mv"); a_sd = sem("a_sd"); a_rs = sem("a_rs"); a_nm = sem("a_nm")
        a_h0 = sem("a_h0"); a_tr = sem("a_tr"); a_hT = sem("a_hT"); a_mm = sem("a_mm"); a_hb = sem("a_hb")
        a_h = sem("a_h"); a_ms = sem("a_ms"); a_md = sem("a_md"); a_es = sem("a_es"); a_ed = sem("a_ed")
        d_split = sem("d_split")
        st_in = [sem(f"st_in{k}") for k in range(2)]
        eg_in = [sem(f"eg_in{k}") for k in range(2)]
        es_mv = [sem(f"es_mv{k}") for k in range(2)]
        d_iod = sem("d_iod"); d_oh = sem("d_oh"); d_tr = sem("d_tr"); d_cp = sem("d_cp"); d_mm = sem("d_mm")
        d_red = sem("d_red"); d_add = sem("d_add"); d_zero = sem("d_zero")
        t_tr = sem("t_tr"); t_cp = sem("t_cp"); t_x = sem("t_x"); t_v = sem("t_v"); t_pe = sem("t_pe")
        t_bt = sem("t_bt"); t_z = sem("t_z"); t_e = sem("t_e"); t_ex = sem("t_ex"); t_co = sem("t_co")
        g_in = [sem(f"g_in{k}") for k in range(RING)]
        in0 = sem("in0"); idx0 = sem("idx0"); msg0 = sem("msg0"); iod0 = sem("iod0")
        hot_f0 = sem("hot_f0"); hot_a0 = sem("hot_a0"); hot_b0 = sem("hot_b0")
        done_f0 = sem("done_f0"); done_a0 = sem("done_a0"); done_b0 = sem("done_b0")
        xl = [sem(f"xl{k}") for k in range(2)]
        x1_out = [sem(f"x1_out{k}") for k in range(2)]
        h1_out = [sem(f"h1_out{k}") for k in range(2)]
        f_r9 = sem("f_r9"); f_rr = sem("f_rr"); f_w = sem("f_w"); f_x1 = sem("f_x1"); f_st = sem("f_st")
        f_mv = sem("f_mv"); f_sd = sem("f_sd"); f_rs = sem("f_rs"); f_nm = sem("f_nm"); f_h1 = sem("f_h1")
        in1 = sem("in1"); idx1 = sem("idx1"); hi1 = sem("hi1"); lo1 = sem("lo1"); iod1 = sem("iod1")
        hot_f1 = sem("hot_f1"); hot_a1 = sem("hot_a1"); hot_b1 = sem("hot_b1")
        done_f1 = sem("done_f1"); done_a1 = sem("done_a1"); done_b1 = sem("done_b1")
        hl = [sem(f"hl{k}") for k in range(2)]
        x1l = [sem(f"x1l{k}") for k in range(2)]
        y_out = [sem(f"y_out{k}") for k in range(2)]
        m_mn = sem("m_mn"); m_htr = sem("m_htr"); m_mtr = sem("m_mtr"); m_hT = sem("m_hT"); m_mT = sem("m_mT")
        m_self = sem("m_self"); m_y = sem("m_y"); n_y = sem("n_y"); n_st = sem("n_st"); n_mv = sem("n_mv")
        n_sd = sem("n_sd"); n_rs = sem("n_rs"); n_nm = sem("n_nm"); n_yn = sem("n_yn"); n_g = sem("n_g")
        n_b = sem("n_b"); n_o = sem("n_o")

        o_in = sem("o_in"); o_v = sem("o_v"); o_pe = sem("o_pe"); o_flag = sem("o_flag")
        c_in = [sem(f"c_in{k}") for k in range(2)]
        c_v = [sem(f"c_v{k}") for k in range(2)]
        c_pe = [sem(f"c_pe{k}") for k in range(2)]
        c_pad = sem("c_pad")
        c_src = sem("c_src"); c_dist = sem("c_dist"); c_start = sem("c_start"); c_sum = sem("c_sum")
        c_o = [sem(f"c_o{k}") for k in range(3)]

        def part_of_coef(first, n):
            return coef[:, first:first + n]

        ones_m, lower, upper, lo_hot, lo_hotT, diag = (part_of_coef(q * P, P) for q in range(6))
        above = part_of_coef(6 * P, BUCKETS + 1)
        hi_hot = part_of_coef(7 * P, BUCKETS)
        table = part_of_coef(8 * P, BUCKETS)
        totals = part_of_coef(9 * P, BUCKETS)
        sums = part_of_coef(10 * P, BUCKETS)
        picked = part_of_coef(11 * P, BUCKETS)
        same_dst = part_of_coef(12 * P, P)
        zeros_m = part_of_coef(13 * P, P)
        dst_f, n_above, lo_f, base_f, rank_f, place_f = (part_of_coef(14 * P + q, 1) for q in range(6))
        dst_col, src_col, place_i = (part_of_coef(15 * P + q, 1).bitcast(I32) for q in range(3))
        dist_col = part_of_coef(16 * P, HEADS)

        block = ctx.enter_context(nc.Block())

        def disorder(eng):
            eng.wait_ge(o_flag, 1)
            c = eng.value_load(flag[0:1, 0:1], min_val=0, max_val=N_EDGES)
            return eng.snap(c)

        def sort_tiles(eng, body):
            body(0, P)
            with eng.Fori(1, FULL_TILES) as t:
                body(t, P)
            body(FULL_TILES, N_EDGES - FULL_TILES * P)

        def bounds(eng, d):
            c = eng.value_load(code[0:1, bass.ds(d, 1)], min_val=0, max_val=LAST_PAIR * CODE + LAST_PAIR)
            lo = nc.s_assert_within(c // CODE, 0, LAST_PAIR, skip_runtime_bounds_check_because="a count of pairs")
            hi = nc.s_assert_within(c % CODE, 0, LAST_PAIR, skip_runtime_bounds_check_because="a count of pairs")
            return eng.snap(lo), eng.snap(hi)

        def rest_of(eng, lo, hi, body):
            with eng.If(lo < hi):
                with eng.Fori(lo + 1, hi + 1) as u:
                    body(u)
                eng.nop()
            eng.nop()

        def second_then_rest(eng, lo, hi, second, between, after, body):
            second_pair = nc.s_assert_within(lo + 1, 1, LAST_PAIR, skip_runtime_bounds_check_because="lo < hi")
            with eng.If(lo < hi):
                second(second_pair)
                eng.nop()
            between()
            with eng.If(lo < hi):
                after(second_pair)
                with eng.If(lo + 1 < hi):
                    with eng.Fori(lo + 2, hi + 1) as u:
                        body(u)
                    eng.nop()
                eng.nop()
            eng.nop()

        def node_tiles(eng, body, peeled=2):
            for d in range(peeled):
                body(d, d % 2)
            with eng.Fori(peeled // 2, NT // 2 - 1) as j:
                body(2 * j, 0)
                body(2 * j + 1, 1)
            for d in range(NT - 3, NT):
                body(d, d % 2)

        def tiles_by_two(eng, body):
            body(0, 0, 0)
            body(1, 1, 0)
            with eng.Fori(1, NT // 2) as j:
                body(2 * j, 0, j)
                body(2 * j + 1, 1, j)
            body(NT - 1, 0, NT // 2)

        def from_tile(d, first):
            return not isinstance(d, int) or d >= first

        def in_tiles(d):
            return not isinstance(d, int) or 0 <= d < NT

        def tile_done(eng, d, lo, done_f, done_b):
            eng.wait_ge(done_f, d)
            eng.wait_ge(done_b, lo + WORK)

        def slot_free(eng, firsts, u, done_f, done_b):
            wait(eng, done_f, firsts)
            wait(eng, done_b, u)

        @block.sync
        def _(sp):
            def edge_rows(part, of, width, signal, skip=0):
                n, rest = FULL_ROWS * ROW_EDGES * width, REST * width - skip
                sp.dma_start(part[0:FULL_ROWS, :],
                             of[skip:n + skip].rearrange("(r e) -> r e", r=FULL_ROWS)).then_inc(signal, 16)
                sp.dma_start(part[FULL_ROWS:FULL_ROWS + 1, 0:rest],
                             of[n + skip:n + skip + rest].rearrange("(r e) -> r e", r=1)).then_inc(signal, 16)

            sp.wait_ge(padded, 5)
            edge_rows(dst_c, dst, 1, o_in)
            edge_rows(dst_next, dst, 1, o_in, skip=1)
            sp.dma_start(xt[0][:, :], x[0:P, :]).then_inc(x_in[0], 16)
            sp.dma_start(w0[:, :].rearrange("p (k n) -> p k n", k=KC),
                         w0t.rearrange("(k p) n -> p k n", p=P)).then_inc(s_w, 16)
            sp.dma_start(xt[1][:, :], x[P:2 * P, :]).then_inc(x_in[1], 16)

            def edge_loads(dst, src, dist):
                edge_rows(src_c, src, 1, s_ec)
                edge_rows(dist_c, dist.rearrange("e h -> (e h)"), HEADS, s_dist)
                for row, of in ((row_b0, b0), (row_as, att_src), (row_ad, att_dst)):
                    load_row(row, of, s_row)
                for c in range(CHUNKS):
                    n = min(CHUNK, N_EDGES - c * CHUNK)
                    sp.dma_start(dst_s[c * HEADS:(c + 1) * HEADS, 0:n],
                                 dst[c * CHUNK:c * CHUNK + n].rearrange("(a n) -> a n", a=1)
                                 .to_broadcast([HEADS, n])).then_inc(s_ds, 16)

            def load_row(row, of, signal):
                sp.dma_start(row[:, :], of.rearrange("(a n) -> a n", a=1).to_broadcast([P, DIM])).then_inc(signal, 16)

            def column(of, t, n):
                return of[bass.ds(t * P, n)].rearrange("(p a) -> p a", a=1)

            def feed_count(t, n):
                sp.wait_ge(c_v[0], COUNT_STEPS * t + 1)
                sp.dma_start(dst_col[0:n, :], column(dst, t, n)).then_inc(c_in[0], 16)

            def feed_place(t, n):
                for q in range(3):
                    wait(sp, c_o[q], 16 * t)
                sp.wait_ge(c_v[1], PLACE_STEPS * t + 1)
                sp.dma_start(dst_col[0:n, :], column(dst, t, n)).then_inc(c_in[1], 16)
                sp.dma_start(src_col[0:n, :], column(src, t, n)).then_inc(c_src, 16)
                sp.dma_start(dist_col[0:n, :], dist[bass.ds(t * P, n), :]).then_inc(c_dist, 16)

            fallen = disorder(sp)
            with sp.If(fallen > 0):
                sp.wait_ge(c_pad, 1)
                sort_tiles(sp, feed_count)
                sp.wait_ge(c_start, 1)
                sort_tiles(sp, feed_place)
                for q in range(3):
                    sp.wait_ge(c_o[q], 16 * (FULL_TILES + 1))
                dst_sorted = dst_tab.rearrange("e a -> (e a)")
                edge_rows(dst_c, dst_sorted, 1, s_ec)
                edge_loads(dst_sorted, src_tab.rearrange("e a -> (e a)"), dist_tab)
            with sp.If(fallen < 1):
                sp.sem_inc(s_ec, 32)
                edge_loads(dst, src, dist)
            sp.nop()

            def store(i, k):
                sp.wait_ge(a_h, i + 1)
                sp.dma_start(h_tab[bass.ds(i * P, P), :], ho[k][:, :]).then_inc(h_out[k], 16)
                sp.wait_ge(a_es, i + 1)
                sp.dma_start(es_tab[bass.ds(i * P, P), :], es_st[k][:, :]).then_inc(es_out[k], 16)

            def load(i, k, n=P):
                sp.wait_ge(a_h0, i - 1)
                sp.dma_start(xt[k][0:n, :], x[bass.ds(i * P, n), :]).then_inc(x_in[k], 16)

            with sp.Fori(0, NT // 2 - 1) as j:
                load(2 * j + 2, 0)
                store(2 * j, 0)
                load(2 * j + 3, 1)
                store(2 * j + 1, 1)
            load(NT - 1, 0, LAST_ROWS)
            store(NT - 3, 0)
            store(NT - 2, 1)
            store(NT - 1, 0)

            sp.wait_ge(e_sg, 1)

            def hand(j, k):
                sp.dma_start(st_i[k][:, :], src_g[:, bass.ds(j * CHUNKS, CHUNKS)]).then_inc(st_in[k], 16)

            def move(j, k, n):
                sp.wait_ge(eg_in[k], 16 * CHUNKS * (n + 1))
                sp.dma_start(es_all[:, bass.ds(j * P, P)], es_r[k][:, :]).then_inc(es_mv[k], 16)

            hand(0, 0)
            hand(1, 1)
            sp.wait_ge(e_ev, 20)
            with sp.Fori(0, TPC // 2 - 1) as j:
                move(2 * j, 0, j)
                hand(2 * j + 2, 0)
                move(2 * j + 1, 1, j)
                hand(2 * j + 3, 1)
            move(TPC - 3, 0, TPC // 2 - 1)
            hand(TPC - 1, 0)
            move(TPC - 2, 1, TPC // 2 - 1)
            move(TPC - 1, 0, TPC // 2)

            with sp.Fori(0, PAIRS // RING) as i:
                for k in range(RING):
                    sp.wait_ge(g_in[k], 32 * (i + 1))
                    sp.sem_inc(in0, 1)
            sp.dma_start(ws.rearrange("p (k n) -> p k n", k=KC),
                         wst.rearrange("(k p) n -> p k n", p=P)).then_inc(s_w1, 16)
            sp.dma_start(wn.rearrange("p (k n) -> p k n", k=KC),
                         wnt.rearrange("(k p) n -> p k n", p=P)).then_inc(s_w1, 16)
            for row, of in ((row_bias, bias), (row_gamma, gamma), (row_beta, beta)):
                load_row(row, of, s_w1)
            with sp.Fori(0, PAIRS // RING) as i:
                for k in range(RING):
                    sp.wait_ge(g_in[k], 32 * (i + 1) + 32 * (PAIRS // RING))
                    sp.sem_inc(in1, 1)

        @block.gpsimd
        def _(pool):
            pool.memset(dst_c, PAD_DST).then_inc(padded, 1)
            pool.memset(src_c, 0).then_inc(padded, 1)
            pool.memset(dst_next, PAD_DST).then_inc(padded, 1)
            pool.memset(ident[:, :], 0.0).then_inc(k_id, 1)
            pool.memset(pick_last[:, :], 0.0).then_inc(k_id, 1)
            pool.iota(iota_i[:, :], pattern=[[1, P]], base=0, channel_multiplier=0).then_inc(k_cst, 1)
            pool.iota(first_i[:, :], pattern=[[P, NT + 1]], base=0, channel_multiplier=0).then_inc(k_cst, 1)
            pool.iota(thr_i[:, :], pattern=[[0, 1]], base=0, channel_multiplier=P).then_inc(k_cst, 1)
            pool.wait_ge(k_id, 2)
            pool.affine_select(out=ident[:, :], in_=ident[:, :], compare_op=ALU.not_equal, fill=1.0, base=0,
                               pattern=[[-1, P]], channel_multiplier=1).then_inc(k_id, 1)
            pool.affine_select(out=pick_last[:, :], in_=pick_last[:, :], compare_op=ALU.not_equal, fill=1.0,
                               base=1 - P, pattern=[[0, 64]], channel_multiplier=1).then_inc(k_id, 1)

            def place(t, n):
                pool.wait_ge(c_v[1], PLACE_STEPS * (t + 1))
                pool.wait_ge(c_src, 16 * (t + 1))
                pool.wait_ge(c_dist, 16 * (t + 1))
                pool.sem_inc(p_go, 1)
                for q, (tab, col) in enumerate(((dst_tab, dst_col), (src_tab, src_col), (dist_tab, dist_col))):
                    pool.indirect_dma_start(tab, bass.IndirectOffsetOnAxis(ap=place_i, axis=0), col,
                                            None).then_inc(c_o[q], 16)

            with pool.If(disorder(pool) > 0):
                sort_tiles(pool, place)
            pool.nop()

            pool.wait_ge(s_row, 48)

            def products(i, k, n):
                pool.wait_ge(a_h, i + 1)
                wait(pool, a_es, i - 1)
                pool.tensor_tensor(ms[k][:, :], ho[k][:, :], row_as[:, :], ALU.mult).then_inc(a_ms, 1)
                wait(pool, a_ed, i - 1)
                pool.tensor_tensor(md[k][:, :], ho[k][:, :], row_ad[:, :], ALU.mult).then_inc(a_md, 1)

            tiles_by_two(pool, products)

            for k in range(2):
                pool.wait_ge(es_out[k], 16 * ((NT + 1 - k) // 2))

            def group(k, n):
                pool.wait_ge(st_in[k], 16 * (n + 1))
                wait(pool, es_mv[k], 16 * n)
                pool.sem_inc(p_go, 1)
                for c in range(CHUNKS):
                    pool.indirect_dma_start(
                        es_r[k][:, c * HEADS:(c + 1) * HEADS], None, es_tab,
                        bass.IndirectOffsetOnAxis(ap=st_i[k][:, c:c + 1], axis=0)).then_inc(eg_in[k], 16)

            group(0, 0)
            group(1, 0)
            with pool.Fori(1, TPC // 2) as j:
                group(0, j)
                group(1, j)
            group(0, TPC // 2)

            def gathers(table, landed, idx_ready, used):
                def pair(i, m):
                    u, k = RING * i + m, m % RING
                    pool.wait_ge(idx_ready, u + 1)
                    wait(pool, used, u + 1 - RING)
                    pool.sem_inc(p_go, 1)
                    for t in range(2):
                        pool.indirect_dma_start(
                            g_ring[:, k * GW + t * DIM:k * GW + (t + 1) * DIM], None, table,
                            bass.IndirectOffsetOnAxis(ap=idx_ring[:, 2 * m + t:2 * m + t + 1], axis=0)
                        ).then_inc(landed[k], 16)

                for m in range(RING):
                    pair(0, m)
                with pool.Fori(1, PAIRS // RING) as i:
                    for m in range(RING):
                        pair(i, m)

            for k in range(2):
                pool.wait_ge(h_out[k], 16 * ((NT + 1 - k) // 2))
            gathers(h_tab, g_in, idx0, msg0)
            for k in range(2):
                pool.wait_ge(h1_out[k], 16 * ((NT + 1 - k) // 2))
            gathers(h1_tab, g_in, idx1, lo1)

        @block.scalar
        def _(act):
            def normalise(i, k, n):
                act.wait_ge(a_mv, i + 1)
                act.activation(sd[k][:, :], mv[k][:, 1:2], ACT.Sqrt, bias=eps_c[:, :]).then_inc(a_sd, 1)
                act.wait_ge(a_nm, i + 1)
                wait(act, a_tr, i - 1)
                act.activation(hn[k][:, :], xt[k][:, :], ACT.Relu, bias=nm[k][:, :],
                               scale=rs[k][:, :]).then_inc(a_h0, 1)
                act.wait_ge(a_tr, i + 1)
                wait(act, a_mm, i - 1)
                act.copy(hT[k][:, :], ps[k][:, :]).then_inc(a_hT, 1)

            act.wait_ge(k_cf, 1)
            tiles_by_two(act, normalise)

            def step_d(d, u):
                s = d + u
                act.wait_ge(d_tr, s + 2)
                act.wait_ge(d_mm, s + 1)
                act.copy(ohT_b[:, :], ps[2][:, 0:P].bitcast(BF16)).then_inc(d_cp, 1)

            def tile_d(d, k):
                lo, hi = bounds(act, d)
                step_d(d, lo)
                rest_of(act, lo, hi, lambda u: step_d(d, u))

            act.wait_ge(b_code, 1)
            node_tiles(act, tile_d)

            act.wait_ge(e_same, 3)
            for g in range(0, TPC, 4):
                m = min(4, TPC - g)
                act.wait_ge(t_tr, g // 4 + 1)
                act.copy(scan[:, g * P:(g + m) * P], ps[g // 4 % 2][:, 0:m * P]).then_inc(t_cp, 1)
            act.wait_ge(t_e, 1)
            act.activation(ex3[:, :, 0:HEADS], ex3[:, :, 0:HEADS], ACT.Exp).then_inc(t_ex, 1)

            def stage(u, ready):
                act.copy(idx_ring[:, bass.ds((u % RING) * 2, 2)], src_e[:, bass.ds(2 * u, 2)]).then_inc(ready, 1)

            for u in range(RING):
                stage(u, idx0)
            for k in range(2):
                act.dma_start(xt[k][:, :], x[k * P:(k + 1) * P, :]).then_inc(xl[k], 16)

            def new_pair0(u):
                act.wait_ge(in0, u + 1)
                stage(u + RING, idx0)

            def normalise0(d, k):
                act.wait_ge(f_rr, d + 1)
                wait(act, x1_out[k], 8 * (d - k))
                for h in range(HEADS):
                    cols = slice(h * HEAD_DIM, (h + 1) * HEAD_DIM)
                    last = act.activation(hn[k][:, cols], ps[k][:, cols], ACT.Copy, scale=rr[k][:, h:h + 1])
                last.then_inc(f_w, 1)

            def flush0(d, k):
                act.wait_ge(f_mv, d + 1)
                act.activation(sd[k][:, :], mv[k][:, 1:2], ACT.Sqrt, bias=eps_c[:, :]).then_inc(f_sd, 1)
                act.wait_ge(f_nm, d + 1)
                wait(act, h1_out[k], 8 * (d - k))
                act.activation(ho[k][:, :], hn[k][:, :], ACT.Relu, bias=nm[k][:, :],
                               scale=rs[k][:, :]).then_inc(f_h1, 1)
                act.dma_start(x1_tab[bass.ds(d * P, P), :], hn[k][:, :]).then_inc(x1_out[k], 16)
                act.wait_ge(f_h1, d + 1)
                act.dma_start(h1_tab[bass.ds(d * P, P), :], ho[k][:, :]).then_inc(h1_out[k], 16)

            def tile0(d, k):
                lo, hi = bounds(act, d)
                if from_tile(d, 2):
                    flush0(d - 2, k)
                    n = LAST_ROWS if isinstance(d, int) and d == NT - 1 else P
                    act.dma_start(xt[k][0:n, :], x[bass.ds(d * P, n), :]).then_inc(xl[k], 16)
                if from_tile(d, 1):
                    normalise0(d - 1, 1 - k)
                rest_of(act, lo, hi, lambda u: new_pair0(u + 1))

            new_pair0(0)
            new_pair0(1)
            node_tiles(act, tile0, 4)
            flush0(NT - 2, 1)
            normalise0(NT - 1, 0)
            flush0(NT - 1, 0)

            act.wait_ge(in0, PAIRS)
            for u in range(RING):
                stage(u, idx1)
            for k in range(2):
                act.wait_ge(x1_out[k], 16 * ((NT + 1 - k) // 2))
            for k in range(2):
                act.wait_ge(h1_out[k], 16 * ((NT + 1 - k) // 2))

            def load_tile(d, k):
                act.dma_start(ho[k][:, :], h1_tab[bass.ds(d * P, P), :]).then_inc(hl[k], 16)

            def load_x1(d, k):
                act.dma_start(xt[k][:, :], x1_tab[bass.ds(d * P, P), :]).then_inc(x1l[k], 16)

            def split(u):
                act.wait_ge(in1, u + 1)
                act.activation(ring(hi_r, u, WORK, GW), ring(g_ring, u, RING, GW), ACT.Copy).then_inc(hi1, 1)
                stage(u + RING, idx1)

            def new_pair1(d, u):
                slot_free(act, d + 1, u, done_f1, done_b1)
                split(u)

            def transposed1(d, k):
                act.wait_ge(m_htr, d + 1)
                wait(act, m_self, d - 1)
                act.copy(hT[k][:, :], ps[4][:, :]).then_inc(m_hT, 1)
                act.wait_ge(m_mtr, d + 1)
                wait(act, m_y, d - 1)
                act.copy(mT[k][:, :], ps[5][:, :]).then_inc(m_mT, 1)

            def mean1(d, k, lo):
                tile_done(act, d + 1, lo, done_f1, done_b1)
                wait(act, m_mtr, d - 1)
                act.activation(hn[k][:, :], ps[k][:, :], ACT.Copy, scale=rdeg[:, bass.ds(d, 1)]).then_inc(m_mn, 1)

            def sqrt1(d, k):
                act.wait_ge(n_mv, d + 1)
                act.activation(sd[k][:, :], mv[k][:, 1:2], ACT.Sqrt, bias=eps_c[:, :]).then_inc(n_sd, 1)

            def normalise1(d, k):
                act.wait_ge(n_nm, d + 1)
                act.activation(yo[k][:, :], yo[k][:, :], ACT.Identity, bias=nm[k][:, :],
                               scale=rs[k][:, :]).then_inc(n_yn, 1)

            def store1(d, k, n=P):
                act.wait_ge(n_o, d + 1)
                act.dma_start(out[bass.ds(d * P, n), :], yo[k][0:n, :]).then_inc(y_out[k], 16)

            def load_h1(d, k):
                act.dma_start(ho[k][:, :], h1_tab[bass.ds(d * P, P), :]).then_inc(hl[k], 16)

            def load_x1(d, k):
                act.dma_start(xt[k][:, :], x1_tab[bass.ds(d * P, P), :]).then_inc(x1l[k], 16)

            def between1(d, k, lo):
                if in_tiles(d - 2):
                    transposed1(d - 2, k)
                    if in_tiles(d):
                        load_h1(d, k)
                if in_tiles(d - 5):
                    store1(d - 5, 1 - k)
                if in_tiles(d - 3):
                    load_x1(d - 3, 1 - k)
                    sqrt1(d - 3, 1 - k)
                if in_tiles(d - 1):
                    mean1(d - 1, 1 - k, lo)
                if in_tiles(d - 3):
                    normalise1(d - 3, 1 - k)

            def tile1(d, k):
                lo, hi = bounds(act, d)
                between1(d, k, lo)
                rest_of(act, lo, hi, lambda u: new_pair1(d, u + 1))

            load_h1(0, 0)
            load_h1(1, 1)
            for u in range(2):
                split(u)
            node_tiles(act, tile1, 6)
            for d in range(NT, NT + 4):
                between1(d, d % 2, LAST_PAIR)
            store1(NT - 1, 0, LAST_ROWS)
            for k in range(2):
                act.wait_ge(y_out[k], 16 * ((NT + 1 - k) // 2))
            act.wait_ge(s_w1, 80)

        @block.tensor
        def _(pe):
            mm = nc.tensor.matmul

            pe.wait_ge(k_cf, 1)
            pe.wait_ge(o_v, 2)
            mm(ps[4][0:1, 0:1], falls[0:ROWS, :], ones_c[0:ROWS, :], start=True, stop=True).then_inc(o_pe, 1)

            def count(t, n):
                pe.wait_ge(c_v[0], COUNT_STEPS * t + 7)
                mm(ps[0][:, 0:BUCKETS], lo_hot, hi_hot, start=True, stop=True).then_inc(c_pe[0], 1)

            def look_up(t, n):
                pe.wait_ge(c_v[1], PLACE_STEPS * t + 8)
                mm(ps[0][:, 0:BUCKETS], lo_hot, hi_hot, start=True, stop=True)
                mm(ps[3][:, 0:P], ones_m, diag, start=True, stop=True)
                pe.transpose(ps[1][:, 0:P], lo_hot, ident[:, :]).then_inc(c_pe[1], 1)
                pe.wait_ge(c_v[1], PLACE_STEPS * t + 9)
                mm(ps[2][:, 0:BUCKETS], lo_hotT, table, start=True, stop=True).then_inc(c_pe[1], 1)

            with pe.If(disorder(pe) > 0):
                sort_tiles(pe, count)
                pe.wait_ge(c_v[0], COUNT_STEPS * (FULL_TILES + 1))
                mm(ps[1][:, 0:BUCKETS], upper, table, start=True, stop=True)
                mm(ps[2][:, 0:BUCKETS], ones_m, table, start=True, stop=True).then_inc(c_sum, 1)
                sort_tiles(pe, look_up)
            pe.nop()

            pe.wait_ge(e_f, 2)
            n = 0
            for part in (dst_cf, src_cf):
                for q in range(2):
                    wait(pe, e_ev, n - 1)
                    for b in range(4):
                        t = part[:, (4 * q + b) * P:(4 * q + b + 1) * P]
                        last = pe.transpose(ps[4 + n % 2][:, b * ROWS:(b + 1) * ROWS], t, ident[0:ROWS, 0:ROWS])
                    last.then_inc(e_tr, 1)
                    n += 1

            pe.wait_ge(s_w, 16)

            def project(i, k, n):
                pe.wait_ge(a_h0, i + 1)
                wait(pe, a_hT, i - 1)
                for c in range(KC):
                    last = pe.transpose(ps[k][:, c * P:(c + 1) * P], hn[k][:, c * P:(c + 1) * P], ident[:, :])
                last.then_inc(a_tr, 1)
                pe.wait_ge(a_hT, i + 1)
                wait(pe, a_hb, i - 1)
                for c in range(KC):
                    last = mm(ps[2 + k][:, :], hT[k][:, c * P:(c + 1) * P], w0[:, c * DIM:(c + 1) * DIM],
                              start=(c == 0), stop=(c == KC - 1))
                last.then_inc(a_mm, 1)

            tiles_by_two(pe, project)

            pe.wait_ge(s_dist, 32)
            for b in range(8):
                for q in range(2):
                    wait(pe, e_ev, n - 1)
                    for h in range(4):
                        t = dist_c[:, b * P * HEADS + 4 * q + h:(b + 1) * P * HEADS:HEADS]
                        last = pe.transpose(ps[4 + n % 2][:, h * ROWS:(h + 1) * ROWS], t, ident[0:ROWS, 0:ROWS])
                    last.then_inc(e_tr, 1)
                    n += 1

            pe.wait_ge(e_ev, 4)
            mm(ps[6][0:64, 0:PAIRS], pick_last[:, :], dst_e[:, 1::2], start=True, stop=True).then_inc(b_mm, 1)
            pe.wait_ge(b_cnt, 1)
            pe.transpose(ps[7][0:1, 0:64], cnt[:, :], ident[0:64, 0:64]).then_inc(b_tr, 1)

            pe.sem_inc(d_tr, 1)
            pe.sem_inc(d_mm, 1)
            pe.wait_ge(d_split, 5)

            def step_d(d, u):
                s = d + u
                pe.wait_ge(d_oh, s + 1)
                pe.wait_ge(d_cp, s + 1)
                for i in range(2):
                    last = pe.transpose(ps[2][:, i * P // 2:(i + 1) * P // 2].bitcast(BF16),
                                        oh_b[:, i * P:(i + 1) * P], ident_b[:, :])
                last.then_inc(d_tr, 1)
                pe.wait_ge(d_cp, s + 2)
                pe.wait_ge(d_red, s + 1)
                for i in range(2):
                    last = mm(ps[3][:, i * 3 * HEADS:(i + 1) * 3 * HEADS], ohT_b[:, i * P:(i + 1) * P],
                              ed3[:, bass.ds(d * 3 * HEADS, 3 * HEADS)], start=True, stop=True)
                last.then_inc(d_mm, 1)

            def tile_d(d, k):
                lo, hi = bounds(pe, d)
                step_d(d, lo)
                rest_of(pe, lo, hi, lambda u: step_d(d, u))

            pe.wait_ge(b_code, 1)
            pe.sem_inc(d_cp, 1)
            node_tiles(pe, tile_d)

            for k in range(2):
                pe.wait_ge(es_mv[k], 16 * ((TPC + 1 - k) // 2))
            for g in range(0, TPC, 4):
                wait(pe, t_cp, g // 4 - 1)
                for j in range(g, min(g + 4, TPC)):
                    last = pe.transpose(ps[g // 4 % 2][:, (j - g) * P:(j - g + 1) * P], es_all[:, j * P:(j + 1) * P],
                                        ident[:, :])
                last.then_inc(t_tr, 1)
            pe.wait_ge(t_v, 6)
            for q in range(4):
                last = pe.transpose(ps[2][0:1, q * P:(q + 1) * P], ends[:, q:q + 1], ident[:, :])
            last.then_inc(t_pe, 1)
            pe.wait_ge(t_v, 20)
            for q in range(2):
                last = pe.transpose(ps[3][:, q:q + 1], inits[q][0:1, :], ident[0:1, 0:1])
            last.then_inc(t_pe, 1)
            pe.wait_ge(t_v, 23)
            for g in range(0, TPC, 4):
                wait(pe, t_z, g // 4 - 1)
                for j in range(g, min(g + 4, TPC)):
                    last = pe.transpose(ps[g // 4 % 2][:, (j - g) * P:(j - g + 1) * P], scan[:, j * P:(j + 1) * P],
                                        ident[:, :])
                last.then_inc(t_bt, 1)

            pe.sem_inc(done_a0, 1)
            pe.sem_inc(done_b0, WORK)
            pe.wait_ge(t_co, 2)

            def add0(k, one_hot, u, t, start):
                mm(ps[k][:, :], one_hot[:, :], msg[:, bass.ds((u % WORK) * GW + t * DIM, DIM)],
                   start=start, stop=True, skip_group_check=True)
                return mm(ps[2 + k][:, 0:EW], one_hot[:, :], ex_buf[:, bass.ds((2 * u + t) * EW, EW)],
                          start=start, stop=True, skip_group_check=True)

            def first0(d, u, k):
                pe.wait_ge(msg0, u + 1)
                pe.wait_ge(hot_f0, d + 1)
                add0(k, oh_first[0], u, 0, True)
                add0(k, oh_first[1], u, 1, False).then_inc(done_f0, 1)

            def step0(u, k):
                pe.wait_ge(msg0, u + 1)
                pe.wait_ge(hot_a0, u)
                add0(k, oh_rest[0], u, 0, False).then_inc(done_a0, 1)
                pe.wait_ge(hot_b0, u)
                add0(k, oh_rest[1], u, 1, False).then_inc(done_b0, 1)

            def tile0(d, k):
                lo, hi = bounds(pe, d)
                wait(pe, f_w, d - 1)
                first0(d, lo, k)
                rest_of(pe, lo, hi, lambda u: step0(u, k))

            node_tiles(pe, tile0, 4)

            pe.sem_inc(done_a1, 1)
            pe.sem_inc(done_b1, WORK)
            pe.wait_ge(s_w1, 80)

            def add1(k, one_hot, u, t, start):
                for part in (hi_r, lo_r):
                    last = mm(ps[k][:, :], one_hot[:, :], part[:, bass.ds((u % WORK) * GW + t * DIM, DIM)],
                              start=start and part is hi_r, stop=True, skip_group_check=True)
                return last

            def first1(d, u, k):
                pe.wait_ge(lo1, u + 1)
                pe.wait_ge(hot_f1, d + 1)
                add1(k, ohr_first[0], u, 0, True)
                add1(k, ohr_first[1], u, 1, False).then_inc(done_f1, 1)

            def step1(u, k):
                pe.wait_ge(lo1, u + 1)
                pe.wait_ge(hot_a1, u)
                add1(k, ohr_rest[0], u, 0, False).then_inc(done_a1, 1)
                pe.wait_ge(hot_b1, u)
                add1(k, ohr_rest[1], u, 1, False).then_inc(done_b1, 1)

            def transpose1(d, k):
                pe.wait_ge(hl[k], 8 * (d - k) + 16)
                wait(pe, m_hT, d)
                for c in range(KC):
                    last = pe.transpose(ps[4][:, c * P:(c + 1) * P], ho[k][:, c * P:(c + 1) * P], ident[:, :])
                last.then_inc(m_htr, 1)
                pe.wait_ge(m_mn, d + 1)
                wait(pe, m_mT, d)
                for c in range(KC):
                    last = pe.transpose(ps[5][:, c * P:(c + 1) * P], hn[k][:, c * P:(c + 1) * P], ident[:, :])
                last.then_inc(m_mtr, 1)

            def update1(d, k):
                pe.wait_ge(m_hT, d + 1)
                wait(pe, n_y, d - 1)
                for c in range(KC):
                    last = mm(ps[6 + k][:, :], hT[k][:, c * P:(c + 1) * P], ws[:, c * DIM:(c + 1) * DIM],
                              start=(c == 0), stop=False)
                last.then_inc(m_self, 1)
                pe.wait_ge(m_mT, d + 1)
                for c in range(KC):
                    last = mm(ps[6 + k][:, :], mT[k][:, c * P:(c + 1) * P], wn[:, c * DIM:(c + 1) * DIM],
                              start=False, stop=(c == KC - 1))
                last.then_inc(m_y, 1)

            def between1(d, k):
                if in_tiles(d - 2):
                    update1(d - 2, k)
                if in_tiles(d - 1):
                    transpose1(d - 1, 1 - k)

            def tile1(d, k):
                lo, hi = bounds(pe, d)
                wait(pe, m_mn, d - 1)
                first1(d, lo, k)
                between1(d, k)
                rest_of(pe, lo, hi, lambda u: step1(u, k))

            node_tiles(pe, tile1, 4)
            between1(NT, 1)
            update1(NT - 1, 0)

        @block.vector
        def _(dve):
            tt, ts, stt = nc.vector.tensor_tensor, nc.vector.tensor_scalar, nc.vector.scalar_tensor_tensor
            copy = nc.vector.tensor_copy

            dve.memset(dist_c, 0.0).then_inc(padded, 1)
            dve.memset(dst_s[96:P, :], PAD_DST).then_inc(padded, 1)
            dve.memset(eps_c[:, :], EPS)
            dve.memset(src_e[:, TILES:], 0)
            dve.wait_ge(k_cst, 3)
            copy(iota_f[:, :], iota_i[:, :])
            copy(first_f[:, :], first_i[:, :])
            copy(thr_f[:, :], thr_i[:, :])
            dve.wait_ge(k_id, 4)
            copy(ident_b[:, :], ident[:, :]).then_inc(k_cf, 1)

            dve.memset(ones_c[:, :], 1.0)
            dve.wait_ge(o_in, 64)
            tt(src_cf, dst_c, dst_next, ALU.is_gt).then_inc(o_v, 1)
            dve.wait_ge(o_v, 1)
            dve.tensor_reduce(falls[0:ROWS, :], src_cf, AX.X, ALU.add).then_inc(o_v, 1)
            dve.wait_ge(o_pe, 1)
            copy(flag[:, :], ps[4][0:1, 0:1]).then_inc(o_flag, 1)

            def one_hots(q, t, n, per_tile):
                done = [0]

                def step(ins):
                    done[0] += 1
                    ins.then_inc(c_v[q], 1)
                    dve.wait_ge(c_v[q], per_tile * t + done[0])

                if n < P:
                    if q:
                        dve.wait_ge(c_o[0], 16 * t)
                    step(dve.memset(dst_col, NT * P))
                else:
                    step(dve.memset(above[:, BUCKETS:], 0.0))
                dve.wait_ge(c_in[q], 16 * (t + 1))
                step(copy(dst_f, dst_col))
                step(ts(above[:, 0:BUCKETS], first_f[:, :], dst_f, None, ALU.is_le, ALU.add, accum_out=n_above))
                step(tt(hi_hot, above[:, 0:BUCKETS], above[:, 1:], ALU.subtract))
                step(ts(n_above, n_above, -float(P), float(P), ALU.mult, ALU.add))
                step(tt(lo_f, n_above, dst_f, ALU.add))
                step(ts(lo_hot, iota_f[:, :], lo_f, None, ALU.is_equal))
                return step

            def count(t, n):
                step = one_hots(0, t, n, COUNT_STEPS)
                dve.wait_ge(c_pe[0], t + 1)
                step(tt(table, table, ps[0][:, 0:BUCKETS], ALU.add))

            def look_up(t, n):
                step = one_hots(1, t, n, PLACE_STEPS)
                step(ts(diag, ident[:, :], dst_f, None, ALU.mult))
                dve.wait_ge(c_pe[1], 2 * t + 1)
                step(copy(lo_hotT, ps[1][:, 0:P]))
                dve.wait_ge(c_pe[1], 2 * t + 2)
                step(tt(picked, hi_hot, ps[2][:, 0:BUCKETS], ALU.mult))
                step(dve.tensor_reduce(base_f, picked, AX.X, ALU.add))
                step(ts(same_dst, ps[3][:, 0:P], dst_f, None, ALU.is_equal))
                step(tt(same_dst, same_dst, lower, ALU.mult))
                step(dve.tensor_reduce(rank_f, same_dst, AX.X, ALU.add))
                step(tt(place_f, base_f, rank_f, ALU.add))
                step(tt(table, table, ps[0][:, 0:BUCKETS], ALU.add))
                step(copy(place_i, place_f))

            with dve.If(disorder(dve) > 0):
                dve.memset(coef[:, :], 0.0).then_inc(o_v, 1)
                dve.wait_ge(o_v, 3)
                dve.memset(dst_col, NT * P)
                dve.memset(src_col, 0)
                dve.memset(ones_m, 1.0).then_inc(c_pad, 1)
                ts(lower, iota_f[:, :], float(P), thr_f[:, :], ALU.mult, ALU.is_lt)
                ts(upper, iota_f[:, :], float(P), thr_f[:, :], ALU.mult, ALU.is_gt)
                sort_tiles(dve, count)
                dve.wait_ge(c_sum, 1)
                copy(totals, ps[2][:, 0:BUCKETS]).then_inc(o_v, 1)
                dve.wait_ge(o_v, 4)
                dve.tensor_tensor_scan(sums, ones_m[:, 0:BUCKETS], totals, 0.0, ALU.mult, ALU.add).then_inc(o_v, 1)
                dve.wait_ge(o_v, 5)
                tt(sums, sums, totals, ALU.subtract).then_inc(o_v, 1)
                dve.wait_ge(o_v, 6)
                tt(table, sums, ps[1][:, 0:BUCKETS], ALU.add).then_inc(c_start, 1)
                dve.wait_ge(c_start, 1)
                sort_tiles(dve, look_up)
            dve.nop()

            dve.wait_ge(s_ec, 64)
            copy(dst_cf, dst_c).then_inc(e_f, 1)
            copy(src_cf, src_c).then_inc(e_f, 1)
            n = 0
            for part in (dst_e, src_e):
                for q in range(2):
                    dve.wait_ge(e_tr, n + 1)
                    o = part[:, 0:TILES].rearrange("p (a b) -> p b a", b=8)[:, 4 * q:4 * q + 4, :]
                    copy(o, ps[4 + n % 2][:, 0:4 * ROWS].rearrange("p (b a) -> p b a", b=4)).then_inc(e_ev, 1)
                    n += 1
            dve.wait_ge(e_ev, 4)
            copy(src_g[:, :].rearrange("p (j c) -> p j c", c=CHUNKS),
                 src_e[:, 0:TILES].rearrange("p (c j) -> p j c", c=CHUNKS)).then_inc(e_sg, 1)
            dve.wait_ge(s_row, 48)

            def stats(src_t, k, s_st, s_mv, d):
                dve.bn_stats(st[k][:, :], src_t).then_inc(s_st, 1)
                dve.wait_ge(s_st, d + 1)
                dve.sem_inc(v_go, 1)
                dve.bn_aggr(mv[k][:, :], st[k][:, :]).then_inc(s_mv, 1)

            def scale_and_shift(k, s_mv, s_sd, s_rs, s_nm, d):
                dve.wait_ge(s_sd, d + 1)
                dve.reciprocal(rs[k][:, :], sd[k][:, :]).then_inc(s_rs, 1)
                dve.wait_ge(s_rs, d + 1)
                stt(nm[k][:, :], mv[k][:, 0:1], -1.0, rs[k][:, :], ALU.mult, ALU.mult).then_inc(s_nm, 1)

            def norm_stats(i, k, n):
                dve.wait_ge(x_in[k], 16 * (n + 1))
                stats(xt[k][:, :], k, a_st, a_mv, i)
                wait(dve, a_h0, i - 1)
                scale_and_shift(k, a_mv, a_sd, a_rs, a_nm, i)

            def head_terms(i, k, n):
                dve.wait_ge(a_mm, i + 1)
                wait(dve, h_out[k], 16 * n)
                wait(dve, a_md, i - 1)
                tt(ho[k][:, :], ps[2 + k][:, :], row_b0[:, :], ALU.add).then_inc(a_hb, 1)
                dve.wait_ge(a_hb, i + 1)
                stt(ho[k][:, :], ho[k][:, :], SLOPE, ho[k][:, :], ALU.mult, ALU.max).then_inc(a_h, 1)

            def head_sums(i, k, n):
                dve.wait_ge(a_ms, i + 1)
                wait(dve, es_out[k], 16 * n)
                dve.tensor_reduce(es_st[k][:, :], ms[k][:, :].rearrange("p (h e) -> p h e", h=HEADS), AX.X,
                                  ALU.add).then_inc(a_es, 1)
                dve.wait_ge(a_md, i + 1)
                dve.tensor_reduce(ed_n[:, bass.ds(i * HEADS, HEADS)],
                                  md[k][:, :].rearrange("p (h e) -> p h e", h=HEADS), AX.X, ALU.add).then_inc(a_ed, 1)

            norm_stats(0, 0, 0)
            norm_stats(1, 1, 0)
            head_terms(0, 0, 0)
            norm_stats(2, 0, 1)
            head_sums(0, 0, 0)
            head_terms(1, 1, 0)
            with dve.Fori(1, NT // 2) as j:
                norm_stats(2 * j + 1, 1, j)
                head_sums(2 * j - 1, 1, j - 1)
                head_terms(2 * j, 0, j)
                norm_stats(2 * j + 2, 0, j + 1)
                head_sums(2 * j, 0, j)
                head_terms(2 * j + 1, 1, j)
            head_sums(NT - 2, 1, NT // 2 - 1)
            head_terms(NT - 1, 0, NT // 2)
            head_sums(NT - 1, 0, NT // 2)

            for b in range(8):
                for q in range(2):
                    dve.wait_ge(e_tr, n + 1)
                    o = coef[:, :].rearrange("p (a b h) -> p b h a", b=8, h=HEADS)[:, b, 4 * q:4 * q + 4, :]
                    copy(o, ps[4 + n % 2][:, 0:4 * ROWS].rearrange("p (h a) -> p h a", h=4)).then_inc(e_ev, 1)
                    n += 1

            dve.wait_ge(b_mm, 1)
            ts(below, ps[6][0:64, 0:PAIRS], thr_f[0:64, :], None, ALU.is_lt, ALU.add,
               accum_out=cnt[:, :]).then_inc(b_cnt, 1)
            dve.wait_ge(b_tr, 1)
            copy(bnd_f[:, :], ps[7][0:1, 0:64]).then_inc(b_row, 1)
            dve.wait_ge(b_row, 1)
            stt(code_f[:, 0:63], bnd_f[:, 0:63], float(CODE), bnd_f[:, 1:64], ALU.mult, ALU.add).then_inc(b_row, 1)
            dve.wait_ge(b_row, 2)
            copy(code[:, 0:63], code_f[:, 0:63]).then_inc(b_code, 1)

            parts = ed3[:, :].rearrange("p (d q h) -> p q d h", q=3, h=HEADS)
            nodes = ed_n[:, :].rearrange("p (d h) -> p d h", h=HEADS)
            rest = ed_r[:, :].rearrange("p (d h) -> p d h", h=HEADS)
            dve.wait_ge(a_ed, NT)
            copy(parts[:, 0], nodes).then_inc(d_split, 1)
            dve.wait_ge(d_split, 1)
            tt(rest, nodes, parts[:, 0], ALU.subtract).then_inc(d_split, 1)
            dve.wait_ge(d_split, 2)
            copy(parts[:, 1], rest).then_inc(d_split, 1)
            dve.wait_ge(d_split, 3)
            tt(rest, rest, parts[:, 1], ALU.subtract).then_inc(d_split, 1)
            dve.wait_ge(d_split, 4)
            copy(parts[:, 2], rest).then_inc(d_split, 1)

            dve.wait_ge(s_ds, 16 * CHUNKS)
            tt(same[:, 1:CHUNK], dst_s[:, 1:CHUNK], dst_s[:, 0:CHUNK - 1], ALU.is_equal).then_inc(e_same, 1)
            copy(ends[:, 2:3], dst_s[:, 0:1])
            copy(ends[:, 3:4], dst_s[:, CHUNK - 1:CHUNK]).then_inc(e_same, 1)
            dve.wait_ge(e_same, 1)
            ts(same[:, 1:CHUNK], same[:, 1:CHUNK], 2 * BIG, -BIG, ALU.mult, ALU.add).then_inc(e_same, 1)
            dve.memset(same[:, 0:1], BIG)
            dve.memset(same[:, CHUNK:CHUNK + 1], BIG)
            dve.wait_ge(e_tr, 20)
            dve.memset(ed_e, 0.0).then_inc(d_zero, 1)
            dve.memset(ex3[:, :, HEADS:EW], 1.0)

            def new_iod(d, k, signal):
                ts(iod[k][:, :], iota_f[:, :], first_f[:, bass.ds(d, 1)], None, ALU.add).then_inc(signal, 1)
                dve.wait_ge(signal, d + 1)

            def hot_d(d, u, k):
                dve.wait_ge(d_tr, d + u + 1)
                ts(oh_b[:, 0:P], iod[k][:, :], dst_e[:, bass.ds(2 * u, 1)], None, ALU.is_equal)
                ts(oh_b[:, P:2 * P], iod[k][:, :], dst_e[:, bass.ds(2 * u + 1, 1)], None, ALU.is_equal).then_inc(d_oh, 1)

            def add_d(s, u):
                dve.wait_ge(d_mm, s + 2)
                wait(dve, d_add, s)
                dve.tensor_reduce(red[:, :].rearrange("p (i h) -> p i h", i=2),
                                  ps[3][:, 0:6 * HEADS].rearrange("p (i q h) -> p i h q", i=2, q=3), AX.X,
                                  ALU.add).then_inc(d_red, 1)
                dve.wait_ge(d_red, s + 2)
                o = ed_e[:, bass.ds(2 * u * HEADS, 2 * HEADS)]
                tt(o, o, red[:, :], ALU.add).then_inc(d_add, 1)

            def tile_d(d, k):
                lo, hi = bounds(dve, d)
                new_iod(d, k, d_iod)
                hot_d(d, lo, k)
                if not isinstance(d, int) or d >= 1:
                    add_d(d + lo - 1, lo)

                def body(u):
                    hot_d(d, u, k)
                    add_d(d + u - 1, u - 1)
                rest_of(dve, lo, hi, body)

            dve.sem_inc(d_red, 1)
            dve.wait_ge(d_zero, 1)
            dve.wait_ge(b_code, 1)
            node_tiles(dve, tile_d)
            add_d(NT - 1 + LAST_PAIR, LAST_PAIR)

            for k in range(2):
                dve.wait_ge(es_mv[k], 16 * ((TPC + 1 - k) // 2))
            dve.wait_ge(d_add, NT + LAST_PAIR)
            by_group = "p (c j h) -> p j c h"
            tt(ex3[:, :, 0:HEADS].rearrange("p (c j) h -> p j c h", j=TPC),
               es_all.rearrange("p (j c h) -> p j c h", c=CHUNKS, h=HEADS),
               ed_e.rearrange(by_group, c=CHUNKS, h=HEADS), ALU.add).then_inc(t_x, 1)
            dve.wait_ge(t_cp, -(-TPC // 4))
            dve.wait_ge(e_same, 3)
            v = [0]

            def link(ins):
                v[0] += 1
                ins.then_inc(t_v, 1)
                dve.wait_ge(t_v, v[0])

            def forward(initial):
                return dve.tensor_tensor_scan(fwd, same[:, 0:CHUNK], scan[:, :], initial, ALU.min, ALU.max)

            def backward(o, initial):
                return dve.tensor_tensor_scan(o[:, ::-1], same[:, CHUNK:0:-1], fwd[:, ::-1], initial, ALU.min, ALU.max)

            dve.wait_ge(t_x, 1)
            link(forward(-BIG))
            link(copy(ends[:, 1:2], fwd[:, CHUNK - 1:CHUNK]))
            link(backward(fwd, -BIG))
            link(copy(ends[:, 0:1], fwd[:, 0:1]))
            link(dve.memset(cont[:, :], -BIG))
            link(dve.memset(kl[:, :], -BIG))
            dve.wait_ge(t_pe, 1)
            link(copy(rows[:, :], ps[2][0:1, :]))
            first_mx, last_mx, first_d, last_d = (rows[:, q * P:(q + 1) * P] for q in range(4))
            link(tt(cont[:, HEADS:P], first_d[:, HEADS:P], last_d[:, 0:P - HEADS], ALU.is_equal))
            link(ts(cont[:, HEADS:P], cont[:, HEADS:P], 2 * BIG, -BIG, ALU.mult, ALU.add))
            link(tt(one[:, :], first_d, last_d, ALU.is_equal))
            link(ts(one[:, :], one[:, :], 2 * BIG, -BIG, ALU.mult, ALU.add))
            link(tt(kl[:, :], cont[:, :], one[:, :], ALU.min))
            for h in range(HEADS):
                last = dve.tensor_tensor_scan(outr[:, h::HEADS], kl[:, h::HEADS], last_mx[:, h::HEADS], -BIG,
                                              ALU.min, ALU.max)
            link(last)
            link(dve.memset(inits[0][:, :], -BIG))
            link(tt(inits[0][:, HEADS:P], cont[:, HEADS:P], outr[:, 0:P - HEADS], ALU.min))
            link(dve.memset(kl[:, :], -BIG))
            link(tt(kl[:, 0:P - HEADS], cont[:, HEADS:P], one[:, 0:P - HEADS], ALU.min))
            for h in range(HEADS):
                last = dve.tensor_tensor_scan(outr[:, h::HEADS][:, ::-1], kl[:, h::HEADS][:, ::-1],
                                              first_mx[:, h::HEADS][:, ::-1], -BIG, ALU.min, ALU.max)
            link(last)
            link(dve.memset(inits[1][:, :], -BIG))
            link(tt(inits[1][:, 0:P - HEADS], cont[:, HEADS:P], outr[:, HEADS:P], ALU.min))
            assert v[0] == 20
            dve.wait_ge(t_pe, 2)
            link(copy(init_c[:, :], ps[3][:, 0:2]))
            link(forward(init_c[:, 0:1]))
            link(backward(scan[:, :], init_c[:, 1:2]))
            assert v[0] == 23

            n_g4 = -(-TPC // 4)
            for g in range(0, TPC, 4):
                m = min(4, TPC - g)
                dve.wait_ge(t_bt, g // 4 + 1)
                sel = slice(g, g + m)
                tt(mx_e.rearrange(by_group, c=CHUNKS, h=HEADS)[:, sel],
                   ps[g // 4 % 2][:, 0:m * P].rearrange("p (j c h) -> p j c h", c=CHUNKS, h=HEADS),
                   ed_e.rearrange(by_group, c=CHUNKS, h=HEADS)[:, sel], ALU.add).then_inc(t_z, 1)
            dve.wait_ge(t_z, n_g4)
            link(stt(mx_e, mx_e, SLOPE, mx_e, ALU.mult, ALU.max))
            e8 = ex3[:, :, 0:HEADS]
            link(stt(e8, e8, SLOPE, e8, ALU.mult, ALU.max))
            tt(e8, e8, mx_e.rearrange("p (t h) -> p t h", h=HEADS), ALU.subtract).then_inc(t_e, 1)
            dve.wait_ge(t_ex, 1)
            c8 = coef[:, :].rearrange("p (t h) -> p t h", h=HEADS)
            dve.wait_ge(e_ev, 20)
            tt(c8, c8, e8, ALU.mult).then_inc(t_co, 1)
            dve.memset(iod[0][0:1, 0:1], 0.0).then_inc(t_co, 1)
            dve.wait_ge(t_co, 2)

            def weigh(u):
                dve.wait_ge(in0, u + 1)
                tt(ring(msg, u, WORK, GW).rearrange("p (a e) -> p a e", e=HEAD_DIM),
                   ring(g_ring, u, RING, GW).rearrange("p (a e) -> p a e", e=HEAD_DIM),
                   coef[:, bass.ds(2 * u * HEADS, 2 * HEADS)].unsqueeze(2).to_broadcast([P, 2 * HEADS, HEAD_DIM]),
                   ALU.mult).then_inc(msg0, 1)

            def new_pair0(d, u):
                slot_free(dve, d, u, done_f0, done_b0)
                weigh(u)

            def one_hot(buf, k, u, t):
                return ts(buf[:, :], iod[k][:, :], dst_e[:, bass.ds(2 * u + t, 1)], None, ALU.is_equal)

            def hot_first(d, u, k, bufs, ready, done):
                wait(dve, done, d)
                one_hot(bufs[0], k, u, 0)
                one_hot(bufs[1], k, u, 1).then_inc(ready, 1)

            def hot_rest(u, k, bufs, ready_a, ready_b, done_a, done_b):
                dve.wait_ge(done_a, u)
                one_hot(bufs[0], k, u, 0).then_inc(ready_a, 1)
                dve.wait_ge(done_b, u - 1 + WORK)
                one_hot(bufs[1], k, u, 1).then_inc(ready_b, 1)

            def divisors0(d, k, lo):
                tile_done(dve, d + 1, lo, done_f0, done_b0)
                ts(r9[k][:, 0:HEADS], ps[2 + k][:, 0:HEADS], 0.5, None, ALU.max)
                ts(r9[k][:, HEADS:EW], ps[2 + k][:, HEADS:EW], 1.0, None, ALU.max).then_inc(f_r9, 1)
                dve.wait_ge(f_r9, d + 1)
                wait(dve, f_w, d - 1)
                dve.reciprocal(rr[k][:, :], r9[k][:, :]).then_inc(f_rr, 1)
                dve.wait_ge(f_rr, d + 1)
                copy(rdeg[:, bass.ds(d, 1)], rr[k][:, HEADS:EW])

            def moments0(d, k):
                dve.wait_ge(f_w, d + 1)
                dve.wait_ge(xl[k], 8 * (d - k) + 16)
                tt(hn[k][:, :], hn[k][:, :], xt[k][:, :], ALU.add).then_inc(f_x1, 1)
                dve.wait_ge(f_x1, d + 1)
                stats(hn[k][:, :], k, f_st, f_mv, d)

            def shift0(d, k):
                wait(dve, f_h1, d - 1)
                scale_and_shift(k, f_mv, f_sd, f_rs, f_nm, d)

            def tile0(d, k):
                lo, hi = bounds(dve, d)
                new_iod(d, k, iod0)
                hot_first(d, lo, k, oh_first, hot_f0, done_f0)

                def hots(u):
                    hot_rest(u, k, oh_rest, hot_a0, hot_b0, done_a0, done_b0)

                def between():
                    if from_tile(d, 1):
                        divisors0(d - 1, 1 - k, lo)
                    if from_tile(d, 2):
                        moments0(d - 2, k)
                        shift0(d - 2, k)

                def body(u):
                    hots(u)
                    new_pair0(d, u + 1)
                second_then_rest(dve, lo, hi, hots, between, lambda u: new_pair0(d, u + 1), body)

            for u in range(2):
                weigh(u)
            node_tiles(dve, tile0, 4)
            moments0(NT - 2, 1)
            divisors0(NT - 1, 0, LAST_PAIR)
            shift0(NT - 2, 1)
            moments0(NT - 1, 0)
            shift0(NT - 1, 0)

            def new_pair1(u):
                dve.wait_ge(hi1, u + 1)
                tt(ring(lo_r, u, WORK, GW), ring(g_ring, u, RING, GW), ring(hi_r, u, WORK, GW).bitcast(F32),
                   ALU.subtract).then_inc(lo1, 1)

            def moments1(d, k):
                dve.wait_ge(m_y, d + 1)
                wait(dve, y_out[k], 8 * (d - k))
                tt(yo[k][:, :], ps[6 + k][:, :], row_bias[:, :], ALU.add).then_inc(n_y, 1)
                dve.wait_ge(n_y, d + 1)
                stats(yo[k][:, :], k, n_st, n_mv, d)

            def final1(d, k):
                dve.wait_ge(n_yn, d + 1)
                tt(yo[k][:, :], yo[k][:, :], row_gamma[:, :], ALU.mult).then_inc(n_g, 1)
                dve.wait_ge(n_g, d + 1)
                tt(yo[k][:, :], yo[k][:, :], row_beta[:, :], ALU.add).then_inc(n_b, 1)
                dve.wait_ge(n_b, d + 1)
                dve.wait_ge(x1l[k], 8 * (d - k) + 16)
                tt(yo[k][:, :], yo[k][:, :], xt[k][:, :], ALU.add).then_inc(n_o, 1)

            def between1(d, k):
                if in_tiles(d - 3):
                    moments1(d - 3, 1 - k)
                if in_tiles(d - 4):
                    final1(d - 4, k)
                if in_tiles(d - 3):
                    scale_and_shift(1 - k, n_mv, n_sd, n_rs, n_nm, d - 3)

            def tile1(d, k):
                lo, hi = bounds(dve, d)
                new_iod(d, k, iod1)
                hot_first(d, lo, k, ohr_first, hot_f1, done_f1)

                def hots(u):
                    hot_rest(u, k, ohr_rest, hot_a1, hot_b1, done_a1, done_b1)

                def body(u):
                    hots(u)
                    new_pair1(u + 1)
                second_then_rest(dve, lo, hi, hots, lambda: between1(d, k), lambda u: new_pair1(u + 1), body)

            for u in range(2):
                new_pair1(u)
            node_tiles(dve, tile1, 6)
            for d in range(NT, NT + 4):
                between1(d, d % 2)


def kernel(x, src, dst, edge_attr_8, L0_gnn_W, L0_gnn_b, L0_gnn_w_att_src, L0_gnn_w_att_dst,
           L1_gnn_W_self, L1_gnn_W_neigh, L1_gnn_bias, L1_gnn_gamma, L1_gnn_beta):
    import numpy as np
    import concourse.bacc as bacc
    from concourse.bass_utils import run_bass_kernel_spmd

    arrays = {
        "x": np.asarray(x), "src": np.asarray(src), "dst": np.asarray(dst), "dist": np.asarray(edge_attr_8),
        "w0t": np.asarray(L0_gnn_W).T, "b0": np.asarray(L0_gnn_b),
        "att_src": np.asarray(L0_gnn_w_att_src).reshape(-1), "att_dst": np.asarray(L0_gnn_w_att_dst).reshape(-1),
        "wst": np.asarray(L1_gnn_W_self).T, "wnt": np.asarray(L1_gnn_W_neigh).T, "bias": np.asarray(L1_gnn_bias),
        "gamma": np.asarray(L1_gnn_gamma), "beta": np.asarray(L1_gnn_beta),
    }
    arrays = {k: np.ascontiguousarray(a) for k, a in arrays.items()}
    nc = bacc.Bacc("TRN2", target_bir_lowering=False, num_devices=1)
    args = [nc.dram_tensor(k, a.shape, mybir.dt.from_np(a.dtype), kind="ExternalInput").ap()
            for k, a in arrays.items()]
    out = nc.dram_tensor("out", (N_NODES, DIM), F32, kind="ExternalOutput").ap()
    gnn_kernel(nc, *args, out)
    return run_bass_kernel_spmd(nc, [arrays], core_ids=[0]).results[0]["out"]
```

```python
import concourse.bass as bass
from concourse import mybir
from contextlib import ExitStack

F32 = mybir.dt.float32
F32R = mybir.dt.float32r
BF16 = mybir.dt.bfloat16
I32 = mybir.dt.int32
ALU = mybir.AluOpType
ACT = mybir.ActivationFunctionType
AX = mybir.AxisListType

N_NODES, N_EDGES, DIM, HEADS = 6250, 100000, 512, 8
HEAD_DIM = DIM // HEADS
P = 128
KC = DIM // P
NT = -(-N_NODES // P)
LAST_ROWS = N_NODES - (NT - 1) * P
CHUNKS = P // HEADS
TILES = -(-N_EDGES // (P * CHUNKS)) * CHUNKS
TPC = TILES // CHUNKS
CHUNK = TPC * P
PAIRS = TILES // 2
LAST_PAIR = (N_EDGES - 1) // (2 * P)
ROWS = TILES // 8
ROW_EDGES = 8 * P
FULL_ROWS = N_EDGES // ROW_EDGES
REST = N_EDGES - FULL_ROWS * ROW_EDGES
FULL_TILES = N_EDGES // P
BUCKETS = NT + 1
PAD_DST = 8000
BIG = 1e38
EPS = 1e-5
SLOPE = 0.2
RING = 8
WEIGHED, WORK = 5, 3
ACT_HEADS = 4
AHEAD = 2
GW = 2 * DIM
EW = HEADS + 1
COUNT_STEPS, PLACE_STEPS = 8, 17
CODE = 512


def wait(eng, sem, value):
    if not (isinstance(value, int) and value <= 0):
        eng.wait_ge(sem, value)


def ring(buf, u, depth, width):
    return buf[:, bass.ds((u % depth) * width, width)]


def gnn_kernel(nc, x, src, dst, dist, w0t, b0, att_src, att_dst, wst, wnt, bias, gamma, beta, out):
    h_tab = nc.dram_tensor("h_tab", (NT * P, DIM), F32).ap()
    es_tab = nc.dram_tensor("es_tab", (NT * P, HEADS), F32).ap()
    x1_tab = nc.dram_tensor("x1_tab", (NT * P, DIM), F32).ap()
    h1_tab = nc.dram_tensor("h1_tab", (NT * P, DIM), F32).ap()
    dst_tab = nc.dram_tensor("dst_tab", (TILES * P, 1), I32).ap()
    src_tab = nc.dram_tensor("src_tab", (TILES * P, 1), I32).ap()
    dist_tab = nc.dram_tensor("dist_tab", (TILES * P, HEADS), F32).ap()

    ctx = ExitStack()
    with ctx:
        def sb(name, shape, dt=F32):
            return ctx.enter_context(nc.sbuf_tensor(name, shape, dt))

        def sem(name):
            return ctx.enter_context(nc.semaphore(name))

        ident = sb("ident", [P, P])
        ident_b = sb("ident_b", [P, P], BF16)
        iota_i = sb("iota_i", [P, P], I32)
        iota_f = sb("iota_f", [P, P])
        first_i = sb("first_i", [P, NT + 1], I32)
        first_f = sb("first_f", [P, NT + 1])
        thr_i = sb("thr_i", [P, 1], I32)
        thr_f = sb("thr_f", [P, 1])
        pick_last = sb("pick_last", [P, 64])
        eps_c = sb("eps_c", [P, 1])
        row_b0 = sb("row_b0", [P, DIM])
        row_as = sb("row_as", [P, DIM])
        row_ad = sb("row_ad", [P, DIM])
        src_e = sb("src_e", [P, TILES + 2 * (RING + 1)], I32)
        src_g = sb("src_g", [P, TILES], I32)
        dst_e = sb("dst_e", [P, TILES])
        same = sb("same", [P, CHUNK + 1], BF16)
        ex_buf = sb("ex_buf", [P, TILES * EW])
        coef = sb("coef", [P, (TILES + 2) * HEADS])
        scan = sb("scan", [P, CHUNK])
        idx_ring = sb("idx_ring", [P, RING * 2], I32)
        xt = [sb(f"xt{k}", [P, DIM]) for k in range(2)]
        hn = [sb(f"hn{k}", [P, DIM]) for k in range(2)]
        hT = [sb(f"hT{k}", [P, DIM]) for k in range(2)]
        ho = [sb(f"ho{k}", [P, DIM]) for k in range(2)]
        st = [sb(f"st{k}", [P, 6]) for k in range(2)]
        mv = [sb(f"mv{k}", [P, 2]) for k in range(2)]
        sd = [sb(f"sd{k}", [P, 1]) for k in range(2)]
        rs = [sb(f"rs{k}", [P, 1]) for k in range(2)]
        nm = [sb(f"nm{k}", [P, 1]) for k in range(2)]
        es_st = [sb(f"es_st{k}", [P, HEADS]) for k in range(2)]
        ed_n = sb("ed_n", [P, NT * HEADS])
        ed_r = sb("ed_r", [P, NT * HEADS])
        ed3 = sb("ed3", [P, NT * 3 * HEADS], BF16)
        rdeg = sb("rdeg", [P, NT])
        cnt = sb("cnt", [64, 1])
        falls = sb("falls", [P, 1])
        ones_c = sb("ones_c", [P, 1])
        flag = sb("flag", [1, 1], I32)
        bnd_f = sb("bnd_f", [1, 64])
        code_f = sb("code_f", [1, 64])
        code = sb("code", [1, 64], I32)
        iod = [sb(f"iod{k}", [P, P]) for k in range(2)]
        oh_b = sb("oh_b", [P, 2 * P], BF16)
        ohT_b = sb("ohT_b", [P, 2 * P], BF16)
        red = sb("red", [P, 2 * HEADS])
        oh_first = [sb(f"oh_first{t}", [P, P]) for t in range(2)]
        oh_rest = [sb(f"oh_rest{t}", [P, P]) for t in range(2)]
        ohr_first = [sb(f"ohr_first{t}", [P, P], F32R) for t in range(2)]
        ohr_rest = [sb(f"ohr_rest{t}", [P, P], F32R) for t in range(2)]
        st_i = [sb(f"st_i{k}", [P, CHUNKS], I32) for k in range(2)]
        es_r = [sb(f"es_r{k}", [P, P]) for k in range(2)]
        ends = sb("ends", [P, 4])
        rows = sb("rows", [1, 4 * P])
        cont = sb("cont", [1, P])
        one = sb("one", [1, P])
        kl = sb("kl", [1, P])
        outr = sb("outr", [1, P])
        inits = [sb(f"inits{k}", [1, P]) for k in range(2)]
        init_c = sb("init_c", [P, 2])
        r9 = [sb(f"r9{k}", [P, EW]) for k in range(2)]
        rr = [sb(f"rr{k}", [P, EW]) for k in range(2)]

        with nc.sbuf_tensor("edf", [P, 2 * CHUNK], F32) as edf:
            pass
        with nc.sbuf_tensor("msg", [P, WEIGHED * GW], F32) as msg:
            pass
        hi_r = sb("hi_r", [P, WORK * GW], F32R)
        lo_r = sb("lo_r", [P, WORK * GW], F32R)
        mT = [sb(f"mT{k}", [P, DIM]) for k in range(2)]
        yo = [sb(f"yo{k}", [P, DIM]) for k in range(2)]
        g_ring = sb("g_ring", [P, RING * GW])

        ps = [ctx.enter_context(nc.psum_tensor(f"bank{b}", [P, 512], F32)) for b in range(8)]

        below = hn[0][0:64, 0:PAIRS]
        src_c = ex_buf[0:ROWS, 0:ROW_EDGES].bitcast(I32)
        dst_c = ex_buf[0:ROWS, ROW_EDGES:2 * ROW_EDGES].bitcast(I32)
        src_cf = ex_buf[0:ROWS, 2 * ROW_EDGES:3 * ROW_EDGES]
        dst_cf = ex_buf[0:ROWS, 3 * ROW_EDGES:4 * ROW_EDGES]
        dst_next = ex_buf[0:ROWS, 4 * ROW_EDGES:5 * ROW_EDGES].bitcast(I32)
        dist_c = edf[0:ROWS, 0:ROW_EDGES * HEADS]
        dst_s = scan[:, :].bitcast(I32)
        ed_e = edf[:, 0:CHUNK]
        es_all = edf[:, CHUNK:2 * CHUNK]
        fwd = edf[:, CHUNK:2 * CHUNK]
        ws = scan[:, 0:KC * DIM]
        wn = scan[:, KC * DIM:2 * KC * DIM]
        late = RING * GW - 2 * KC * DIM
        w0 = g_ring[:, late:late + KC * DIM]
        ms, md = ([g_ring[:, late + (KC + 2 * q + k) * DIM:late + (KC + 2 * q + k + 1) * DIM] for k in range(2)]
                  for q in range(2))
        row_bias, row_gamma, row_beta = (scan[:, (2 * KC + q) * DIM:(2 * KC + q + 1) * DIM] for q in range(3))
        ones_r = cont[:, :]
        ex3 = ex_buf[:, :].rearrange("p (t h) -> p t h", h=EW)

        s_w = sem("s_w"); s_row = sem("s_row"); s_ec = sem("s_ec"); s_dist = sem("s_dist")
        s_ds = sem("s_ds"); s_w1 = sem("s_w1")
        padded = sem("padded"); p_go = sem("p_go"); v_go = sem("v_go")
        k_id = sem("k_id"); k_cst = sem("k_cst"); k_cf = sem("k_cf")
        e_f = sem("e_f"); e_tr = sem("e_tr"); e_ev = sem("e_ev"); e_same = sem("e_same"); e_sg = sem("e_sg")
        b_mm = sem("b_mm"); b_cnt = sem("b_cnt"); b_tr = sem("b_tr"); b_row = sem("b_row"); b_code = sem("b_code")
        x_in = [sem(f"x_in{k}") for k in range(2)]
        h_out = [sem(f"h_out{k}") for k in range(2)]
        es_out = [sem(f"es_out{k}") for k in range(2)]
        a_st = sem("a_st"); a_mv = sem("a_mv"); a_sd = sem("a_sd"); a_rs = sem("a_rs"); a_nm = sem("a_nm")
        a_h0 = sem("a_h0"); a_tr = sem("a_tr"); a_hT = sem("a_hT"); a_mm = sem("a_mm"); a_hb = sem("a_hb")
        a_h = sem("a_h"); a_ms = sem("a_ms"); a_md = sem("a_md"); a_es = sem("a_es"); a_ed = sem("a_ed")
        d_split = sem("d_split")
        st_in = [sem(f"st_in{k}") for k in range(2)]
        eg_in = [sem(f"eg_in{k}") for k in range(2)]
        es_mv = [sem(f"es_mv{k}") for k in range(2)]
        d_oh = sem("d_oh"); d_tr = sem("d_tr"); d_cp = sem("d_cp"); d_mm = sem("d_mm")
        d_red = sem("d_red"); d_add = sem("d_add"); d_zero = sem("d_zero")
        t_tr = sem("t_tr"); t_cp = sem("t_cp"); t_x = sem("t_x"); t_v = sem("t_v"); t_pe = sem("t_pe")
        t_bt = sem("t_bt"); t_z = sem("t_z"); t_f = sem("t_f"); t_sum = sem("t_sum"); t_ex = sem("t_ex"); t_co = sem("t_co")
        g_in = [sem(f"g_in{k}") for k in range(RING)]
        in0 = sem("in0"); idx0 = sem("idx0"); msg0 = sem("msg0"); msg_act0 = sem("msg_act0")
        hot_f0 = sem("hot_f0"); hot_a0 = sem("hot_a0"); hot_b0 = sem("hot_b0")
        done_f0 = sem("done_f0"); done_a0 = sem("done_a0"); done_b0 = sem("done_b0")
        xl = [sem(f"xl{k}") for k in range(2)]
        x1_out = [sem(f"x1_out{k}") for k in range(2)]
        h1_out = [sem(f"h1_out{k}") for k in range(2)]
        f_r9 = sem("f_r9"); f_rr = sem("f_rr"); f_w = sem("f_w"); f_x1 = sem("f_x1"); f_st = sem("f_st")
        f_mv = sem("f_mv"); f_sd = sem("f_sd"); f_rs = sem("f_rs"); f_nm = sem("f_nm"); f_h1 = sem("f_h1")
        numbers = sem("numbers")
        in1 = sem("in1"); idx1 = sem("idx1"); hi1 = sem("hi1"); lo1 = sem("lo1")
        hot_f1 = sem("hot_f1"); hot_a1 = sem("hot_a1"); hot_b1 = sem("hot_b1")
        done_f1 = sem("done_f1"); done_a1 = sem("done_a1"); done_b1 = sem("done_b1")
        hl = [sem(f"hl{k}") for k in range(2)]
        x1l = [sem(f"x1l{k}") for k in range(2)]
        y_out = [sem(f"y_out{k}") for k in range(2)]
        m_mn = sem("m_mn"); m_htr = sem("m_htr"); m_mtr = sem("m_mtr"); m_hT = sem("m_hT"); m_mT = sem("m_mT")
        m_one = sem("m_one"); m_self = sem("m_self"); m_y = sem("m_y"); n_st = sem("n_st"); n_mv = sem("n_mv")
        n_sd = sem("n_sd"); n_rs = sem("n_rs"); n_nm = sem("n_nm"); n_yn = sem("n_yn"); n_g = sem("n_g")
        n_b = sem("n_b"); n_o = sem("n_o")

        o_in = sem("o_in"); o_v = sem("o_v"); o_pe = sem("o_pe"); o_flag = sem("o_flag")
        c_in = [sem(f"c_in{k}") for k in range(2)]
        c_v = [sem(f"c_v{k}") for k in range(2)]
        c_pe = [sem(f"c_pe{k}") for k in range(2)]
        c_pad = sem("c_pad")
        c_src = sem("c_src"); c_dist = sem("c_dist"); c_start = sem("c_start"); c_sum = sem("c_sum")
        c_o = [sem(f"c_o{k}") for k in range(3)]

        def part_of_coef(first, n):
            return coef[:, first:first + n]

        ones_m, lower, upper, lo_hot, lo_hotT, diag = (part_of_coef(q * P, P) for q in range(6))
        above = part_of_coef(6 * P, BUCKETS + 1)
        hi_hot = part_of_coef(7 * P, BUCKETS)
        table = part_of_coef(8 * P, BUCKETS)
        totals = part_of_coef(9 * P, BUCKETS)
        sums = part_of_coef(10 * P, BUCKETS)
        picked = part_of_coef(11 * P, BUCKETS)
        same_dst = part_of_coef(12 * P, P)
        zeros_m = part_of_coef(13 * P, P)
        dst_f, n_above, lo_f, base_f, rank_f, place_f = (part_of_coef(14 * P + q, 1) for q in range(6))
        dst_col, src_col, place_i = (part_of_coef(15 * P + q, 1).bitcast(I32) for q in range(3))
        dist_col = part_of_coef(16 * P, HEADS)

        block = ctx.enter_context(nc.Block())

        def disorder(eng):
            eng.wait_ge(o_flag, 1)
            c = eng.value_load(flag[0:1, 0:1], min_val=0, max_val=N_EDGES)
            return eng.snap(c)

        def sort_tiles(eng, body):
            body(0, P)
            with eng.Fori(1, FULL_TILES) as t:
                body(t, P)
            body(FULL_TILES, N_EDGES - FULL_TILES * P)

        def bounds(eng, d):
            c = eng.value_load(code[0:1, bass.ds(d, 1)], min_val=0, max_val=LAST_PAIR * CODE + LAST_PAIR)
            lo = nc.s_assert_within(c // CODE, 0, LAST_PAIR, skip_runtime_bounds_check_because="a count of pairs")
            hi = nc.s_assert_within(c % CODE, 0, LAST_PAIR, skip_runtime_bounds_check_because="a count of pairs")
            return eng.snap(lo), eng.snap(hi)

        def rest_of(eng, lo, hi, body):
            with eng.If(lo < hi):
                with eng.Fori(lo + 1, hi + 1) as u:
                    body(u)
                eng.nop()
            eng.nop()

        def second_then_rest(eng, lo, hi, second, between, body, after=None, end=None, last=None):
            second_pair = nc.s_assert_within(lo + 1, 1, LAST_PAIR, skip_runtime_bounds_check_because="lo < hi")

            def if_second(step):
                with eng.If(lo < hi):
                    step()
                    eng.nop()
                eng.nop()

            if_second(lambda: second(second_pair))
            between()
            if after:
                if_second(lambda: after(second_pair))
            with eng.If(lo + 1 < hi):
                with eng.Fori(lo + 2, hi + 1) as u:
                    body(u)
                eng.nop()
            eng.nop()
            if end:
                end()
            if last:
                if_second(lambda: last(hi))

        def node_tiles(eng, body, peeled=2):
            for d in range(peeled):
                body(d, d % 2)
            with eng.Fori(peeled // 2, NT // 2 - 1) as j:
                body(2 * j, 0)
                body(2 * j + 1, 1)
            for d in range(NT - 3, NT):
                body(d, d % 2)

        def tiles_by_two(eng, body):
            for i in range(4):
                body(i, i % 2, i // 2)
            with eng.Fori(2, NT // 2 - 1) as j:
                body(2 * j, 0, j)
                body(2 * j + 1, 1, j)
            for i in range(NT - 3, NT):
                body(i, i % 2, i // 2)

        def from_tile(d, first):
            return not isinstance(d, int) or d >= first

        def in_tiles(d):
            return not isinstance(d, int) or 0 <= d < NT

        def tile_done(eng, d, lo, done_f, done_b):
            eng.wait_ge(done_f, d)
            eng.wait_ge(done_b, lo + WORK)

        def slot_free(eng, firsts, u, done_f, done_b):
            wait(eng, done_f, firsts)
            wait(eng, done_b, u)

        def load_row(eng, row, of, signal):
            eng.dma_start(row[:, :], of.rearrange("(a n) -> a n", a=1).to_broadcast([P, DIM])).then_inc(signal, 16)

        @block.sync
        def _(sp):
            def edge_rows(part, of, width, signal, skip=0):
                n, rest = FULL_ROWS * ROW_EDGES * width, REST * width - skip
                sp.dma_start(part[0:FULL_ROWS, :],
                             of[skip:n + skip].rearrange("(r e) -> r e", r=FULL_ROWS)).then_inc(signal, 16)
                sp.dma_start(part[FULL_ROWS:FULL_ROWS + 1, 0:rest],
                             of[n + skip:n + skip + rest].rearrange("(r e) -> r e", r=1)).then_inc(signal, 16)

            sp.dma_start(xt[0][:, :], x[0:P, :]).then_inc(x_in[0], 16)
            sp.wait_ge(padded, 5)
            edge_rows(dst_c, dst, 1, o_in)
            edge_rows(dst_next, dst, 1, o_in, skip=1)
            sp.dma_start(xt[1][:, :], x[P:2 * P, :]).then_inc(x_in[1], 16)

            def edge_loads(dst, src, dist):
                edge_rows(src_c, src, 1, s_ec)
                edge_rows(dist_c, dist.rearrange("e h -> (e h)"), HEADS, s_dist)
                for c in range(CHUNKS):
                    n = min(CHUNK, N_EDGES - c * CHUNK)
                    sp.dma_start(dst_s[c * HEADS:(c + 1) * HEADS, 0:n],
                                 dst[c * CHUNK:c * CHUNK + n].rearrange("(a n) -> a n", a=1)
                                 .to_broadcast([HEADS, n])).then_inc(s_ds, 16)

            def column(of, t, n):
                return of[bass.ds(t * P, n)].rearrange("(p a) -> p a", a=1)

            def feed_count(t, n):
                sp.wait_ge(c_v[0], COUNT_STEPS * t + 1)
                sp.dma_start(dst_col[0:n, :], column(dst, t, n)).then_inc(c_in[0], 16)

            def feed_place(t, n):
                for q in range(3):
                    wait(sp, c_o[q], 16 * t)
                sp.wait_ge(c_v[1], PLACE_STEPS * t + 1)
                sp.dma_start(dst_col[0:n, :], column(dst, t, n)).then_inc(c_in[1], 16)
                sp.dma_start(src_col[0:n, :], column(src, t, n)).then_inc(c_src, 16)
                sp.dma_start(dist_col[0:n, :], dist[bass.ds(t * P, n), :]).then_inc(c_dist, 16)

            fallen = disorder(sp)
            with sp.If(fallen > 0):
                sp.wait_ge(c_pad, 1)
                sort_tiles(sp, feed_count)
                sp.wait_ge(c_start, 1)
                sort_tiles(sp, feed_place)
                for q in range(3):
                    sp.wait_ge(c_o[q], 16 * (FULL_TILES + 1))
                dst_sorted = dst_tab.rearrange("e a -> (e a)")
                edge_rows(dst_c, dst_sorted, 1, s_ec)
                edge_loads(dst_sorted, src_tab.rearrange("e a -> (e a)"), dist_tab)
            with sp.If(fallen < 1):
                sp.sem_inc(s_ec, 32)
                edge_loads(dst, src, dist)
            sp.nop()

            def store(i, k):
                sp.wait_ge(a_h, i + 1)
                sp.dma_start(h_tab[bass.ds(i * P, P), :], ho[k][:, :]).then_inc(h_out[k], 16)
                sp.wait_ge(a_es, i + 1)
                sp.dma_start(es_tab[bass.ds(i * P, P), :], es_st[k][:, :]).then_inc(es_out[k], 16)

            with sp.Fori(0, NT // 2) as j:
                store(2 * j, 0)
                store(2 * j + 1, 1)
            store(NT - 1, 0)

            sp.wait_ge(e_sg, 1)

            def hand(j, k):
                sp.dma_start(st_i[k][:, :], src_g[:, bass.ds(j * CHUNKS, CHUNKS)]).then_inc(st_in[k], 16)

            def move(j, k, n):
                sp.wait_ge(eg_in[k], 16 * CHUNKS * (n + 1))
                sp.dma_start(es_all[:, bass.ds(j * P, P)], es_r[k][:, :]).then_inc(es_mv[k], 16)

            hand(0, 0)
            hand(1, 1)
            sp.wait_ge(e_ev, 20)
            with sp.Fori(0, TPC // 2 - 1) as j:
                move(2 * j, 0, j)
                hand(2 * j + 2, 0)
                move(2 * j + 1, 1, j)
                hand(2 * j + 3, 1)
            move(TPC - 3, 0, TPC // 2 - 1)
            hand(TPC - 1, 0)
            move(TPC - 2, 1, TPC // 2 - 1)
            move(TPC - 1, 0, TPC // 2)

            with sp.Fori(0, PAIRS // RING) as i:
                for k in range(RING):
                    sp.wait_ge(g_in[k], 32 * (i + 1))
                    sp.sem_inc(in0, 1)
            sp.sem_inc(in0, AHEAD - 1)
            sp.dma_start(ws.rearrange("p (k n) -> p k n", k=KC),
                         wst.rearrange("(k p) n -> p k n", p=P)).then_inc(s_w1, 16)
            sp.dma_start(wn.rearrange("p (k n) -> p k n", k=KC),
                         wnt.rearrange("(k p) n -> p k n", p=P)).then_inc(s_w1, 16)
            for row, of in ((row_bias, bias), (row_gamma, gamma), (row_beta, beta)):
                load_row(sp, row, of, s_w1)
            with sp.Fori(0, PAIRS // RING) as i:
                for k in range(RING):
                    sp.wait_ge(g_in[k], 32 * (i + 1) + 32 * (PAIRS // RING))
                    sp.sem_inc(in1, 1)

        @block.gpsimd
        def _(pool):
            pool.memset(ident[:, :], 0.0).then_inc(k_id, 1)
            pool.memset(pick_last[:, :], 0.0).then_inc(k_id, 1)
            pool.iota(iota_i[:, :], pattern=[[1, P]], base=0, channel_multiplier=0).then_inc(k_cst, 1)
            pool.iota(first_i[:, :], pattern=[[P, NT + 1]], base=0, channel_multiplier=0).then_inc(k_cst, 1)
            pool.iota(thr_i[:, :], pattern=[[0, 1]], base=0, channel_multiplier=P).then_inc(k_cst, 1)
            pool.wait_ge(k_id, 2)
            pool.affine_select(out=ident[:, :], in_=ident[:, :], compare_op=ALU.not_equal, fill=1.0, base=0,
                               pattern=[[-1, P]], channel_multiplier=1).then_inc(k_id, 1)
            pool.affine_select(out=pick_last[:, :], in_=pick_last[:, :], compare_op=ALU.not_equal, fill=1.0,
                               base=1 - P, pattern=[[0, 64]], channel_multiplier=1).then_inc(k_id, 1)

            def place(t, n):
                pool.wait_ge(c_v[1], PLACE_STEPS * (t + 1))
                pool.wait_ge(c_src, 16 * (t + 1))
                pool.wait_ge(c_dist, 16 * (t + 1))
                pool.sem_inc(p_go, 1)
                for q, (tab, col) in enumerate(((dst_tab, dst_col), (src_tab, src_col), (dist_tab, dist_col))):
                    pool.indirect_dma_start(tab, bass.IndirectOffsetOnAxis(ap=place_i, axis=0), col,
                                            None).then_inc(c_o[q], 16)

            with pool.If(disorder(pool) > 0):
                sort_tiles(pool, place)
            pool.nop()

            pool.wait_ge(s_row, 48)

            def products(i, k, n):
                pool.wait_ge(a_h, i + 1)
                wait(pool, a_es, i - 1)
                pool.tensor_tensor(ms[k][:, :], ho[k][:, :], row_as[:, :], ALU.mult).then_inc(a_ms, 1)
                wait(pool, a_ed, i - 1)
                pool.tensor_tensor(md[k][:, :], ho[k][:, :], row_ad[:, :], ALU.mult).then_inc(a_md, 1)

            tiles_by_two(pool, products)

            for k in range(2):
                pool.wait_ge(es_out[k], 16 * ((NT + 1 - k) // 2))

            def group(k, n):
                pool.wait_ge(st_in[k], 16 * (n + 1))
                wait(pool, es_mv[k], 16 * n)
                pool.sem_inc(p_go, 1)
                for c in range(CHUNKS):
                    pool.indirect_dma_start(
                        es_r[k][:, c * HEADS:(c + 1) * HEADS], None, es_tab,
                        bass.IndirectOffsetOnAxis(ap=st_i[k][:, c:c + 1], axis=0)).then_inc(eg_in[k], 16)

            group(0, 0)
            group(1, 0)
            with pool.Fori(1, TPC // 2) as j:
                group(0, j)
                group(1, j)
            group(0, TPC // 2)

            def gathers(table, landed, idx_ready, used):
                def pair(i, m):
                    u, k = RING * i + m, m % RING
                    pool.wait_ge(idx_ready, u + 1)
                    for signal in used:
                        wait(pool, signal, u + 1 - RING)
                    pool.sem_inc(p_go, 1)
                    for t in range(2):
                        pool.indirect_dma_start(
                            g_ring[:, k * GW + t * DIM:k * GW + (t + 1) * DIM], None, table,
                            bass.IndirectOffsetOnAxis(ap=idx_ring[:, 2 * m + t:2 * m + t + 1], axis=0)
                        ).then_inc(landed[k], 16)

                for m in range(RING):
                    pair(0, m)
                with pool.Fori(1, PAIRS // RING) as i:
                    for m in range(RING):
                        pair(i, m)

            for k in range(2):
                pool.wait_ge(h_out[k], 16 * ((NT + 1 - k) // 2))
            gathers(h_tab, g_in, idx0, (msg0, msg_act0))
            for k in range(2):
                pool.wait_ge(h1_out[k], 16 * ((NT + 1 - k) // 2))
            gathers(h1_tab, g_in, idx1, (lo1,))

        @block.scalar
        def _(act):
            def normalise(i, k, n):
                act.wait_ge(a_mv, i + 1)
                act.activation(sd[k][:, :], mv[k][:, 1:2], ACT.Sqrt, bias=eps_c[:, :]).then_inc(a_sd, 1)
                act.wait_ge(a_nm, i + 1)
                wait(act, a_tr, i - 1)
                act.activation(hn[k][:, :], xt[k][:, :], ACT.Relu, bias=nm[k][:, :],
                               scale=rs[k][:, :]).then_inc(a_h0, 1)
                act.wait_ge(a_tr, i + 1)
                wait(act, a_mm, i - 1)
                act.copy(hT[k][:, :], ps[k][:, :]).then_inc(a_hT, 1)
                if in_tiles(i + 2):
                    rows = LAST_ROWS if isinstance(i, int) and i + 2 == NT - 1 else P
                    act.wait_ge(a_h0, i + 1)
                    act.dma_start(xt[k][0:rows, :], x[bass.ds((i + 2) * P, rows), :]).then_inc(x_in[k], 16)

            act.dma_start(w0[:, :].rearrange("p (k n) -> p k n", k=KC),
                         w0t.rearrange("(k p) n -> p k n", p=P)).then_inc(s_w, 16)
            for row, of in ((row_b0, b0), (row_as, att_src), (row_ad, att_dst)):
                load_row(act, row, of, s_row)
            act.wait_ge(k_cf, 1)
            tiles_by_two(act, normalise)

            def step_d(d, u):
                s = d + u
                act.wait_ge(d_tr, s + 2)
                act.wait_ge(d_mm, s + 1)
                act.copy(ohT_b[:, :], ps[2][:, 0:P].bitcast(BF16)).then_inc(d_cp, 1)

            def tile_d(d, k):
                lo, hi = bounds(act, d)
                step_d(d, lo)
                rest_of(act, lo, hi, lambda u: step_d(d, u))

            act.wait_ge(b_code, 1)
            node_tiles(act, tile_d)

            e_by_group = ex3[:, :, 0:HEADS].rearrange("p (c j) h -> p j c h", j=TPC)
            es_by_group = es_all.rearrange("p (j c h) -> p j c h", c=CHUNKS, h=HEADS)
            act.wait_ge(e_same, 3)
            for g in range(0, TPC, 4):
                m = min(4, TPC - g)
                act.wait_ge(t_x, g // 4 + 1)
                act.copy(e_by_group[:, g:g + m], es_by_group[:, g:g + m])
                act.wait_ge(t_tr, g // 4 + 1)
                act.copy(scan[:, g * P:(g + m) * P], ps[g // 4 % 2][:, 0:m * P]).then_inc(t_cp, 1)
            def stage(u, ready):
                act.copy(idx_ring[:, bass.ds((u % RING) * 2, 2)], src_e[:, bass.ds(2 * u, 2)]).then_inc(ready, 1)

            act.wait_ge(t_v, 22)
            for u in range(RING):
                stage(u, idx0)
            for k in range(2):
                act.dma_start(xt[k][:, :], x[k * P:(k + 1) * P, :]).then_inc(xl[k], 16)
            for g in range(0, TPC, 4):
                act.wait_ge(t_z, g // 4 + 1)
                some = e_by_group[:, g:min(g + 4, TPC)]
                act.activation(some, some, ACT.Exp).then_inc(t_ex, 1)

            def new_pair0(u):
                act.wait_ge(in0, u + 1)
                stage(u + RING, idx0)

            def weigh_act(u):
                act.wait_ge(in0, u + 1)
                if not isinstance(u, int) or u > AHEAD:
                    act.wait_ge(done_b0, u - WEIGHED + 1 + WORK)
                for h in range(HEADS - ACT_HEADS, HEADS):
                    col = DIM + h * HEAD_DIM
                    last = act.activation(msg[:, bass.ds((u % WEIGHED) * GW + col, HEAD_DIM)],
                                          g_ring[:, bass.ds((u % RING) * GW + col, HEAD_DIM)], ACT.Copy,
                                          scale=coef[:, bass.ds((2 * u + 1) * HEADS + h, 1)])
                last.then_inc(msg_act0, 1)

            def normalise0(d, k):
                act.wait_ge(f_rr, d + 1)
                wait(act, x1_out[k], 8 * (d - k))
                act.copy(rdeg[:, bass.ds(d, 1)], rr[k][:, HEADS:EW])
                for h in range(HEADS):
                    cols = slice(h * HEAD_DIM, (h + 1) * HEAD_DIM)
                    last = act.activation(hn[k][:, cols], ps[k][:, cols], ACT.Copy, scale=rr[k][:, h:h + 1])
                last.then_inc(f_w, 1)

            def sqrt0(d, k):
                act.wait_ge(f_mv, d + 1)
                act.activation(sd[k][:, :], mv[k][:, 1:2], ACT.Sqrt, bias=eps_c[:, :]).then_inc(f_sd, 1)
                act.dma_start(x1_tab[bass.ds(d * P, P), :], hn[k][:, :]).then_inc(x1_out[k], 16)

            def normed0(d, k):
                act.wait_ge(f_nm, d + 1)
                wait(act, h1_out[k], 8 * (d - k))
                act.activation(ho[k][:, :], hn[k][:, :], ACT.Relu, bias=nm[k][:, :],
                               scale=rs[k][:, :]).then_inc(f_h1, 1)
                act.wait_ge(f_h1, d + 1)
                act.dma_start(h1_tab[bass.ds(d * P, P), :], ho[k][:, :]).then_inc(h1_out[k], 16)

            def tile0(d, k):
                lo, hi = bounds(act, d)
                if from_tile(d, 3):
                    normed0(d - 3, 1 - k)
                if from_tile(d, 1):
                    normalise0(d - 1, 1 - k)
                if from_tile(d, 2):
                    sqrt0(d - 2, k)
                    n = LAST_ROWS if isinstance(d, int) and d == NT - 1 else P
                    act.dma_start(xt[k][0:n, :], x[bass.ds(d * P, n), :]).then_inc(xl[k], 16)

                def body(u):
                    new_pair0(u + 1)
                    weigh_act(u + AHEAD)
                rest_of(act, lo, hi, body)

            new_pair0(0)
            new_pair0(1)
            act.wait_ge(t_co, -(-TPC // 4))
            for u in range(AHEAD + 1):
                weigh_act(u)
            node_tiles(act, tile0, 6)
            normed0(NT - 3, 0)
            normalise0(NT - 1, 0)
            sqrt0(NT - 2, 1)
            normed0(NT - 2, 1)
            sqrt0(NT - 1, 0)
            normed0(NT - 1, 0)

            act.wait_ge(in0, PAIRS)
            for u in range(RING):
                stage(u, idx1)
            for k in range(2):
                act.wait_ge(x1_out[k], 16 * ((NT + 1 - k) // 2))
            for k in range(2):
                act.wait_ge(h1_out[k], 16 * ((NT + 1 - k) // 2))

            def load_x1(d, k):
                act.dma_start(xt[k][:, :], x1_tab[bass.ds(d * P, P), :]).then_inc(x1l[k], 16)

            def split(u):
                act.wait_ge(in1, u + 1)
                act.activation(ring(hi_r, u, WORK, GW), ring(g_ring, u, RING, GW), ACT.Copy).then_inc(hi1, 1)
                stage(u + RING, idx1)

            def new_pair1(d, u):
                slot_free(act, d + 1, u, done_f1, done_b1)
                split(u)

            def transposed1(d, k):
                act.wait_ge(m_htr, d + 1)
                wait(act, m_self, d - 1)
                act.copy(hT[k][:, :], ps[4][:, :]).then_inc(m_hT, 1)
                act.wait_ge(m_mtr, d + 1)
                wait(act, m_y, d - 1)
                act.copy(mT[k][:, :], ps[5][:, :]).then_inc(m_mT, 1)

            def mean1(d, k, lo):
                tile_done(act, d + 1, lo, done_f1, done_b1)
                wait(act, m_mtr, d - 1)
                act.activation(hn[k][:, :], ps[k][:, :], ACT.Copy, scale=rdeg[:, bass.ds(d, 1)]).then_inc(m_mn, 1)

            def sqrt1(d, k):
                act.wait_ge(n_mv, d + 1)
                act.activation(sd[k][:, :], mv[k][:, 1:2], ACT.Sqrt, bias=eps_c[:, :]).then_inc(n_sd, 1)

            def normalise1(d, k):
                act.wait_ge(n_nm, d + 1)
                wait(act, y_out[k], 8 * (d - k))
                act.activation(yo[k][:, :], ps[6 + k][:, :], ACT.Identity, bias=nm[k][:, :],
                               scale=rs[k][:, :]).then_inc(n_yn, 1)

            def store1(d, k, n=P):
                act.wait_ge(n_o, d + 1)
                act.dma_start(out[bass.ds(d * P, n), :], yo[k][0:n, :]).then_inc(y_out[k], 16)

            def load_h1(d, k):
                act.dma_start(ho[k][:, :], h1_tab[bass.ds(d * P, P), :]).then_inc(hl[k], 16)

            def load_x1(d, k):
                act.dma_start(xt[k][:, :], x1_tab[bass.ds(d * P, P), :]).then_inc(x1l[k], 16)

            def between1(d, k, lo):
                if in_tiles(d - 4):
                    normalise1(d - 4, k)
                if in_tiles(d - 2):
                    transposed1(d - 2, k)
                    if in_tiles(d):
                        load_h1(d, k)
                if in_tiles(d - 5):
                    store1(d - 5, 1 - k)
                if in_tiles(d - 3):
                    load_x1(d - 3, 1 - k)
                    sqrt1(d - 3, 1 - k)
                if in_tiles(d - 1):
                    mean1(d - 1, 1 - k, lo)

            def tile1(d, k):
                lo, hi = bounds(act, d)
                between1(d, k, lo)
                rest_of(act, lo, hi, lambda u: new_pair1(d, u + 1))

            load_h1(0, 0)
            load_h1(1, 1)
            for u in range(2):
                split(u)
            node_tiles(act, tile1, 6)
            for d in range(NT, NT + 4):
                between1(d, d % 2, LAST_PAIR)
            store1(NT - 1, 0, LAST_ROWS)
            for k in range(2):
                act.wait_ge(y_out[k], 16 * ((NT + 1 - k) // 2))
            act.wait_ge(s_w1, 80)

        @block.tensor
        def _(pe):
            mm = nc.tensor.matmul

            pe.wait_ge(k_cf, 1)
            pe.wait_ge(o_v, 2)
            mm(ps[4][0:1, 0:1], falls[0:ROWS, :], ones_c[0:ROWS, :], start=True, stop=True).then_inc(o_pe, 1)

            def count(t, n):
                pe.wait_ge(c_v[0], COUNT_STEPS * t + 7)
                mm(ps[0][:, 0:BUCKETS], lo_hot, hi_hot, start=True, stop=True).then_inc(c_pe[0], 1)

            def look_up(t, n):
                pe.wait_ge(c_v[1], PLACE_STEPS * t + 8)
                mm(ps[0][:, 0:BUCKETS], lo_hot, hi_hot, start=True, stop=True)
                mm(ps[3][:, 0:P], ones_m, diag, start=True, stop=True)
                pe.transpose(ps[1][:, 0:P], lo_hot, ident[:, :]).then_inc(c_pe[1], 1)
                pe.wait_ge(c_v[1], PLACE_STEPS * t + 9)
                mm(ps[2][:, 0:BUCKETS], lo_hotT, table, start=True, stop=True).then_inc(c_pe[1], 1)

            with pe.If(disorder(pe) > 0):
                sort_tiles(pe, count)
                pe.wait_ge(c_v[0], COUNT_STEPS * (FULL_TILES + 1))
                mm(ps[1][:, 0:BUCKETS], upper, table, start=True, stop=True)
                mm(ps[2][:, 0:BUCKETS], ones_m, table, start=True, stop=True).then_inc(c_sum, 1)
                sort_tiles(pe, look_up)
            pe.nop()

            pe.wait_ge(e_f, 2)
            n = 0
            for part in (dst_cf, src_cf):
                for q in range(2):
                    wait(pe, e_ev, n - 1)
                    for b in range(4):
                        t = part[:, (4 * q + b) * P:(4 * q + b + 1) * P]
                        last = pe.transpose(ps[4 + n % 2][:, b * ROWS:(b + 1) * ROWS], t, ident[0:ROWS, 0:ROWS])
                    last.then_inc(e_tr, 1)
                    n += 1

            pe.wait_ge(s_w, 16)

            def transpose_in(i, k):
                pe.wait_ge(a_h0, i + 1)
                wait(pe, a_hT, i - 1)
                for c in range(KC):
                    last = pe.transpose(ps[k][:, c * P:(c + 1) * P], hn[k][:, c * P:(c + 1) * P], ident[:, :])
                last.then_inc(a_tr, 1)

            def project(i, k, n):
                if in_tiles(i + 1):
                    transpose_in(i + 1, 1 - k)
                pe.wait_ge(a_hT, i + 1)
                wait(pe, a_hb, i - 1)
                for c in range(KC):
                    last = mm(ps[2 + k][:, :], hT[k][:, c * P:(c + 1) * P], w0[:, c * DIM:(c + 1) * DIM],
                              start=(c == 0), stop=(c == KC - 1))
                last.then_inc(a_mm, 1)

            transpose_in(0, 0)
            tiles_by_two(pe, project)

            pe.wait_ge(s_dist, 32)
            for b in range(8):
                for q in range(2):
                    wait(pe, e_ev, n - 1)
                    for h in range(4):
                        t = dist_c[:, b * P * HEADS + 4 * q + h:(b + 1) * P * HEADS:HEADS]
                        last = pe.transpose(ps[4 + n % 2][:, h * ROWS:(h + 1) * ROWS], t, ident[0:ROWS, 0:ROWS])
                    last.then_inc(e_tr, 1)
                    n += 1

            pe.wait_ge(e_ev, 4)
            mm(ps[6][0:64, 0:PAIRS], pick_last[:, :], dst_e[:, 1::2], start=True, stop=True).then_inc(b_mm, 1)
            pe.wait_ge(b_cnt, 1)
            pe.transpose(ps[7][0:1, 0:64], cnt[:, :], ident[0:64, 0:64]).then_inc(b_tr, 1)

            pe.sem_inc(d_tr, 1)
            pe.sem_inc(d_mm, 1)
            pe.wait_ge(d_split, 5)

            def step_d(d, u):
                s = d + u
                pe.wait_ge(d_oh, s + 1)
                pe.wait_ge(d_cp, s + 1)
                for i in range(2):
                    last = pe.transpose(ps[2][:, i * P // 2:(i + 1) * P // 2].bitcast(BF16),
                                        oh_b[:, i * P:(i + 1) * P], ident_b[:, :])
                last.then_inc(d_tr, 1)
                pe.wait_ge(d_cp, s + 2)
                pe.wait_ge(d_red, s + 1)
                for i in range(2):
                    last = mm(ps[3][:, i * 3 * HEADS:(i + 1) * 3 * HEADS], ohT_b[:, i * P:(i + 1) * P],
                              ed3[:, bass.ds(d * 3 * HEADS, 3 * HEADS)], start=True, stop=True)
                last.then_inc(d_mm, 1)

            def tile_d(d, k):
                lo, hi = bounds(pe, d)
                step_d(d, lo)
                rest_of(pe, lo, hi, lambda u: step_d(d, u))

            pe.wait_ge(b_code, 1)
            pe.sem_inc(d_cp, 1)
            node_tiles(pe, tile_d)

            for g in range(0, TPC, 4):
                pe.wait_ge(t_x, g // 4 + 1)
                wait(pe, t_cp, g // 4 - 1)
                for j in range(g, min(g + 4, TPC)):
                    last = pe.transpose(ps[g // 4 % 2][:, (j - g) * P:(j - g + 1) * P], es_all[:, j * P:(j + 1) * P],
                                        ident[:, :])
                last.then_inc(t_tr, 1)
            pe.wait_ge(t_v, 5)
            for q in range(4):
                last = pe.transpose(ps[2][0:1, q * P:(q + 1) * P], ends[:, q:q + 1], ident[:, :])
            last.then_inc(t_pe, 1)
            pe.wait_ge(t_v, 19)
            for q in range(2):
                last = pe.transpose(ps[3][:, q:q + 1], inits[q][0:1, :], ident[0:1, 0:1])
            last.then_inc(t_pe, 1)
            pe.wait_ge(t_v, 22)
            for g in range(0, TPC, 4):
                wait(pe, t_z, g // 4 - 1)
                for j in range(g, min(g + 4, TPC)):
                    last = pe.transpose(ps[g // 4 % 2][:, (j - g) * P:(j - g + 1) * P], scan[:, j * P:(j + 1) * P],
                                        ident[:, :])
                last.then_inc(t_bt, 1)

            pe.sem_inc(done_a0, 1)
            pe.sem_inc(done_b0, WORK)
            pe.wait_ge(t_co, -(-TPC // 4))

            def add0(k, one_hot, u, t, start):
                mm(ps[k][:, :], one_hot[:, :], msg[:, bass.ds((u % WEIGHED) * GW + t * DIM, DIM)],
                   start=start, stop=True, skip_group_check=True)
                return mm(ps[2 + k][:, 0:EW], one_hot[:, :], ex_buf[:, bass.ds((2 * u + t) * EW, EW)],
                          start=start, stop=True, skip_group_check=True)

            def first0(d, u, k):
                pe.wait_ge(msg0, u + 1)
                pe.wait_ge(msg_act0, u + 1)
                pe.wait_ge(hot_f0, d + 1)
                add0(k, oh_first[0], u, 0, True)
                add0(k, oh_first[1], u, 1, False).then_inc(done_f0, 1)

            def step0(u, k):
                pe.wait_ge(msg0, u + 1)
                pe.wait_ge(msg_act0, u + 1)
                pe.wait_ge(hot_a0, u)
                add0(k, oh_rest[0], u, 0, False).then_inc(done_a0, 1)
                pe.wait_ge(hot_b0, u)
                add0(k, oh_rest[1], u, 1, False).then_inc(done_b0, 1)

            def tile0(d, k):
                lo, hi = bounds(pe, d)
                wait(pe, f_w, d - 1)
                first0(d, lo, k)
                rest_of(pe, lo, hi, lambda u: step0(u, k))

            node_tiles(pe, tile0, 4)

            pe.wait_ge(m_one, 1)
            pe.sem_inc(done_a1, 1)
            pe.sem_inc(done_b1, WORK)
            pe.wait_ge(s_w1, 80)

            def add1(k, one_hot, u, t, start):
                for part in (hi_r, lo_r):
                    last = mm(ps[k][:, :], one_hot[:, :], part[:, bass.ds((u % WORK) * GW + t * DIM, DIM)],
                              start=start and part is hi_r, stop=True, skip_group_check=True)
                return last

            def first1(d, u, k):
                pe.wait_ge(lo1, u + 1)
                pe.wait_ge(hot_f1, d + 1)
                add1(k, ohr_first[0], u, 0, True)
                add1(k, ohr_first[1], u, 1, False).then_inc(done_f1, 1)

            def step1(u, k):
                pe.wait_ge(lo1, u + 1)
                pe.wait_ge(hot_a1, u)
                add1(k, ohr_rest[0], u, 0, False).then_inc(done_a1, 1)
                pe.wait_ge(hot_b1, u)
                add1(k, ohr_rest[1], u, 1, False).then_inc(done_b1, 1)

            def transpose1(d, k):
                pe.wait_ge(hl[k], 8 * (d - k) + 16)
                wait(pe, m_hT, d)
                for c in range(KC):
                    last = pe.transpose(ps[4][:, c * P:(c + 1) * P], ho[k][:, c * P:(c + 1) * P], ident[:, :])
                last.then_inc(m_htr, 1)
                pe.wait_ge(m_mn, d + 1)
                wait(pe, m_mT, d)
                for c in range(KC):
                    last = pe.transpose(ps[5][:, c * P:(c + 1) * P], hn[k][:, c * P:(c + 1) * P], ident[:, :])
                last.then_inc(m_mtr, 1)

            def own1(d, k):
                pe.wait_ge(m_hT, d + 1)
                wait(pe, n_yn, d - 1)
                mm(ps[6 + k][:, :], ones_r, row_bias[0:1, :], start=True, stop=False)
                for c in range(KC):
                    last = mm(ps[6 + k][:, :], hT[k][:, c * P:(c + 1) * P], ws[:, c * DIM:(c + 1) * DIM],
                              start=False, stop=False)
                last.then_inc(m_self, 1)

            def neighbours1(d, k, half):
                if half == 0:
                    pe.wait_ge(m_mT, d + 1)
                for c in range(half * KC // 2, (half + 1) * KC // 2):
                    last = mm(ps[6 + k][:, :], mT[k][:, c * P:(c + 1) * P], wn[:, c * DIM:(c + 1) * DIM],
                              start=False, stop=(c == KC - 1))
                if half == 1:
                    last.then_inc(m_y, 1)

            def tile1(d, k):
                lo, hi = bounds(pe, d)
                wait(pe, m_mn, d - 1)
                first1(d, lo, k)
                if in_tiles(d - 2):
                    own1(d - 2, k)

                second_pair = nc.s_assert_within(lo + 1, 1, LAST_PAIR, skip_runtime_bounds_check_because="lo < hi")
                third_pair = nc.s_assert_within(lo + 2, 2, LAST_PAIR, skip_runtime_bounds_check_because="lo + 1 < hi")
                with pe.If(lo < hi):
                    step1(second_pair, k)
                    pe.nop()
                if in_tiles(d - 2):
                    neighbours1(d - 2, k, 0)
                with pe.If(lo + 1 < hi):
                    step1(third_pair, k)
                    pe.nop()
                if in_tiles(d - 2):
                    neighbours1(d - 2, k, 1)
                if in_tiles(d - 1):
                    transpose1(d - 1, 1 - k)
                with pe.If(lo + 2 < hi):
                    with pe.Fori(lo + 3, hi + 1) as u:
                        step1(u, k)
                    pe.nop()
                pe.nop()

            node_tiles(pe, tile1, 4)
            own1(NT - 2, 1)
            neighbours1(NT - 2, 1, 0)
            neighbours1(NT - 2, 1, 1)
            transpose1(NT - 1, 0)
            own1(NT - 1, 0)
            neighbours1(NT - 1, 0, 0)
            neighbours1(NT - 1, 0, 1)

        @block.vector
        def _(dve):
            tt, ts, stt = nc.vector.tensor_tensor, nc.vector.tensor_scalar, nc.vector.scalar_tensor_tensor
            copy = nc.vector.tensor_copy

            dve.memset(dst_c[96:ROWS, REST:], PAD_DST).then_inc(padded, 1)
            dve.memset(dst_next[96:ROWS, REST - 1:], PAD_DST).then_inc(padded, 1)
            dve.memset(src_c[96:ROWS, REST:], 0).then_inc(padded, 1)
            dve.memset(dist_c[96:ROWS, REST * HEADS:], 0.0).then_inc(padded, 1)
            dve.memset(dst_s[96:P, N_EDGES - (CHUNKS - 1) * CHUNK:], PAD_DST).then_inc(padded, 1)
            dve.memset(eps_c[:, :], EPS)
            dve.memset(src_e[:, TILES:], 0)
            dve.wait_ge(k_cst, 3)
            copy(iota_f[:, :], iota_i[:, :])
            copy(first_f[:, :], first_i[:, :])
            copy(thr_f[:, :], thr_i[:, :])
            dve.wait_ge(k_id, 4)
            copy(ident_b[:, :], ident[:, :]).then_inc(k_cf, 1)

            dve.memset(ones_c[:, :], 1.0)
            dve.wait_ge(o_in, 64)
            tt(src_cf, dst_c, dst_next, ALU.is_gt).then_inc(o_v, 1)
            dve.wait_ge(o_v, 1)
            dve.tensor_reduce(falls[0:ROWS, :], src_cf, AX.X, ALU.add).then_inc(o_v, 1)
            dve.wait_ge(o_pe, 1)
            copy(flag[:, :], ps[4][0:1, 0:1]).then_inc(o_flag, 1)

            def one_hots(q, t, n, per_tile):
                done = [0]

                def step(ins):
                    done[0] += 1
                    ins.then_inc(c_v[q], 1)
                    dve.wait_ge(c_v[q], per_tile * t + done[0])

                if n < P:
                    if q:
                        dve.wait_ge(c_o[0], 16 * t)
                    step(dve.memset(dst_col, NT * P))
                else:
                    step(dve.memset(above[:, BUCKETS:], 0.0))
                dve.wait_ge(c_in[q], 16 * (t + 1))
                step(copy(dst_f, dst_col))
                step(ts(above[:, 0:BUCKETS], first_f[:, :], dst_f, None, ALU.is_le, ALU.add, accum_out=n_above))
                step(tt(hi_hot, above[:, 0:BUCKETS], above[:, 1:], ALU.subtract))
                step(ts(n_above, n_above, -float(P), float(P), ALU.mult, ALU.add))
                step(tt(lo_f, n_above, dst_f, ALU.add))
                step(ts(lo_hot, iota_f[:, :], lo_f, None, ALU.is_equal))
                return step

            def count(t, n):
                step = one_hots(0, t, n, COUNT_STEPS)
                dve.wait_ge(c_pe[0], t + 1)
                step(tt(table, table, ps[0][:, 0:BUCKETS], ALU.add))

            def look_up(t, n):
                step = one_hots(1, t, n, PLACE_STEPS)
                step(ts(diag, ident[:, :], dst_f, None, ALU.mult))
                dve.wait_ge(c_pe[1], 2 * t + 1)
                step(copy(lo_hotT, ps[1][:, 0:P]))
                dve.wait_ge(c_pe[1], 2 * t + 2)
                step(tt(picked, hi_hot, ps[2][:, 0:BUCKETS], ALU.mult))
                step(dve.tensor_reduce(base_f, picked, AX.X, ALU.add))
                step(ts(same_dst, ps[3][:, 0:P], dst_f, None, ALU.is_equal))
                step(tt(same_dst, same_dst, lower, ALU.mult))
                step(dve.tensor_reduce(rank_f, same_dst, AX.X, ALU.add))
                step(tt(place_f, base_f, rank_f, ALU.add))
                step(tt(table, table, ps[0][:, 0:BUCKETS], ALU.add))
                step(copy(place_i, place_f))

            with dve.If(disorder(dve) > 0):
                dve.memset(coef[:, :], 0.0).then_inc(o_v, 1)
                dve.wait_ge(o_v, 3)
                dve.memset(dst_col, NT * P)
                dve.memset(src_col, 0)
                dve.memset(ones_m, 1.0).then_inc(c_pad, 1)
                ts(lower, iota_f[:, :], float(P), thr_f[:, :], ALU.mult, ALU.is_lt)
                ts(upper, iota_f[:, :], float(P), thr_f[:, :], ALU.mult, ALU.is_gt)
                sort_tiles(dve, count)
                dve.wait_ge(c_sum, 1)
                copy(totals, ps[2][:, 0:BUCKETS]).then_inc(o_v, 1)
                dve.wait_ge(o_v, 4)
                dve.tensor_tensor_scan(sums, ones_m[:, 0:BUCKETS], totals, 0.0, ALU.mult, ALU.add).then_inc(o_v, 1)
                dve.wait_ge(o_v, 5)
                tt(sums, sums, totals, ALU.subtract).then_inc(o_v, 1)
                dve.wait_ge(o_v, 6)
                tt(table, sums, ps[1][:, 0:BUCKETS], ALU.add).then_inc(c_start, 1)
                dve.wait_ge(c_start, 1)
                sort_tiles(dve, look_up)
            dve.nop()

            dve.wait_ge(s_ec, 64)
            copy(dst_cf, dst_c).then_inc(e_f, 1)
            copy(src_cf, src_c).then_inc(e_f, 1)
            n = 0
            for part in (dst_e, src_e):
                for q in range(2):
                    dve.wait_ge(e_tr, n + 1)
                    o = part[:, 0:TILES].rearrange("p (a b) -> p b a", b=8)[:, 4 * q:4 * q + 4, :]
                    copy(o, ps[4 + n % 2][:, 0:4 * ROWS].rearrange("p (b a) -> p b a", b=4)).then_inc(e_ev, 1)
                    n += 1
            dve.wait_ge(e_ev, 4)
            copy(src_g[:, :].rearrange("p (j c) -> p j c", c=CHUNKS),
                 src_e[:, 0:TILES].rearrange("p (c j) -> p j c", c=CHUNKS)).then_inc(e_sg, 1)
            dve.wait_ge(s_row, 48)

            def stats(src_t, k, s_st, s_mv, d):
                dve.bn_stats(st[k][:, :], src_t).then_inc(s_st, 1)
                dve.wait_ge(s_st, d + 1)
                dve.sem_inc(v_go, 1)
                dve.bn_aggr(mv[k][:, :], st[k][:, :]).then_inc(s_mv, 1)

            def scale_and_shift(k, s_mv, s_sd, s_rs, s_nm, d):
                dve.wait_ge(s_sd, d + 1)
                dve.reciprocal(rs[k][:, :], sd[k][:, :]).then_inc(s_rs, 1)
                dve.wait_ge(s_rs, d + 1)
                stt(nm[k][:, :], mv[k][:, 0:1], -1.0, rs[k][:, :], ALU.mult, ALU.mult).then_inc(s_nm, 1)

            def moments(i, k, n):
                dve.wait_ge(x_in[k], 16 * (n + 1))
                stats(xt[k][:, :], k, a_st, a_mv, i)

            def shift(i, k):
                wait(dve, a_h0, i - 1)
                scale_and_shift(k, a_mv, a_sd, a_rs, a_nm, i)

            def head_terms(i, k, n):
                dve.wait_ge(a_mm, i + 1)
                wait(dve, h_out[k], 16 * n)
                wait(dve, a_md, i - 1)
                tt(ho[k][:, :], ps[2 + k][:, :], row_b0[:, :], ALU.add).then_inc(a_hb, 1)
                dve.wait_ge(a_hb, i + 1)
                stt(ho[k][:, :], ho[k][:, :], SLOPE, ho[k][:, :], ALU.mult, ALU.max).then_inc(a_h, 1)

            def head_sums(i, k, n):
                dve.wait_ge(a_ms, i + 1)
                wait(dve, es_out[k], 16 * n)
                dve.tensor_reduce(es_st[k][:, :], ms[k][:, :].rearrange("p (h e) -> p h e", h=HEADS), AX.X,
                                  ALU.add).then_inc(a_es, 1)
                dve.wait_ge(a_md, i + 1)
                dve.tensor_reduce(ed_n[:, bass.ds(i * HEADS, HEADS)],
                                  md[k][:, :].rearrange("p (h e) -> p h e", h=HEADS), AX.X, ALU.add).then_inc(a_ed, 1)

            def tile_a(i, k, n):
                if in_tiles(i + 2):
                    moments(i + 2, k, n + 1)
                if in_tiles(i - 2):
                    head_sums(i - 2, k, n - 1)
                if in_tiles(i + 2):
                    shift(i + 2, k)
                head_terms(i, k, n)

            moments(0, 0, 0)
            shift(0, 0)
            moments(1, 1, 0)
            shift(1, 1)
            tiles_by_two(dve, tile_a)
            head_sums(NT - 2, 1, NT // 2 - 1)
            head_sums(NT - 1, 0, NT // 2)

            for b in range(8):
                for q in range(2):
                    dve.wait_ge(e_tr, n + 1)
                    o = coef[:, 0:TILES * HEADS].rearrange("p (a b h) -> p b h a", b=8, h=HEADS)[:, b, 4 * q:4 * q + 4, :]
                    copy(o, ps[4 + n % 2][:, 0:4 * ROWS].rearrange("p (h a) -> p h a", h=4)).then_inc(e_ev, 1)
                    n += 1

            dve.wait_ge(b_mm, 1)
            ts(below, ps[6][0:64, 0:PAIRS], thr_f[0:64, :], None, ALU.is_lt, ALU.add,
               accum_out=cnt[:, :]).then_inc(b_cnt, 1)
            dve.wait_ge(b_tr, 1)
            copy(bnd_f[:, :], ps[7][0:1, 0:64]).then_inc(b_row, 1)
            dve.wait_ge(b_row, 1)
            stt(code_f[:, 0:63], bnd_f[:, 0:63], float(CODE), bnd_f[:, 1:64], ALU.mult, ALU.add).then_inc(b_row, 1)
            dve.wait_ge(b_row, 2)
            copy(code[:, 0:63], code_f[:, 0:63]).then_inc(b_code, 1)

            parts = ed3[:, :].rearrange("p (d q h) -> p q d h", q=3, h=HEADS)
            nodes = ed_n[:, :].rearrange("p (d h) -> p d h", h=HEADS)
            rest = ed_r[:, :].rearrange("p (d h) -> p d h", h=HEADS)
            dve.wait_ge(a_ed, NT)
            copy(parts[:, 0], nodes).then_inc(d_split, 1)
            dve.wait_ge(d_split, 1)
            tt(rest, nodes, parts[:, 0], ALU.subtract).then_inc(d_split, 1)
            dve.wait_ge(d_split, 2)
            copy(parts[:, 1], rest).then_inc(d_split, 1)
            dve.wait_ge(d_split, 3)
            tt(rest, rest, parts[:, 1], ALU.subtract).then_inc(d_split, 1)
            dve.wait_ge(d_split, 4)
            copy(parts[:, 2], rest).then_inc(d_split, 1)

            dve.wait_ge(s_ds, 16 * CHUNKS)
            tt(same[:, 1:CHUNK], dst_s[:, 1:CHUNK], dst_s[:, 0:CHUNK - 1], ALU.is_equal).then_inc(e_same, 1)
            copy(ends[:, 2:3], dst_s[:, 0:1])
            copy(ends[:, 3:4], dst_s[:, CHUNK - 1:CHUNK]).then_inc(e_same, 1)
            dve.wait_ge(e_same, 1)
            ts(same[:, 1:CHUNK], same[:, 1:CHUNK], 2 * BIG, -BIG, ALU.mult, ALU.add).then_inc(e_same, 1)
            dve.memset(same[:, 0:1], BIG)
            dve.memset(same[:, CHUNK:CHUNK + 1], BIG)
            dve.wait_ge(e_tr, 20)
            dve.memset(ed_e, 0.0).then_inc(d_zero, 1)
            dve.memset(ex3[:, :, HEADS:EW], 1.0)
            dve.memset(coef[:, TILES * HEADS:], 0.0)

            def new_numbers(d, k):
                ts(iod[k][:, :], iota_f[:, :], first_f[:, bass.ds(d, 1)], None, ALU.add).then_inc(numbers, 1)

            def wait_numbers(walk, d):
                dve.wait_ge(numbers, walk * NT + d + 1)

            def one_hot(o, k, u, t):
                return ts(o, iod[k][:, :], dst_e[:, bass.ds(2 * u + t, 1)], None, ALU.is_equal)

            def hot_d(d, u, k):
                dve.wait_ge(d_tr, d + u + 1)
                one_hot(oh_b[:, 0:P], k, u, 0)
                one_hot(oh_b[:, P:2 * P], k, u, 1).then_inc(d_oh, 1)

            def add_d(s, u):
                dve.wait_ge(d_mm, s + 2)
                wait(dve, d_add, s)
                dve.tensor_reduce(red[:, :].rearrange("p (i h) -> p i h", i=2),
                                  ps[3][:, 0:6 * HEADS].rearrange("p (i q h) -> p i h q", i=2, q=3), AX.X,
                                  ALU.add).then_inc(d_red, 1)
                dve.wait_ge(d_red, s + 2)
                o = ed_e[:, bass.ds(2 * u * HEADS, 2 * HEADS)]
                tt(o, o, red[:, :], ALU.add).then_inc(d_add, 1)

            def tile_d(d, k):
                lo, hi = bounds(dve, d)
                new_numbers(d, k)
                wait_numbers(0, d)
                hot_d(d, lo, k)
                if not isinstance(d, int) or d >= 1:
                    add_d(d + lo - 1, lo)

                def body(u):
                    hot_d(d, u, k)
                    add_d(d + u - 1, u - 1)
                rest_of(dve, lo, hi, body)

            dve.sem_inc(d_red, 1)
            dve.wait_ge(d_zero, 1)
            dve.wait_ge(b_code, 1)
            node_tiles(dve, tile_d)
            add_d(NT - 1 + LAST_PAIR, LAST_PAIR)

            by_group = "p (c j h) -> p j c h"
            e_by_group = ex3[:, :, 0:HEADS].rearrange("p (c j) h -> p j c h", j=TPC)
            es_by_group = es_all.rearrange("p (j c h) -> p j c h", c=CHUNKS, h=HEADS)
            ed_by_group = ed_e.rearrange(by_group, c=CHUNKS, h=HEADS)
            dve.wait_ge(d_add, NT + LAST_PAIR)
            dve.wait_ge(e_same, 3)

            def forward_piece(g):
                dve.wait_ge(t_cp, g // 4 + 1)
                cols = slice(g * P, min(g + 4, TPC) * P)
                dve.tensor_tensor_scan(fwd[:, cols], same[:, cols], scan[:, cols],
                                       fwd[:, g * P - 1:g * P] if g else -BIG, ALU.min, ALU.max).then_inc(t_f, 1)
                dve.wait_ge(t_f, g // 4 + 1)

            for g in range(0, TPC, 4):
                m = min(4, TPC - g)
                sel = slice(g, g + m)
                for k in range(2):
                    dve.wait_ge(es_mv[k], 16 * ((g + m + 1 - k) // 2))
                tt(es_by_group[:, sel], es_by_group[:, sel], ed_by_group[:, sel], ALU.add).then_inc(t_sum, 1)
                dve.wait_ge(t_sum, g // 4 + 1)
                block = es_all[:, g * P:(g + m) * P]
                stt(block, block, SLOPE, block, ALU.mult, ALU.max).then_inc(t_x, 1)
                if g:
                    forward_piece(g - 4)
            forward_piece(g)
            v = [0]

            def link(ins):
                v[0] += 1
                ins.then_inc(t_v, 1)
                dve.wait_ge(t_v, v[0])

            def forward(initial):
                return dve.tensor_tensor_scan(fwd, same[:, 0:CHUNK], scan[:, :], initial, ALU.min, ALU.max)

            def backward(o, initial):
                return dve.tensor_tensor_scan(o[:, ::-1], same[:, CHUNK:0:-1], fwd[:, ::-1], initial, ALU.min, ALU.max)

            link(copy(ends[:, 1:2], fwd[:, CHUNK - 1:CHUNK]))
            link(backward(fwd, -BIG))
            link(copy(ends[:, 0:1], fwd[:, 0:1]))
            link(dve.memset(cont[:, :], -BIG))
            link(dve.memset(kl[:, :], -BIG))
            dve.wait_ge(t_pe, 1)
            link(copy(rows[:, :], ps[2][0:1, :]))
            first_mx, last_mx, first_d, last_d = (rows[:, q * P:(q + 1) * P] for q in range(4))
            link(tt(cont[:, HEADS:P], first_d[:, HEADS:P], last_d[:, 0:P - HEADS], ALU.is_equal))
            link(ts(cont[:, HEADS:P], cont[:, HEADS:P], 2 * BIG, -BIG, ALU.mult, ALU.add))
            link(tt(one[:, :], first_d, last_d, ALU.is_equal))
            link(ts(one[:, :], one[:, :], 2 * BIG, -BIG, ALU.mult, ALU.add))
            link(tt(kl[:, :], cont[:, :], one[:, :], ALU.min))
            for h in range(HEADS):
                last = dve.tensor_tensor_scan(outr[:, h::HEADS], kl[:, h::HEADS], last_mx[:, h::HEADS], -BIG,
                                              ALU.min, ALU.max)
            link(last)
            link(dve.memset(inits[0][:, :], -BIG))
            link(tt(inits[0][:, HEADS:P], cont[:, HEADS:P], outr[:, 0:P - HEADS], ALU.min))
            link(dve.memset(kl[:, :], -BIG))
            link(tt(kl[:, 0:P - HEADS], cont[:, HEADS:P], one[:, 0:P - HEADS], ALU.min))
            for h in range(HEADS):
                last = dve.tensor_tensor_scan(outr[:, h::HEADS][:, ::-1], kl[:, h::HEADS][:, ::-1],
                                              first_mx[:, h::HEADS][:, ::-1], -BIG, ALU.min, ALU.max)
            link(last)
            link(dve.memset(inits[1][:, :], -BIG))
            link(tt(inits[1][:, 0:P - HEADS], cont[:, HEADS:P], outr[:, HEADS:P], ALU.min))
            assert v[0] == 19
            dve.wait_ge(t_pe, 2)
            link(copy(init_c[:, :], ps[3][:, 0:2]))
            link(forward(init_c[:, 0:1]))
            link(backward(scan[:, :], init_c[:, 1:2]))
            assert v[0] == 22

            pieces = range(0, TPC, 4)
            coef_by_group = coef[:, 0:TILES * HEADS].rearrange(by_group, c=CHUNKS, h=HEADS)
            dve.wait_ge(e_ev, 20)

            def weights(g):
                sel = slice(g, min(g + 4, TPC))
                dve.wait_ge(t_ex, g // 4 + 1)
                tt(coef_by_group[:, sel], coef_by_group[:, sel], e_by_group[:, sel], ALU.mult).then_inc(t_co, 1)

            for g in pieces:
                m = min(4, TPC - g)
                dve.wait_ge(t_bt, g // 4 + 1)
                tt(e_by_group[:, g:g + m], e_by_group[:, g:g + m],
                   ps[g // 4 % 2][:, 0:m * P].rearrange("p (j c h) -> p j c h", c=CHUNKS, h=HEADS),
                   ALU.subtract).then_inc(t_z, 1)
                if g:
                    weights(g - 4)
            weights(g)
            dve.wait_ge(t_co, len(pieces))

            def weigh(u):
                dve.wait_ge(in0, u + 1)
                heads = 2 * HEADS - ACT_HEADS
                tt(msg[:, bass.ds((u % WEIGHED) * GW, heads * HEAD_DIM)].rearrange("p (a e) -> p a e", e=HEAD_DIM),
                   g_ring[:, bass.ds((u % RING) * GW, heads * HEAD_DIM)].rearrange("p (a e) -> p a e", e=HEAD_DIM),
                   coef[:, bass.ds(2 * u * HEADS, heads)].unsqueeze(2).to_broadcast([P, heads, HEAD_DIM]),
                   ALU.mult).then_inc(msg0, 1)

            def hot_first(walk, d, u, k, bufs, ready, done):
                wait(dve, done, d)
                wait_numbers(walk, d)
                one_hot(bufs[0][:, :], k, u, 0)
                one_hot(bufs[1][:, :], k, u, 1).then_inc(ready, 1)

            def hot_rest(u, k, bufs, ready_a, ready_b, done_a, done_b):
                dve.wait_ge(done_a, u)
                one_hot(bufs[0][:, :], k, u, 0).then_inc(ready_a, 1)
                dve.wait_ge(done_b, u - 1 + WORK)
                one_hot(bufs[1][:, :], k, u, 1).then_inc(ready_b, 1)

            def divisors0(d, k, lo):
                tile_done(dve, d + 1, lo, done_f0, done_b0)
                ts(r9[k][:, :], ps[2 + k][:, 0:EW], 0.5, None, ALU.max).then_inc(f_r9, 1)
                dve.wait_ge(f_r9, d + 1)
                wait(dve, f_w, d - 1)
                dve.reciprocal(rr[k][:, :], r9[k][:, :]).then_inc(f_rr, 1)

            def moments0(d, k):
                dve.wait_ge(f_w, d + 1)
                dve.wait_ge(xl[k], 8 * (d - k) + 16)
                tt(hn[k][:, :], hn[k][:, :], xt[k][:, :], ALU.add).then_inc(f_x1, 1)
                dve.wait_ge(f_x1, d + 1)
                stats(hn[k][:, :], k, f_st, f_mv, d)

            def shift0(d, k):
                wait(dve, f_h1, d - 1)
                scale_and_shift(k, f_mv, f_sd, f_rs, f_nm, d)

            def tile0(d, k):
                lo, hi = bounds(dve, d)

                def hots(u):
                    hot_rest(u, k, oh_rest, hot_a0, hot_b0, done_a0, done_b0)

                def between():
                    if from_tile(d, 1):
                        divisors0(d - 1, 1 - k, lo)
                    if from_tile(d, 2):
                        moments0(d - 2, k)
                    if in_tiles(d + 1):
                        new_numbers(d + 1, 1 - k)

                def end():
                    if in_tiles(d + 1):
                        hot_first(1, d + 1, hi, 1 - k, oh_first, hot_f0, done_f0)
                    if from_tile(d, 2):
                        shift0(d - 2, k)

                def body(u):
                    hots(u)
                    weigh(u + AHEAD - 1)
                second_then_rest(dve, lo, hi, hots, between, body, end=end, last=lambda u: weigh(u + AHEAD))

            for u in range(AHEAD + 1):
                weigh(u)
            new_numbers(0, 0)
            hot_first(1, 0, 0, 0, oh_first, hot_f0, done_f0)
            node_tiles(dve, tile0, 4)
            divisors0(NT - 1, 0, LAST_PAIR)
            moments0(NT - 2, 1)
            shift0(NT - 2, 1)
            moments0(NT - 1, 0)
            shift0(NT - 1, 0)

            def new_pair1(u):
                dve.wait_ge(hi1, u + 1)
                tt(ring(lo_r, u, WORK, GW), ring(g_ring, u, RING, GW), ring(hi_r, u, WORK, GW).bitcast(F32),
                   ALU.subtract).then_inc(lo1, 1)

            def moments1(d, k):
                dve.wait_ge(m_y, d + 1)
                stats(ps[6 + k][:, :], k, n_st, n_mv, d)

            def final1(d, k):
                dve.wait_ge(n_yn, d + 1)
                tt(yo[k][:, :], yo[k][:, :], row_gamma[:, :], ALU.mult).then_inc(n_g, 1)
                dve.wait_ge(n_g, d + 1)
                tt(yo[k][:, :], yo[k][:, :], row_beta[:, :], ALU.add).then_inc(n_b, 1)
                dve.wait_ge(n_b, d + 1)
                dve.wait_ge(x1l[k], 8 * (d - k) + 16)
                tt(yo[k][:, :], yo[k][:, :], xt[k][:, :], ALU.add).then_inc(n_o, 1)

            def between1(d, k):
                if in_tiles(d - 3):
                    moments1(d - 3, 1 - k)
                if in_tiles(d - 4):
                    final1(d - 4, k)
                if in_tiles(d - 3):
                    scale_and_shift(1 - k, n_mv, n_sd, n_rs, n_nm, d - 3)

            def tile1(d, k):
                lo, hi = bounds(dve, d)

                def hots(u):
                    hot_rest(u, k, ohr_rest, hot_a1, hot_b1, done_a1, done_b1)

                def body(u):
                    hots(u)
                    new_pair1(u + 1)
                def between():
                    between1(d, k)
                    if in_tiles(d + 1):
                        if from_tile(d, 1):
                            tile_done(dve, d, lo, done_f1, done_b1)
                        new_numbers(d + 1, 1 - k)
                        hot_first(2, d + 1, hi, 1 - k, ohr_first, hot_f1, done_f1)
                second_then_rest(dve, lo, hi, hots, between, body, after=lambda u: new_pair1(u + 1))

            dve.memset(ones_r, 1.0).then_inc(m_one, 1)
            for u in range(2):
                new_pair1(u)
            new_numbers(0, 0)
            hot_first(2, 0, 0, 0, ohr_first, hot_f1, done_f1)
            node_tiles(dve, tile1, 6)
            for d in range(NT, NT + 4):
                between1(d, d % 2)


def kernel(x, src, dst, edge_attr_8, L0_gnn_W, L0_gnn_b, L0_gnn_w_att_src, L0_gnn_w_att_dst,
           L1_gnn_W_self, L1_gnn_W_neigh, L1_gnn_bias, L1_gnn_gamma, L1_gnn_beta):
    import numpy as np
    import concourse.bacc as bacc
    from concourse.bass_utils import run_bass_kernel_spmd

    arrays = {
        "x": np.asarray(x), "src": np.asarray(src), "dst": np.asarray(dst), "dist": np.asarray(edge_attr_8),
        "w0t": np.asarray(L0_gnn_W).T, "b0": np.asarray(L0_gnn_b),
        "att_src": np.asarray(L0_gnn_w_att_src).reshape(-1), "att_dst": np.asarray(L0_gnn_w_att_dst).reshape(-1),
        "wst": np.asarray(L1_gnn_W_self).T, "wnt": np.asarray(L1_gnn_W_neigh).T, "bias": np.asarray(L1_gnn_bias),
        "gamma": np.asarray(L1_gnn_gamma), "beta": np.asarray(L1_gnn_beta),
    }
    arrays = {k: np.ascontiguousarray(a) for k, a in arrays.items()}
    nc = bacc.Bacc("TRN2", target_bir_lowering=False, num_devices=1)
    args = [nc.dram_tensor(k, a.shape, mybir.dt.from_np(a.dtype), kind="ExternalInput").ap()
            for k, a in arrays.items()]
    out = nc.dram_tensor("out", (N_NODES, DIM), F32, kind="ExternalOutput").ap()
    gnn_kernel(nc, *args, out)
    return run_bass_kernel_spmd(nc, [arrays], core_ids=[0]).results[0]["out"]
```
